# Optimizing a Trainium2 kernel written in Bass

```python
import numpy as np
import jax
import jax.numpy as jnp

def _softmax(x, axis=-1):
    return jax.nn.softmax(x, axis=axis)

def _gelu(x):
    return jax.nn.gelu(x, approximate=True)

def _silu(x):
    return jax.nn.silu(x)

def _sigmoid(x):
    return jax.nn.sigmoid(x)

def _layernorm(x, axis=-1, eps=1e-05):
    m = jnp.mean(x, axis=axis, keepdims=True)
    v = jnp.var(x, axis=axis, keepdims=True)
    return (x - m) / jnp.sqrt(v + eps)

def _scatter_add(tgt, idx, src, axis=0):
    return tgt.at[idx].add(src)

def _segment_sum(src, seg, n):
    return jax.ops.segment_sum(src, seg, n)
kernel_name = 'mk_macaron_d2_jaxref_r8_3c898a'

def setup_inputs(seed: int=0):
    np.random.seed(seed)
    _w = jnp.asarray

    def _L0_attn_setup():
        import jax, jax.numpy as jnp
        import numpy as np
        B, L, D_MODEL = (2, 256, 128)
        D_STATE, D_CONV, EXPAND = (8, 4, 2)
        D_INNER = EXPAND * D_MODEL
        DT_RANK = (D_MODEL + 15) // 16
        key = jax.random.key(seed)
        ks = jax.random.split(key, 8)
        s = 0.02
        x = jax.random.normal(ks[0], (B, L, D_MODEL), dtype=jnp.float32)
        W_in = jax.random.normal(ks[1], (D_MODEL, 2 * D_INNER), dtype=jnp.float32) * s
        dw_kernel = jax.random.normal(ks[2], (D_CONV, D_INNER), dtype=jnp.float32) * s
        pw_kernel = jax.random.normal(ks[3], (D_INNER, D_INNER), dtype=jnp.float32) * s
        conv_bias = jnp.zeros((D_INNER,), dtype=jnp.float32)
        W_x = jax.random.normal(ks[4], (D_INNER, DT_RANK + 2 * D_STATE), dtype=jnp.float32) * s
        W_dt = jax.random.normal(ks[5], (DT_RANK, D_INNER), dtype=jnp.float32) * s
        b_dt = jnp.zeros((D_INNER,), dtype=jnp.float32)
        A_init = np.repeat(np.arange(1, D_STATE + 1, dtype=np.float32), D_INNER).reshape(D_INNER, D_STATE)
        A_log = jnp.asarray(np.log(A_init))
        D = jnp.ones((D_INNER,), dtype=jnp.float32)
        W_out = jax.random.normal(ks[6], (D_INNER, D_MODEL), dtype=jnp.float32) * s
        return {'x': x, 'W_in': W_in, 'dw_kernel': dw_kernel, 'pw_kernel': pw_kernel, 'conv_bias': conv_bias, 'W_x': W_x, 'W_dt': W_dt, 'b_dt': b_dt, 'A_log': A_log, 'D': D, 'W_out': W_out}
    _L0_attn_in = _L0_attn_setup()

    def _L0_ffn_setup():
        import jax, jax.numpy as jnp
        import numpy as np
        B, S, D, F, E, TOPK = (4, 256, 128, 512, 8, 2)

        def _moe_forward(x, W_router, W_gate, W_up, W_down):
            logits = jnp.einsum('bsd,ed->bse', x, W_router)
            probs = jax.nn.softmax(logits, axis=-1)
            gates, indices = jax.lax.top_k(probs, TOPK)
            gates = gates / jnp.sum(gates, axis=-1, keepdims=True)
            weights = jnp.sum(gates[..., None] * jax.nn.one_hot(indices, E, dtype=x.dtype), axis=-2)
            weights_e = jnp.moveaxis(weights, -1, 0)

            def body(acc, params):
                wg, wu, wd, wt = params
                gate = jax.nn.silu(jnp.einsum('bsd,fd->bsf', x, wg))
                up = jnp.einsum('bsd,fd->bsf', x, wu)
                y = jnp.einsum('bsf,df->bsd', gate * up, wd)
                return (acc + wt[..., None] * y, None)
            out, _ = jax.lax.scan(body, jnp.zeros_like(x), (W_gate, W_up, W_down, weights_e))
            return out
        key = jax.random.key(seed)
        k1, k2, k3, k4, k5 = jax.random.split(key, 5)
        x = jax.random.normal(k1, (B, S, D), dtype=jnp.float32)
        W_router = jax.random.normal(k2, (E, D), dtype=jnp.float32) / np.sqrt(D)
        W_gate = jax.random.normal(k3, (E, F, D), dtype=jnp.float32) / np.sqrt(D)
        W_up = jax.random.normal(k4, (E, F, D), dtype=jnp.float32) / np.sqrt(D)
        W_down = jax.random.normal(k5, (E, D, F), dtype=jnp.float32) / np.sqrt(F)
        return {'x': x, 'W_router': W_router, 'W_gate': W_gate, 'W_up': W_up, 'W_down': W_down}
    _L0_ffn_in = _L0_ffn_setup()

    def _L1_attn_setup():
        import jax, jax.numpy as jnp
        import numpy as np
        EMBED_DIM = 128
        NUM_HEADS = 16
        HEAD_DIM = EMBED_DIM // NUM_HEADS
        ROPE_BASE = 10000.0

        def _rotary_emb(seq_len, dtype=jnp.float32):
            half = HEAD_DIM // 2
            inv_freq = 1.0 / ROPE_BASE ** (jnp.arange(half, dtype=dtype) / half)
            pos = jnp.arange(seq_len, dtype=dtype)
            sinusoid = pos[:, None] * inv_freq[None, :]
            sin = jnp.sin(sinusoid)
            cos = jnp.cos(sinusoid)
            sin = jnp.stack((sin, sin), axis=-1).reshape(seq_len, HEAD_DIM)
            cos = jnp.stack((cos, cos), axis=-1).reshape(seq_len, HEAD_DIM)
            return (sin, cos)

        def _rotate_half(x):
            x1 = x[..., ::2]
            x2 = x[..., 1::2]
            return jnp.stack((-x2, x1), axis=-1).reshape(x.shape)

        def _apply_rope(x, sin, cos):
            return x * cos[None, None] + _rotate_half(x) * sin[None, None]
        key = jax.random.key(seed)
        ks = jax.random.split(key, 9)
        B, S, E = (2, 256, EMBED_DIM)
        scale = 1.0 / np.sqrt(E)
        x = jax.random.normal(ks[0], (B, S, E), dtype=jnp.float32)
        Wq = jax.random.normal(ks[1], (E, E), dtype=jnp.float32) * scale
        bq = jnp.zeros((E,), dtype=jnp.float32)
        Wk = jax.random.normal(ks[2], (E, E), dtype=jnp.float32) * scale
        bk = jnp.zeros((E,), dtype=jnp.float32)
        Wv = jax.random.normal(ks[3], (E, E), dtype=jnp.float32) * scale
        bv = jnp.zeros((E,), dtype=jnp.float32)
        Wo = jax.random.normal(ks[4], (E, E), dtype=jnp.float32) * scale
        bo = jnp.zeros((E,), dtype=jnp.float32)
        return {'x': x, 'Wq': Wq, 'bq': bq, 'Wk': Wk, 'bk': bk, 'Wv': Wv, 'bv': bv, 'Wo': Wo, 'bo': bo}
    _L1_attn_in = _L1_attn_setup()

    def _L1_ffn_setup():
        import jax, jax.numpy as jnp
        import numpy as np
        D_MODEL = 128
        EXPANSION = 4
        D_HIDDEN = D_MODEL * EXPANSION
        NUM_STAGES = int(np.log2(D_HIDDEN))

        def butterfly(y, weights, dim):
            lead = y.shape[:-1]
            for stage in range(weights.shape[0]):
                s = 2 ** stage
                nb = dim // (2 * s)
                yr = y.reshape(*lead, nb, 2, s)
                a = yr[..., 0, :]
                b = yr[..., 1, :]
                w = weights[stage].reshape(nb, s, 2, 2)
                na = w[..., 0, 0] * a + w[..., 0, 1] * b
                nb2 = w[..., 1, 0] * a + w[..., 1, 1] * b
                y = jnp.stack([na, nb2], axis=-2).reshape(*lead, dim)
            return y
        key = jax.random.key(seed)
        ks = jax.random.split(key, 6)
        B, S = (4, 256)
        x = jax.random.normal(ks[0], (B, S, D_MODEL), jnp.float32)
        W_exp = jax.random.normal(ks[1], (D_MODEL, D_HIDDEN), jnp.float32) * 0.02
        b_exp = jnp.zeros((D_HIDDEN,), jnp.float32)
        up_weights = jax.random.normal(ks[2], (NUM_STAGES, D_HIDDEN // 2, 2, 2), jnp.float32) * 0.02
        up_bias = jnp.zeros((D_HIDDEN,), jnp.float32)
        down_weights = jax.random.normal(ks[3], (NUM_STAGES, D_HIDDEN // 2, 2, 2), jnp.float32) * 0.02
        W_con = jax.random.normal(ks[4], (D_HIDDEN, D_MODEL), jnp.float32) * 0.02
        b_con = jnp.zeros((D_MODEL,), jnp.float32)
        down_bias = jnp.zeros((D_MODEL,), jnp.float32)
        return dict(x=x, W_exp=W_exp, b_exp=b_exp, up_weights=up_weights, up_bias=up_bias, down_weights=down_weights, W_con=W_con, b_con=b_con, down_bias=down_bias)
    _L1_ffn_in = _L1_ffn_setup()
    _d = {'L0_attn_x': _L0_attn_in['x'], 'L0_attn_W_in': _L0_attn_in['W_in'], 'L0_attn_dw_kernel': _L0_attn_in['dw_kernel'], 'L0_attn_pw_kernel': _L0_attn_in['pw_kernel'], 'L0_attn_conv_bias': _L0_attn_in['conv_bias'], 'L0_attn_W_x': _L0_attn_in['W_x'], 'L0_attn_W_dt': _L0_attn_in['W_dt'], 'L0_attn_b_dt': _L0_attn_in['b_dt'], 'L0_attn_A_log': _L0_attn_in['A_log'], 'L0_attn_D': _L0_attn_in['D'], 'L0_attn_W_out': _L0_attn_in['W_out'], 'L0_ffn_W_router': _L0_ffn_in['W_router'], 'L0_ffn_W_gate': _L0_ffn_in['W_gate'], 'L0_ffn_W_up': _L0_ffn_in['W_up'], 'L0_ffn_W_down': _L0_ffn_in['W_down'], 'L1_attn_Wq': _L1_attn_in['Wq'], 'L1_attn_bq': _L1_attn_in['bq'], 'L1_attn_Wk': _L1_attn_in['Wk'], 'L1_attn_bk': _L1_attn_in['bk'], 'L1_attn_Wv': _L1_attn_in['Wv'], 'L1_attn_bv': _L1_attn_in['bv'], 'L1_attn_Wo': _L1_attn_in['Wo'], 'L1_attn_bo': _L1_attn_in['bo'], 'L1_ffn_W_exp': _L1_ffn_in['W_exp'], 'L1_ffn_b_exp': _L1_ffn_in['b_exp'], 'L1_ffn_up_weights': _L1_ffn_in['up_weights'], 'L1_ffn_up_bias': _L1_ffn_in['up_bias'], 'L1_ffn_down_weights': _L1_ffn_in['down_weights'], 'L1_ffn_W_con': _L1_ffn_in['W_con'], 'L1_ffn_b_con': _L1_ffn_in['b_con'], 'L1_ffn_down_bias': _L1_ffn_in['down_bias']}
    _x0 = _d['L0_attn_x']
    _d['L0_attn_x'] = jax.random.normal(jax.random.fold_in(jax.random.key(seed), 1), (4, 512, 128), dtype=_x0.dtype)
    del _x0
    return _d

def reference(L0_attn_x, L0_attn_W_in, L0_attn_dw_kernel, L0_attn_pw_kernel, L0_attn_conv_bias, L0_attn_W_x, L0_attn_W_dt, L0_attn_b_dt, L0_attn_A_log, L0_attn_D, L0_attn_W_out, L0_ffn_W_router, L0_ffn_W_gate, L0_ffn_W_up, L0_ffn_W_down, L1_attn_Wq, L1_attn_bq, L1_attn_Wk, L1_attn_bk, L1_attn_Wv, L1_attn_bv, L1_attn_Wo, L1_attn_bo, L1_ffn_W_exp, L1_ffn_b_exp, L1_ffn_up_weights, L1_ffn_up_bias, L1_ffn_down_weights, L1_ffn_W_con, L1_ffn_b_con, L1_ffn_down_bias):

    def _L0_attn_ref(x, W_in, dw_kernel, pw_kernel, conv_bias, W_x, W_dt, b_dt, A_log, D, W_out):
        import jax, jax.numpy as jnp
        import numpy as np
        B, L, D_MODEL = (2, 256, 128)
        D_STATE, D_CONV, EXPAND = (8, 4, 2)
        D_INNER = EXPAND * D_MODEL
        DT_RANK = (D_MODEL + 15) // 16
        d_inner, d_state = A_log.shape
        dt_rank = W_dt.shape[0]
        d_conv = dw_kernel.shape[0]
        bsz = x.shape[0]
        xz = x @ W_in
        x_in, z = jnp.split(xz, 2, axis=-1)
        xp = jnp.pad(x_in, ((0, 0), (d_conv - 1, 0), (0, 0)))
        xc = jax.lax.conv_general_dilated(xp, dw_kernel[:, None, :], window_strides=(1,), padding='VALID', dimension_numbers=('NWC', 'WIO', 'NWC'), feature_group_count=d_inner)
        xc = jax.nn.silu(xc @ pw_kernel + conv_bias)
        x_dbl = xc @ W_x
        delta = x_dbl[..., :dt_rank]
        Bm = x_dbl[..., dt_rank:dt_rank + d_state]
        C = x_dbl[..., dt_rank + d_state:]
        delta = jax.nn.softplus(delta @ W_dt + b_dt)
        A = -jnp.exp(A_log)
        deltaA = jnp.exp(jnp.einsum('bld,dn->bldn', delta, A))
        deltaB_u = jnp.einsum('bld,bln,bld->bldn', delta, Bm, xc)

        def step(h, inp):
            dA_t, dBu_t, C_t = inp
            h = dA_t * h + dBu_t
            y_t = jnp.einsum('bn,bdn->bd', C_t, h)
            return (h, y_t)
        h0 = jnp.zeros((bsz, d_inner, d_state), dtype=x.dtype)
        elems = (deltaA.transpose(1, 0, 2, 3), deltaB_u.transpose(1, 0, 2, 3), C.transpose(1, 0, 2))
        _, ys = jax.lax.scan(step, h0, elems)
        y = ys.transpose(1, 0, 2)
        y = y + xc * D
        y = y * jax.nn.silu(z)
        return y @ W_out

    def _L0_ffn_ref(x, W_router, W_gate, W_up, W_down):
        import jax, jax.numpy as jnp
        import numpy as np
        B, S, D, F, E, TOPK = (4, 256, 128, 512, 8, 2)

        def _moe_forward(x, W_router, W_gate, W_up, W_down):
            logits = jnp.einsum('bsd,ed->bse', x, W_router)
            probs = jax.nn.softmax(logits, axis=-1)
            gates, indices = jax.lax.top_k(probs, TOPK)
            gates = gates / jnp.sum(gates, axis=-1, keepdims=True)
            weights = jnp.sum(gates[..., None] * jax.nn.one_hot(indices, E, dtype=x.dtype), axis=-2)
            weights_e = jnp.moveaxis(weights, -1, 0)

            def body(acc, params):
                wg, wu, wd, wt = params
                gate = jax.nn.silu(jnp.einsum('bsd,fd->bsf', x, wg))
                up = jnp.einsum('bsd,fd->bsf', x, wu)
                y = jnp.einsum('bsf,df->bsd', gate * up, wd)
                return (acc + wt[..., None] * y, None)
            out, _ = jax.lax.scan(body, jnp.zeros_like(x), (W_gate, W_up, W_down, weights_e))
            return out
        return _moe_forward(x, W_router, W_gate, W_up, W_down)

    def _L1_attn_ref(x, Wq, bq, Wk, bk, Wv, bv, Wo, bo):
        import jax, jax.numpy as jnp
        import numpy as np
        EMBED_DIM = 128
        NUM_HEADS = 16
        HEAD_DIM = EMBED_DIM // NUM_HEADS
        ROPE_BASE = 10000.0

        def _rotary_emb(seq_len, dtype=jnp.float32):
            half = HEAD_DIM // 2
            inv_freq = 1.0 / ROPE_BASE ** (jnp.arange(half, dtype=dtype) / half)
            pos = jnp.arange(seq_len, dtype=dtype)
            sinusoid = pos[:, None] * inv_freq[None, :]
            sin = jnp.sin(sinusoid)
            cos = jnp.cos(sinusoid)
            sin = jnp.stack((sin, sin), axis=-1).reshape(seq_len, HEAD_DIM)
            cos = jnp.stack((cos, cos), axis=-1).reshape(seq_len, HEAD_DIM)
            return (sin, cos)

        def _rotate_half(x):
            x1 = x[..., ::2]
            x2 = x[..., 1::2]
            return jnp.stack((-x2, x1), axis=-1).reshape(x.shape)

        def _apply_rope(x, sin, cos):
            return x * cos[None, None] + _rotate_half(x) * sin[None, None]
        B, S, E = x.shape
        H, D = (NUM_HEADS, HEAD_DIM)

        def proj(W, b):
            t = x @ W.T + b
            return t.reshape(B, S, H, D).transpose(0, 2, 1, 3)
        q = proj(Wq, bq)
        k = proj(Wk, bk)
        v = proj(Wv, bv)
        sin, cos = _rotary_emb(S, x.dtype)
        q = _apply_rope(q, sin, cos)
        k = _apply_rope(k, sin, cos)
        scores = jnp.einsum('bhqd,bhkd->bhqk', q, k) / jnp.sqrt(jnp.asarray(D, x.dtype))
        causal = jnp.tril(jnp.ones((S, S), dtype=bool))
        scores = jnp.where(causal[None, None], scores, -jnp.inf)
        weights = jax.nn.softmax(scores, axis=-1)
        out = jnp.einsum('bhqk,bhkd->bhqd', weights, v)
        out = out.transpose(0, 2, 1, 3).reshape(B, S, E)
        return out @ Wo.T + bo

    def _L1_ffn_ref(x, W_exp, b_exp, up_weights, up_bias, down_weights, W_con, b_con, down_bias):
        import jax, jax.numpy as jnp
        import numpy as np
        D_MODEL = 128
        EXPANSION = 4
        D_HIDDEN = D_MODEL * EXPANSION
        NUM_STAGES = int(np.log2(D_HIDDEN))

        def butterfly(y, weights, dim):
            lead = y.shape[:-1]
            for stage in range(weights.shape[0]):
                s = 2 ** stage
                nb = dim // (2 * s)
                yr = y.reshape(*lead, nb, 2, s)
                a = yr[..., 0, :]
                b = yr[..., 1, :]
                w = weights[stage].reshape(nb, s, 2, 2)
                na = w[..., 0, 0] * a + w[..., 0, 1] * b
                nb2 = w[..., 1, 0] * a + w[..., 1, 1] * b
                y = jnp.stack([na, nb2], axis=-2).reshape(*lead, dim)
            return y
        h = jnp.einsum('bsd,dh->bsh', x, W_exp) + b_exp
        h = butterfly(h, up_weights, D_HIDDEN)
        h = jax.nn.gelu(h + up_bias, approximate=False)
        h = butterfly(h, down_weights, D_HIDDEN)
        y = jnp.einsum('bsh,hd->bsd', h, W_con) + b_con
        return y + down_bias
    x = L0_attn_x
    x = x + 0.5 * _L0_ffn_ref(_layernorm(x, axis=-1), L0_ffn_W_router, L0_ffn_W_gate, L0_ffn_W_up, L0_ffn_W_down)
    x = x + _L0_attn_ref(_layernorm(x, axis=-1), L0_attn_W_in, L0_attn_dw_kernel, L0_attn_pw_kernel, L0_attn_conv_bias, L0_attn_W_x, L0_attn_W_dt, L0_attn_b_dt, L0_attn_A_log, L0_attn_D, L0_attn_W_out)
    x = x + 0.5 * _L0_ffn_ref(_layernorm(x, axis=-1), L0_ffn_W_router, L0_ffn_W_gate, L0_ffn_W_up, L0_ffn_W_down)
    x = x + 0.5 * _L1_ffn_ref(_layernorm(x, axis=-1), L1_ffn_W_exp, L1_ffn_b_exp, L1_ffn_up_weights, L1_ffn_up_bias, L1_ffn_down_weights, L1_ffn_W_con, L1_ffn_b_con, L1_ffn_down_bias)
    x = x + _L1_attn_ref(_layernorm(x, axis=-1), L1_attn_Wq, L1_attn_bq, L1_attn_Wk, L1_attn_bk, L1_attn_Wv, L1_attn_bv, L1_attn_Wo, L1_attn_bo)
    x = x + 0.5 * _L1_ffn_ref(_layernorm(x, axis=-1), L1_ffn_W_exp, L1_ffn_b_exp, L1_ffn_up_weights, L1_ffn_up_bias, L1_ffn_down_weights, L1_ffn_W_con, L1_ffn_b_con, L1_ffn_down_bias)
    return x

_drawn_inputs = setup_inputs


def setup_inputs(seed=0):
    import zlib

    import numpy as np

    out = dict(_drawn_inputs(seed))
    spreads = {'L0_attn_conv_bias': (0.0, 0.8),
     'L0_attn_b_dt': (0.0, 0.8),
     'L0_attn_D': (1.0, 0.6),
     'L1_attn_bq': (0.0, 2.0),
     'L1_attn_bk': (0.0, 2.0),
     'L1_attn_bv': (0.0, 0.8),
     'L1_attn_bo': (0.0, 0.8),
     'L1_ffn_b_exp': (0.0, 0.1),
     'L1_ffn_up_bias': (0.0, 0.1),
     'L1_ffn_b_con': (0.0, 0.8),
     'L1_ffn_down_bias': (0.0, 0.8)}
    factors = {'L0_attn_W_in': 8.0,
     'L0_attn_dw_kernel': 8.0,
     'L0_attn_pw_kernel': 8.0,
     'L0_attn_W_x': 8.0,
     'L0_attn_W_dt': 8.0,
     'L0_attn_A_log': 8.0,
     'L0_attn_W_out': 8.0,
     'L1_attn_Wq': 8.0,
     'L1_attn_Wk': 8.0,
     'L1_attn_Wv': 8.0,
     'L1_attn_Wo': 8.0}
    for name, (base, spread) in spreads.items():
        noise = np.random.default_rng([zlib.crc32(name.encode()), seed]).standard_normal(out[name].shape)
        drawn = base * np.exp(spread * noise) if base else spread * noise
        out[name] = jnp.asarray(drawn.astype(out[name].dtype))
    for name, factor in factors.items():
        out[name] = (out[name] * factor).astype(out[name].dtype)
    return out
```

```python
from contextlib import ExitStack

import concourse.bass as bass
from concourse import mybir

STAGES = 6

P = 128
ALU = mybir.AluOpType
ACT = mybir.ActivationFunctionType
AX = mybir.AxisListType
F32 = mybir.dt.float32
BF16 = mybir.dt.bfloat16


def macaron_kernel(nc, t, out):
    TOK, D = t["x"].shape
    NT = TOK // P
    NB = 4
    TPB = NT // NB
    L = TPB * P
    E = t["w_router"].shape[1]
    F = t["w_gate"].shape[2]
    FC = F // P
    DI = t["pw"].shape[2]
    C2 = DI // P
    NS = t["a_log"].shape[2]
    TAPS = t["dw"].shape[2]
    R = t["w_dt"].shape[0]
    HID = t["w_exp"].shape[1]
    HC = HID // P
    STG = t["up_w"].shape[0]
    NH = 16
    HD = D // NH
    GH = 4
    NG = NH // GH
    SEG = [0, 512, 1024, 896]
    PTW = 1280
    EPS = 1e-5
    KR = 72
    assert D == P and L == 512 and TAPS == 4 and NS == 8 and R == 8

    with ExitStack() as ctx:
        def sb(name, shape, dt=F32):
            return ctx.enter_context(nc.sbuf_tensor(name, shape, dt))

        def sem(name):
            return ctx.enter_context(nc.semaphore(name))

        ps = ctx.enter_context(nc.psum_tensor("ps", [P, 8, 512], F32))

        def bank(k):
            return ps[:, k, :]

        x = sb("x", [P, NT, D])
        xn = sb("xn", [P, 2, TPB, D])
        xnT = sb("xnT", [P, TOK])
        st = sb("st", [P, 2, TPB, 6])
        mv = sb("mv", [P, 2, TPB, 2])
        rs = sb("rs", [P, 2, TPB])
        ve = sb("ve", [P, TPB])
        mhalf = sb("mhalf", [P, TPB])
        ident = sb("ident", [P, P])
        ident_b = sb("ident_b", [P, P], BF16)
        ones = sb("ones", [P, P])
        wr = sb("wr", [P, E])
        wg = sb("wg", [P, E, F])
        wu = sb("wu", [P, E, F])
        wd = sb("wd", [P, E, FC, D])
        r8 = sb("r8", [P, E])
        lg = sb("lg", [P, NT, E])
        ex = sb("ex", [P, NT, E])
        oh = sb("oh", [P, 2, NT, E])
        tmp8 = sb("tmp8", [P, NT, E])
        red = sb("red", [P, 6, NT])
        wt = sb("wt", [P, NT, E])
        wtile = sb("wtile", [P, E])
        ve2 = sb("ve2", [P, NB])
        xt = sb("xt", [P, P])
        ARENA = 29 * 1024
        ar = sb("ar", [P, ARENA])

        class Arena:
            def __init__(self):
                self.at = 0

            def take(self, count, pattern=None, **k):
                a = ar[:, self.at:self.at + count]
                self.at += count
                assert self.at <= ARENA, self.at
                return a.rearrange(pattern, **k) if pattern else a

        m = Arena()
        sil = m.take(2 * F, "p (b f) -> p b f", b=2)
        hh = m.take(2 * F, "p (b f) -> p b f", b=2)
        hT = m.take(2 * F, "p (b f) -> p b f", b=2)
        bw = m.take(2 * 2 * HID, "p (b f) -> p b f", b=2)
        va_ = m.take(2 * HID, "p (b f) -> p b f", b=2)
        vb_ = m.take(2 * HID, "p (b f) -> p b f", b=2)
        vt_ = m.take(HID)
        wup = sb("wup", [P, HID])
        wdn = sb("wdn", [P, HC, D])
        bup = sb("bup", [P, HC])
        ubias = sb("ubias", [P, HC])
        ffbr = sb("ffbr", [1, 3, D])
        a_neg = sb("a_neg", [P, C2, NS])
        s = Arena()
        pwt = s.take(C2 * DI, "p (c o) -> p c o", c=C2)
        wxT = s.take(C2 * P, "p (c d) -> p c d", c=C2)
        wxs = s.take(TAPS * C2 * P, "p (k c d) -> p k c d", k=TAPS, c=C2)
        cw = s.take(TAPS * DI, "p (k o) -> p k o", k=TAPS)
        wz = s.take(DI)
        diagD = s.take(C2 * P, "p (c d) -> p c d", c=C2)
        wout = s.take(C2 * D, "p (c d) -> p c d", c=C2)
        wx3 = s.take(C2 * 96, "p (c r) -> p c r", c=C2)
        dA = s.take(C2 * NS * L, "p (c n l) -> p c n l", c=C2, n=NS)
        hs = s.take(C2 * NS * L, "p (c n l) -> p c n l", c=C2, n=NS)
        xc = s.take(C2 * L, "p (c l) -> p c l", c=C2)
        sz = s.take(C2 * L, "p (c l) -> p c l", c=C2)
        xb = s.take(L)
        eb = s.take(L)
        lb = s.take(L)
        dl = s.take(C2 * L, "p (c l) -> p c l", c=C2)
        uu = s.take(C2 * L, "p (c l) -> p c l", c=C2)
        yz = s.take(C2 * L, "p (c l) -> p c l", c=C2)
        xdf = s.take(L)
        r1 = s.take(L)
        r2 = s.take(L)
        hib = s.take(L // 2).bitcast(BF16)
        mib = s.take(L // 2).bitcast(BF16)
        xsb = s.take(L // 2).bitcast(BF16)
        selb = sb("selb", [P, 2 * NS, P], BF16)
        self_ = hs.rearrange("p c n l -> p (c n l)")[:, 0:2 * NS * P].rearrange("p (j m) -> p j m", j=2 * NS)
        cbias = sb("cbias", [P, C2])
        bdt = sb("bdt", [P, C2])
        dcol = sb("dcol", [P, C2])
        dwc = sb("dwc", [P, C2, TAPS])
        wdt = sb("wdt", [R, DI])
        f = Arena()
        gT = f.take(2 * HC * L, "p (b c l) -> p b c l", b=2, c=HC)
        a = Arena()
        wq = a.take(4 * D, "p (w d) -> p w d", w=4)
        wv = a.take(D)
        wo = a.take(D)
        cs = a.take(2 * L, "p (w l) -> p w l", w=2)
        t1 = a.take(L)
        t2 = a.take(L)
        qk = a.take(2 * L, "p (w l) -> p w l", w=2)
        q1 = a.take(2 * L, "p (w l) -> p w l", w=2)
        spl = a.take(3 * L, "p f -> p f").bitcast(BF16).rearrange("p (j w l) -> p j w l", j=3, w=2)
        qs = a.take(NH * L // 2).bitcast(BF16).rearrange("p (h l) -> p h l", h=NH)
        ks = a.take(NH * L // 2).bitcast(BF16).rearrange("p (h l) -> p h l", h=NH)
        va = a.take(TPB * NH * 32, "p (k h e) -> p k h e", k=TPB, h=NH)
        pt = a.take(GH * PTW, "p (h f) -> p h f", h=GH)
        ob = a.take(L)
        on = a.take(TPB * D, "p (k e) -> p k e", k=TPB)
        onT = a.take(L)
        nm = a.take(TPB * NH // 2).bitcast(BF16).rearrange("p (k h) -> p k h", k=TPB)
        mTs = a.take(L // 2).bitcast(BF16)
        rden = a.take(TPB * GH, "p (k j) -> p k j", k=TPB)
        maskf = a.take(2 * P, "p (w d) -> p w d", w=2)
        maskb = sb("maskb", [P, 2, P], BF16)
        bqk = sb("bqk", [P, 4])
        abr = sb("abr", [1, 2, D])

        qk_dram = nc.dram_tensor("qk_parts", [NB, 3, 2, P, L], BF16, kind="Internal").ap()

        m_dram = nc.dram_tensor("row_maxima", [NB, NH, L], BF16, kind="Internal").ap()

        x_loaded = sem("x_loaded")
        const_loaded = sem("const_loaded")
        moe_loaded = sem("moe_loaded")
        small_loaded = sem("small_loaded")
        pool_chain = sem("pool_chain")
        vec_chain = sem("vec_chain")
        act_chain = sem("act_chain")
        ln_stats_ready = sem("ln_stats_ready")
        ln_rstd_ready = sem("ln_rstd_ready")
        xn_ready = sem("xn_ready")
        xn_turned = sem("xn_turned")
        xnT_ready = sem("xnT_ready")
        logits_ready = sem("logits_ready")
        shifted_ready = sem("shifted_ready")
        expl_ready = sem("expl_ready")
        xt_ready = sem("xt_ready")
        wtile_ready = sem("wtile_ready")
        gate_ready = sem("gate_ready")
        up_ready = sem("up_ready")
        sil_ready = sem("sil_ready")
        h_ready = sem("h_ready")
        h_turned = sem("h_turned")
        hT_ready = sem("hT_ready")
        down_done = sem("down_done")
        y_used = sem("y_used")
        bw_loaded = [sem("bw_loaded_even"), sem("bw_loaded_odd")]
        bw_used = sem("bw_used")
        fly_ready = sem("fly_ready")
        fly_turned = sem("fly_turned")
        ffn_w_ready = sem("ffn_w_ready")
        scan_loaded = sem("scan_loaded")
        scan_vec_ready = sem("scan_vec_ready")
        cw_psum = sem("cw_psum")
        cw_ready = sem("cw_ready")
        aexp_ready = sem("aexp_ready")
        xc_psum = sem("xc_psum")
        z_psum = sem("z_psum")
        xc_ready = sem("xc_ready")
        sz_ready = sem("sz_ready")
        xd_psum = sem("xd_psum")
        xd_act = sem("xd_act")
        xd_vec = sem("xd_vec")
        xs_ready = sem("xs_ready")
        dt_psum = sem("dt_psum")
        sp_ready = sem("sp_ready")
        delta_ready = sem("delta_ready")
        u_ready = sem("u_ready")
        dA_ready = sem("dA_ready")
        b_psum = sem("b_psum")
        b_used = sem("b_used")
        c_psum = sem("c_psum")
        hc_ready = sem("hc_ready")
        ysum_ready = sem("ysum_ready")
        yz_ready = sem("yz_ready")
        o_psum = sem("o_psum")
        scan_used = sem("scan_used")
        ff_h_psum = sem("ff_h_psum")
        ff_g_ready = sem("ff_g_ready")
        ff_o_psum = sem("ff_o_psum")
        ff_o_used = sem("ff_o_used")
        att_loaded = sem("att_loaded")
        att_const = sem("att_const")
        qkv_psum = sem("qkv_psum")
        rope_ready = sem("rope_ready")
        part_act = sem("part_act")
        part_vec = sem("part_vec")
        parts_stored = sem("parts_stored")
        qk_loaded = sem("qk_loaded")
        v_ready = sem("v_ready")
        max_psum = sem("max_psum")
        max_used = sem("max_used")
        m_turned = sem("m_turned")
        m_copied = sem("m_copied")
        m_stored = sem("m_stored")
        m_loaded = sem("m_loaded")
        s_psum = sem("s_psum")
        p_ready = sem("p_ready")
        pv_psum = sem("pv_psum")
        o_copied = sem("o_copied")
        o_turned = sem("o_turned")
        on_ready = sem("on_ready")
        on_turned = sem("on_turned")
        onT_ready = sem("onT_ready")
        ao_psum = sem("ao_psum")
        ao_used = sem("ao_used")
        x_done = sem("x_done")
        out_stored = sem("out_stored")

        x_tiles = t["x"].rearrange("(i p) d -> p i d", p=P)
        out_tiles = out.rearrange("(i p) d -> p i d", p=P)
        NMAX = [(3, 2, 1), (2, 2, 1), (1, 4, 2), (0, 8, 4)]
        MAXSTEPS = [(qt, h0, nh, pb) for qt, nh, pb in NMAX for h0 in range(0, NH, nh)]
        NMS = len(MAXSTEPS)

        block = ctx.enter_context(nc.Block())

        @block.sync
        def _(sp):
            sp.dma_start(x[:, :, :], x_tiles).then_inc(x_loaded, 16)
            for dst, src in ((ident[:, :], t["ident"]), (wr[:, :], t["w_router"]), (r8[:, :], t["rank8"])):
                sp.dma_start(dst, src).then_inc(const_loaded, 16)
            sp.dma_start(wg[:, :, :], t["w_gate"]).then_inc(moe_loaded, 16)
            sp.dma_start(wu[:, :, :], t["w_up"]).then_inc(moe_loaded, 16)
            sp.dma_start(wd[:, :, :, :], t["w_down"]).then_inc(moe_loaded, 16)
            small = [(ubias[:, :], t["up_bias"]), (ffbr[:, 0, :], t["b_con"]), (ffbr[:, 1, :], t["down_bias"]),
                     (cbias[:, :], t["conv_bias"]), (bdt[:, :], t["b_dt"]), (dcol[:, :], t["dskip"]),
                     (dwc[:, :, :], t["dw"]), (wdt[:, :], t["w_dt"]), (a_neg[:, :, :], t["a_log"]),
                     (bqk[:, :], t["bqk"]), (abr[:, 0, :], t["bv"]), (abr[:, 1, :], t["bo"]),
                     (va_[:, 0, :], t["w_exp"]), (va_[0:1, 1, :], t["b_exp"])]
            for dst, src in small:
                sp.dma_start(dst, src).then_inc(small_loaded, 16)
            for k in range(2 * STG):
                src = t["up_w"][k] if k < STG else t["down_w"][2 * STG - 1 - k]
                if k >= 2:
                    sp.wait_ge(bw_used, k - 1)
                sp.dma_start(bw[:, k % 2, :], src.partition_broadcast(P)).then_inc(bw_loaded[k % 2], 16)
                if k == STG - 1:
                    sp.wait_ge(fly_turned, 1)
                    sp.dma_start(va_[:, 0, :], t["w_conT"]).then_inc(small_loaded, 16)
            if STAGES > 1:
                sp.wait_ge(y_used, NT + 1)
                sp.wait_ge(fly_turned, 2)
                for dst, src in ((pwt, t["pw"]), (wxT, t["wxT"]), (wz, t["wz"]), (wout, t["w_out"]),
                                 (wx3, t["w_x3"]), (self_[0:96], t["sel"])):
                    sp.dma_start(dst, src).then_inc(scan_loaded, 16)
            if STAGES > 4:
                sp.wait_ge(ff_o_used, NB)
                for dst, src in ((wq, t["wq"]), (wv, t["wv"]), (wo, t["wo"]), (cs, t["cossin"]),
                                 (maskf, t["mask"])):
                    sp.dma_start(dst, src).then_inc(att_loaded, 16)
                sp.wait_ge(att_const, 2)
                sp.dma_start(ks[48:49, :, :], t["ones_row"]).then_inc(att_loaded, 16)
                for b in range(NB):
                    sp.wait_ge(part_vec, 2 * b + 2)
                    sp.wait_ge(part_act, 2 * b + 2)
                    sp.dma_start(qk_dram[b].rearrange("j w p l -> p j w l"), spl).then_inc(parts_stored, 16)
                    sp.wait_ge(parts_stored, 16 * (b + 1))
                    if b >= 1:
                        sp.wait_ge(pv_psum, NG * b)
                    for r, (i, j) in enumerate(((0, 0), (0, 1), (1, 0), (1, 1), (0, 2), (2, 0))):
                        sp.dma_start(qs[8 * r:8 * r + 8, :, :],
                                     qk_dram[b, i, 0].rearrange("(h d) l -> d h l", d=HD)).then_inc(qk_loaded, 16)
                        sp.dma_start(ks[8 * r:8 * r + 8, :, :],
                                     qk_dram[b, j, 1].rearrange("(h d) l -> d h l", d=HD)).then_inc(qk_loaded, 16)
                    sp.wait_ge(m_copied, b + 1)
                    sp.dma_start(m_dram[b], mTs[0:NH, :]).then_inc(m_stored, 16)
                    sp.wait_ge(m_stored, 16 * (b + 1))
                    sp.dma_start(qs[48:49, :, :], m_dram[b].unsqueeze(0)).then_inc(m_loaded, 16)
            for b in range(NB):
                sp.wait_ge(x_done, b + 1)
                sp.dma_start(out_tiles[:, TPB * b:TPB * (b + 1), :],
                             x[:, TPB * b:TPB * (b + 1), :]).then_inc(out_stored, 16)
            sp.wait_ge(out_stored, 16 * NB)

        @block.gpsimd
        def _(pool):
            chain = [0]

            def link(ins):
                chain[0] += 1
                ins.then_inc(pool_chain, 1)
                pool.wait_ge(pool_chain, chain[0])

            def ln_rstd(n):
                pool.wait_ge(ln_stats_ready, n + 1)
                link(nc.gpsimd.tensor_scalar(ve[:, :], mv[:, n % 2, :, 1], EPS, None, ALU.add))
                nc.gpsimd.tensor_tensor(rs[:, n % 2, :], ve[:, :], mhalf[:, :], ALU.pow).then_inc(ln_rstd_ready, 1)

            nc.gpsimd.memset(ones[:, :], 1.0)
            nc.gpsimd.memset(vb_[:, :, :], 0.0)
            link(nc.gpsimd.memset(mhalf[:, :], -0.5))
            for g in range(NB):
                ln_rstd(g)

            def stage(k, strd, parts, src, dst, up):
                nb = HID // (2 * strd)
                pool.wait_ge(bw_loaded[k % 2], 16 * (k // 2 + 1))
                w = bw[:, k % 2, :].rearrange("p (n s o i) -> p n s o i", n=nb, s=strd, o=2)
                for q in range(parts):
                    np_ = P if q == 0 else 1
                    a_ = src[0:np_, q, :].rearrange("p (n o s) -> p n o s", n=nb, o=2)
                    d_ = dst[0:np_, q, :].rearrange("p (n o s) -> p n o s", n=nb, o=2)
                    t_ = vt_[0:np_, :].rearrange("p (n o s) -> p n o s", n=nb, o=2)
                    for o in range(2):
                        w0 = w[0:np_, :, :, o, 0] if up else w[0:np_, :, :, 0, o]
                        w1 = w[0:np_, :, :, o, 1] if up else w[0:np_, :, :, 1, o]
                        nc.gpsimd.tensor_tensor(d_[:, :, o, :], a_[:, :, 0, :], w0, ALU.mult)
                        link(nc.gpsimd.tensor_tensor(t_[:, :, o, :], a_[:, :, 1, :], w1, ALU.mult))
                        link(nc.gpsimd.tensor_tensor(d_[:, :, o, :], d_[:, :, o, :], t_[:, :, o, :], ALU.add))

            pool.wait_ge(small_loaded, 16 * 14)
            src, dst = va_, vb_
            for k in range(STG):
                stage(k, 2 ** k, 2, src, dst, True)
                pool.sem_inc(bw_used, 1)
                src, dst = dst, src
            link(nc.gpsimd.tensor_copy(wup[:, :], src[:, 0, :]))
            pool.sem_inc(fly_ready, 1)
            pool.wait_ge(fly_turned, 1)
            pool.wait_ge(small_loaded, 16 * 15)
            src, dst = va_, vb_
            for k in range(STG, 2 * STG):
                stage(k, 2 ** (2 * STG - 1 - k), 1, src, dst, False)
                pool.sem_inc(bw_used, 1)
                src, dst = dst, src
            pool.sem_inc(fly_ready, 1)
            for n in range(NB, NB * STAGES):
                if n == 4 * NB:
                    pool.wait_ge(ff_o_used, NB)
                    nc.gpsimd.memset(qs[0:KR, :, :], 0.0)
                    nc.gpsimd.memset(va[:, :, :, :], 1.0)
                    nc.gpsimd.memset(ks[0:KR, :, :], 0.0).then_inc(att_const, 1)
                ln_rstd(n)

        @block.tensor
        def _(pe):
            def mm(o, l, r, first=True, last=True):
                return nc.tensor.matmul(o, l, r, start=first, stop=last)

            def turn(n):
                pe.wait_ge(xn_ready, n + 1)
                if n >= 1:
                    pe.wait_ge(xnT_ready, n)
                for k in range(TPB):
                    ins = nc.tensor.transpose(ps[:, 7, k * P:(k + 1) * P], xn[:, n % 2, k, :], ident[:, :])
                ins.then_inc(xn_turned, 1)

            def moe(u, n0):
                for g in range(NB):
                    turn(n0 + g)
                pe.wait_ge(xnT_ready, n0 + NB)
                for i in range(NT):
                    ins = mm(ps[:, 6, E * i:E * i + E], xnT[:, i * P:(i + 1) * P], wr[:, :])
                ins.then_inc(logits_ready, 1)
                pe.wait_ge(moe_loaded, 48)
                pe.wait_ge(shifted_ready, u + 1)
                with pe.Fori(0, NT) as i:
                    s0 = u * NT * E + i * E
                    pe.wait_ge(y_used, i + (u * NT + 1))
                    pe.wait_ge(xt_ready, i + (u * NT + 1))
                    for e in range(E + 2):
                        if e < E:
                            if e >= 2:
                                pe.wait_ge(sil_ready, s0 + (e - 1))
                            mm(bank(e % 2), xt[:, :], wg[:, e, :]).then_inc(gate_ready, 1)
                            if e >= 2:
                                pe.wait_ge(h_ready, s0 + (e - 1))
                            mm(bank(2 + e % 2), xt[:, :], wu[:, e, :]).then_inc(up_ready, 1)
                        if 1 <= e <= E:
                            q = e - 1
                            pe.wait_ge(h_ready, s0 + (q + 1))
                            if q >= 2:
                                pe.wait_ge(hT_ready, s0 + (q - 1))
                            for f_ in range(FC):
                                ins = nc.tensor.transpose(ps[:, 4 + q % 2, f_ * P:(f_ + 1) * P],
                                                          hh[:, q % 2, f_ * P:(f_ + 1) * P], ident[:, :])
                            ins.then_inc(h_turned, 1)
                        if e >= 2:
                            q = e - 2
                            pe.wait_ge(hT_ready, s0 + (q + 1))
                            for f_ in range(FC):
                                ins = mm(ps[:, 6, 0:D], hT[:, q % 2, f_ * P:(f_ + 1) * P], wd[:, q, f_, :],
                                         first=(q == 0 and f_ == 0), last=(q == E - 1 and f_ == FC - 1))
                            ins.then_inc(down_done, 1)

            def fly():
                pe.wait_ge(fly_ready, 1)
                for c in range(HC):
                    ins = mm(ps[:, 7, c:c + 1], vb_[0:1, 1, c * P:(c + 1) * P], ones[0:1, 0:1])
                ins.then_inc(fly_turned, 1)
                pe.wait_ge(fly_ready, 2)
                pe.wait_ge(ffn_w_ready, 1)
                fin = vb_ if STG % 2 else va_
                for c in range(HC):
                    ins = nc.tensor.transpose(ps[:, 7, c * P:(c + 1) * P], fin[:, 0, c * P:(c + 1) * P], ident[:, :])
                ins.then_inc(fly_turned, 1)
                pe.wait_ge(ffn_w_ready, 2)

            def scan(n0):
                pe.wait_ge(scan_loaded, 16 * 6)
                pe.wait_ge(scan_vec_ready, 1)
                for k in range(TAPS):
                    for c in range(C2):
                        ins = mm(ps[:, k // 2, (k % 2) * DI:(k % 2 + 1) * DI], wxs[:, k, c, :], pwt[:, c, :],
                                 first=(c == 0), last=(c == C2 - 1))
                ins.then_inc(cw_psum, 1)
                pe.wait_ge(cw_ready, 1)
                pe.wait_ge(scan_vec_ready, 2)
                for b in range(NB):
                    turn(n0 + b)
                    pe.wait_ge(xnT_ready, n0 + b + 1)
                    xb_ = xnT[:, b * L:(b + 1) * L]
                    if b >= 1:
                        pe.wait_ge(scan_used, b)
                    for c in range(C2):
                        for k in (3, 2, 1, 0):
                            d_ = TAPS - 1 - k
                            ins = nc.tensor.matmul(ps[:, c, d_:L], cw[:, k, c * P:(c + 1) * P], xb_[:, 0:L - d_],
                                                   start=(k == 3), stop=(k == 0))
                        ins.then_inc(xc_psum, 1)
                    for c in range(C2):
                        mm(bank(2 + c), wz[:, c * P:(c + 1) * P], xb_).then_inc(z_psum, 1)
                    pe.wait_ge(xc_ready, 2 * b + 2)
                    for c in range(C2):
                        ins = mm(ps[0:96, 6, :], wx3[:, c, :], xc[:, c, :], first=(c == 0), last=(c == 1))
                    ins.then_inc(xd_psum, 1)
                    pe.wait_ge(xd_act, 4 * b + 1)
                    for c in range(C2):
                        mm(bank(c), wdt[:, c * P:(c + 1) * P], xdf[0:R, :]).then_inc(dt_psum, 1)
                    pe.wait_ge(xs_ready, b + 1)
                    pe.wait_ge(sz_ready, 2 * b + 2)
                    pe.wait_ge(sp_ready, 2 * b + 2)

                    def ysum(j):
                        for c in range(C2):
                            pe.wait_ge(hc_ready, 8 * b + 2 * j + c + 1)
                            for q in range(2):
                                ins = mm(bank(c), ident[:, :], hs[:, c, 2 * j + q, :],
                                         first=(j == 0 and q == 0), last=False)
                        return ins

                    for j in range(NS // 2):
                        if j >= 1:
                            pe.wait_ge(b_used, 8 * b + 2 * j)
                        for q in range(2):
                            ins = mm(bank(2 + q), selb[0:96, 2 * j + q, :], xsb[0:96, :])
                        ins.then_inc(b_psum, 1)
                        if j >= 1:
                            pe.wait_ge(hc_ready, 8 * b + 2 * j)
                        for q in range(2):
                            ins = mm(bank(4 + q), selb[0:96, NS + 2 * j + q, :], xsb[0:96, :])
                        ins.then_inc(c_psum, 1)
                        if j >= 1:
                            ysum(j - 1)
                    ysum(NS // 2 - 1)
                    for c in range(C2):
                        ins = mm(bank(c), diagD[:, c, :], xc[:, c, :], first=False, last=True)
                    ins.then_inc(ysum_ready, 1)
                    pe.wait_ge(yz_ready, 2 * b + 2)
                    for k in range(TPB):
                        for c in range(C2):
                            ins = mm(ps[:, 6, k * P:(k + 1) * P], yz[:, c, k * P:(k + 1) * P], wout[:, c, :],
                                     first=(c == 0), last=(c == 1))
                    ins.then_inc(o_psum, 1)

            def ffn(u, n0):
                for g in range(NB):
                    turn(n0 + g)
                for b in range(NB):
                    n = u * NB + b
                    pe.wait_ge(xnT_ready, n0 + b + 1)
                    for c in range(HC):
                        if n * HC + c >= 2:
                            pe.wait_ge(ff_g_ready, n * HC + c - 1)
                        mm(bank(c % 2), wup[:, c * P:(c + 1) * P], xnT[:, b * L:(b + 1) * L]).then_inc(ff_h_psum, 1)
                    if n >= 2:
                        pe.wait_ge(ff_o_used, n - 1)
                    pe.wait_ge(ff_g_ready, n * HC + HC)
                    for k in range(TPB):
                        o_ = ps[:, 2 + b % 2, k * P:(k + 1) * P]
                        mm(o_, ones[0:1, :], ffbr[0:1, 2, :], True, False)
                        for c in range(HC):
                            ins = mm(o_, gT[:, b % 2, c, k * P:(k + 1) * P], wdn[:, c, :], False, c == HC - 1)
                    ins.then_inc(ff_o_psum, 1)

            def attend(n0):
                pe.wait_ge(att_loaded, 16 * 5)
                for b in range(NB):
                    turn(n0 + b)
                    pe.wait_ge(xnT_ready, n0 + b + 1)
                    if b >= 1:
                        pe.wait_ge(ao_used, b)
                    for w in range(4):
                        mm(bank(w), wq[:, w, :], xnT[:, b * L:(b + 1) * L]).then_inc(qkv_psum, 1)
                    for k in range(TPB):
                        o_ = ps[:, 4, k * P:(k + 1) * P]
                        mm(o_, ones[0:1, :], abr[0:1, 0, :], True, False)
                        ins = mm(o_, xnT[:, b * L + k * P:b * L + (k + 1) * P], wv, False, True)
                    ins.then_inc(qkv_psum, 1)
                    pe.wait_ge(v_ready, b + 1)
                    pe.wait_ge(rope_ready, b + 1)
                    pe.wait_ge(qk_loaded, 16 * 12 * (b + 1))
                    pe.wait_ge(att_loaded, 16 * 6)
                    for j, (qt, h0, nh, pb) in enumerate(MAXSTEPS):
                        n = b * NMS + j
                        if n >= 3:
                            pe.wait_ge(max_used, n - 2)
                        w_ = P * (qt + 1)
                        for h in range(h0, h0 + nh):
                            k_ = 2 * (j % 3) + (h - h0) // pb
                            c_ = ((h - h0) % pb) * w_
                            mm(ps[:, k_, c_:c_ + w_], qs[0:48, h, qt * P:(qt + 1) * P], ks[0:48, h, 0:w_],
                               True, False)
                            ins = mm(ps[:, k_, c_ + qt * P:c_ + w_], ident_b[:, :], maskb[:, 0, :], False, True)
                        ins.then_inc(max_psum, 1)
                    pe.wait_ge(max_used, (b + 1) * NMS)
                    mt_ = ps[0:NH, 7, 0:L // 2].bitcast(BF16)
                    for k in range(TPB):
                        ins = nc.tensor.transpose(mt_[:, k * P:(k + 1) * P], nm[:, k, :], ident_b[:, :])
                    ins.then_inc(m_turned, 1)
                    pe.wait_ge(m_loaded, 16 * (b + 1))

                    def scores(h):
                        n = b * NH + h
                        if h >= 2:
                            pe.wait_ge(p_ready, n - 1)
                        s_ = ps[:, 3 * (h % 2):3 * (h % 2) + 3, :].rearrange("p k f -> p (k f)")
                        for kt in range(TPB):
                            w_ = L - kt * P
                            mm(s_[:, SEG[kt]:SEG[kt] + w_], ks[0:KR, h, kt * P:(kt + 1) * P],
                               qs[0:KR, h, kt * P:L], True, False)
                            ins = mm(s_[:, SEG[kt]:SEG[kt] + P], ident_b[:, :], maskb[:, 1, :], False, True)
                        ins.then_inc(s_psum, 1)

                    def values(g):
                        pe.wait_ge(p_ready, b * NH + GH * (g + 1))
                        if b * NG + g >= 1:
                            pe.wait_ge(o_copied, b * NG + g)
                        for kt in range(TPB):
                            w_ = L - kt * P
                            for j in range(GH):
                                ins = nc.tensor.matmul(ps[32 * j:32 * j + 32, 6, kt * P:L], va[:, kt, GH * g + j, :],
                                                       pt[:, j, SEG[kt]:SEG[kt] + w_],
                                                       start=(kt == 0), stop=(kt == TPB - 1))
                        ins.then_inc(pv_psum, 1)

                    def turn_o(g):
                        n = b * NG + g
                        pe.wait_ge(o_copied, n + 1)
                        pe.wait_ge(on_ready, n) if g >= 1 else None
                        for k in range(TPB):
                            ins = nc.tensor.transpose(ps[:, 7, k * P:(k + 1) * P], ob[:, k * P:(k + 1) * P],
                                                      ident[:, :])
                        ins.then_inc(o_turned, 1)

                    for g in range(NG):
                        for h in range(GH * g, GH * g + GH):
                            scores(h)
                        values(g)
                        turn_o(g)
                    pe.wait_ge(on_ready, NG * (b + 1))
                    for k in range(TPB):
                        ins = nc.tensor.transpose(ps[:, 7, k * P:(k + 1) * P], on[:, k, :], ident[:, :])
                    ins.then_inc(on_turned, 1)
                    pe.wait_ge(onT_ready, b + 1)
                    for k in range(TPB):
                        o_ = ps[:, 0, k * P:(k + 1) * P]
                        mm(o_, ones[0:1, :], abr[0:1, 1, :], True, False)
                        ins = mm(o_, onT[:, k * P:(k + 1) * P], wo, False, True)
                    ins.then_inc(ao_psum, 1)

            pe.wait_ge(const_loaded, 48)
            pe.wait_ge(small_loaded, 16 * 14)
            moe(0, 0)
            fly()
            if STAGES > 1:
                scan(NB)
            if STAGES > 2:
                moe(1, 2 * NB)
            if STAGES > 3:
                ffn(0, 3 * NB)
            if STAGES > 4:
                attend(4 * NB)
            if STAGES > 5:
                ffn(1, 5 * NB)

        @block.scalar
        def _(act):
            chain = [0]

            def link(ins):
                chain[0] += 1
                ins.then_inc(act_chain, 1)
                act.wait_ge(act_chain, chain[0])

            def take_turned(n, g):
                act.wait_ge(xn_turned, n + 1)
                nc.scalar.copy(xnT[:, g * L:(g + 1) * L], bank(7)).then_inc(xnT_ready, 1)

            def moe(u, n0):
                for g in range(NB):
                    take_turned(n0 + g, g)
                act.wait_ge(shifted_ready, u + 1)
                nc.scalar.activation(ex[:, :, :], tmp8[:, :, :], ACT.Exp).then_inc(expl_ready, 1)
                act.wait_ge(xnT_ready, n0 + NB)
                with act.Fori(0, NT) as i:
                    s0 = u * NT * E + i * E
                    act.wait_ge(y_used, i + (u * NT + 1))
                    nc.scalar.copy(xt[:, :], xnT[:, bass.ds(i * P, P)]).then_inc(xt_ready, 1)
                    for e in range(E + 1):
                        if e < E:
                            act.wait_ge(gate_ready, s0 + (e + 1))
                            if e >= 2:
                                act.wait_ge(h_ready, s0 + (e - 1))
                            nc.scalar.activation(sil[:, e % 2, :], bank(e % 2), ACT.Silu).then_inc(sil_ready, 1)
                        if e >= 1:
                            q = e - 1
                            act.wait_ge(h_turned, s0 + (q + 1))
                            if q >= 2:
                                act.wait_ge(down_done, s0 + (q - 1))
                            nc.scalar.copy(hT[:, q % 2, :], bank(4 + q % 2)).then_inc(hT_ready, 1)

            def scan(n0):
                act.wait_ge(cw_psum, 1)
                nc.scalar.copy(cw.rearrange("p k o -> p (k o)"),
                               ps[:, 0:2, :].rearrange("p k f -> p (k f)")).then_inc(cw_ready, 1)
                for b in range(NB):
                    take_turned(n0 + b, b)
                    if b >= 1:
                        act.wait_ge(scan_used, b)
                    for c in range(C2):
                        act.wait_ge(xc_psum, 2 * b + c + 1)
                        nc.scalar.activation(xc[:, c, :], bank(c), ACT.Silu,
                                             bias=cbias[:, c:c + 1]).then_inc(xc_ready, 1)
                    for c in range(C2):
                        act.wait_ge(z_psum, 2 * b + c + 1)
                        nc.scalar.activation(sz[:, c, :], bank(2 + c), ACT.Silu).then_inc(sz_ready, 1)
                    act.wait_ge(xd_psum, b + 1)
                    nc.scalar.copy(xdf[0:R, :], ps[0:R, 6, :]).then_inc(xd_act, 1)
                    nc.scalar.copy(hib[0:96, :], ps[0:96, 6, :]).then_inc(xd_act, 1)
                    nc.scalar.copy(xsb[0:32, :], ps[0:32, 6, :]).then_inc(xd_act, 1)
                    act.wait_ge(xd_vec, 2 * b + 1)
                    nc.scalar.copy(mib[0:96, :], r1[0:96, :]).then_inc(xd_act, 1)
                    nc.scalar.copy(xsb[32:64, :], r1[32:64, :])
                    act.wait_ge(xd_vec, 2 * b + 2)
                    nc.scalar.copy(xsb[64:96, :], r2[64:96, :]).then_inc(xs_ready, 1)
                    for c in range(C2):
                        act.wait_ge(dt_psum, 2 * b + c + 1)
                        if c == 1:
                            act.wait_ge(delta_ready, 2 * b + 1)
                        nc.scalar.activation(xb, bank(c), ACT.Identity, bias=bdt[:, c:c + 1])
                        link(nc.scalar.activation(eb, bank(c), ACT.Abs, bias=bdt[:, c:c + 1]))
                        link(nc.scalar.activation(eb, eb, ACT.Exp, scale=-1.0))
                        nc.scalar.activation(lb, eb, ACT.Ln, bias=1.0).then_inc(sp_ready, 1)
                    for j in range(NS // 2):
                        for c in range(C2):
                            act.wait_ge(delta_ready, 2 * b + c + 1)
                            for n in (2 * j, 2 * j + 1):
                                ins = nc.scalar.activation(dA[:, c, n, 1:L], dl[:, c, 1:L], ACT.Exp,
                                                           scale=a_neg[:, c, n:n + 1])
                            ins.then_inc(dA_ready, 1)

            def ffn(u, n0):
                for g in range(NB):
                    take_turned(n0 + g, g)
                for b in range(NB):
                    n = u * NB + b
                    for c in range(HC):
                        act.wait_ge(ff_h_psum, n * HC + c + 1)
                        if n >= 2:
                            act.wait_ge(ff_o_psum, n - 1)
                        nc.scalar.activation(gT[:, b % 2, c, :], bank(c % 2), ACT.Gelu,
                                             bias=bup[:, c:c + 1]).then_inc(ff_g_ready, 1)

            def attend(n0):
                for b in range(NB):
                    take_turned(n0 + b, b)
                    act.wait_ge(rope_ready, b + 1)
                    nc.scalar.copy(spl[:, 0, :, :], qk).then_inc(part_act, 1)
                    act.wait_ge(part_vec, 2 * b + 1)
                    nc.scalar.copy(spl[:, 1, :, :], q1).then_inc(part_act, 1)
                    act.wait_ge(m_turned, b + 1)
                    nc.scalar.copy(mTs[0:NH, :], ps[0:NH, 7, 0:L // 2].bitcast(BF16)).then_inc(m_copied, 1)
                    for g in range(NG):
                        if b * NG + g >= 1:
                            act.wait_ge(pv_psum, b * NG + g)
                        for j in range(GH):
                            h = GH * g + j
                            act.wait_ge(s_psum, b * NH + h + 1)
                            s_ = ps[:, 3 * (h % 2):3 * (h % 2) + 3, :].rearrange("p k f -> p (k f)")
                            nc.scalar.activation(pt[:, j, :], s_[:, 0:PTW], ACT.Exp,
                                                 scale=float(HD) ** -0.5).then_inc(p_ready, 1)
                        act.wait_ge(pv_psum, b * NG + g + 1)
                        if b * NG + g >= 1:
                            act.wait_ge(o_turned, b * NG + g)
                        nc.scalar.copy(ob, bank(6)).then_inc(o_copied, 1)
                    act.wait_ge(on_turned, b + 1)
                    nc.scalar.copy(onT, bank(7)).then_inc(onT_ready, 1)

            moe(0, 0)
            act.wait_ge(small_loaded, 16 * 14)
            nc.scalar.activation(a_neg[:, :, :], a_neg[:, :, :], ACT.Exp).then_inc(aexp_ready, 1)
            if STAGES > 1:
                scan(NB)
            if STAGES > 2:
                moe(1, 2 * NB)
            if STAGES > 3:
                ffn(0, 3 * NB)
            if STAGES > 4:
                attend(4 * NB)
            if STAGES > 5:
                ffn(1, 5 * NB)

        @block.vector
        def _(dve):
            chain = [0]
            v = nc.vector

            def link(ins):
                chain[0] += 1
                ins.then_inc(vec_chain, 1)
                dve.wait_ge(vec_chain, chain[0])

            def norm(n, g):
                q = n % 2
                for k in range(TPB):
                    ins = v.bn_stats(st[:, q, k, :], x[:, TPB * g + k, :])
                link(ins)
                for k in range(TPB):
                    ins = v.bn_aggr(mv[:, q, k, :], st[:, q, k, :])
                ins.then_inc(ln_stats_ready, 1)
                dve.wait_ge(ln_rstd_ready, n + 1)
                if n >= 2:
                    dve.wait_ge(xn_turned, n - 1)
                for k in range(TPB):
                    ins = v.tensor_scalar(xn[:, q, k, :], x[:, TPB * g + k, :], mv[:, q, k, 0:1], rs[:, q, k:k + 1],
                                          ALU.subtract, ALU.mult)
                ins.then_inc(xn_ready, 1)

            def pick(k, scores):
                link(v.tensor_reduce(red[:, k, :], scores, AX.X, ALU.max))
                link(v.tensor_tensor(oh[:, k, :, :], scores, red[:, k, :].unsqueeze(2).to_broadcast([P, NT, E]),
                                     ALU.is_equal))
                link(v.tensor_tensor(oh[:, k, :, :], oh[:, k, :, :],
                                     r8[:, :].unsqueeze(1).to_broadcast([P, NT, E]), ALU.mult))
                link(v.tensor_reduce(red[:, 2 + k, :], oh[:, k, :, :], AX.X, ALU.max))
                link(v.tensor_tensor(oh[:, k, :, :], oh[:, k, :, :],
                                     red[:, 2 + k, :].unsqueeze(2).to_broadcast([P, NT, E]), ALU.is_equal))

            def route(u):
                dve.wait_ge(logits_ready, u + 1)
                link(v.tensor_copy(lg[:, :, :], ps[:, 6, 0:NT * E].rearrange("p (i e) -> p i e", e=E)))
                pick(0, lg[:, :, :])
                v.tensor_tensor(tmp8[:, :, :], lg[:, :, :], red[:, 0, :].unsqueeze(2).to_broadcast([P, NT, E]),
                                ALU.subtract).then_inc(shifted_ready, 1)
                link(v.scalar_tensor_tensor(lg[:, :, :], oh[:, 0, :, :], -3.0e38, lg[:, :, :], ALU.mult, ALU.add))
                pick(1, lg[:, :, :])
                link(v.tensor_tensor(oh[:, 0, :, :], oh[:, 0, :, :], oh[:, 1, :, :], ALU.add))
                dve.wait_ge(expl_ready, u + 1)
                link(v.tensor_tensor(wt[:, :, :], oh[:, 0, :, :], ex[:, :, :], ALU.mult))
                link(v.tensor_reduce(red[:, 4, :], wt[:, :, :], AX.X, ALU.add))
                link(v.reciprocal(red[:, 5, :], red[:, 4, :]))
                link(v.tensor_tensor(wt[:, :, :], wt[:, :, :], red[:, 5, :].unsqueeze(2).to_broadcast([P, NT, E]),
                                     ALU.mult))

            def moe(u, n0):
                for g in range(NB):
                    norm(n0 + g, g)
                route(u)
                with dve.Fori(0, NT) as i:
                    s0 = u * NT * E + i * E
                    v.tensor_copy(wtile[:, :], wt[:, bass.ds(i, 1), :].rearrange("p o e -> p (o e)")
                                  ).then_inc(wtile_ready, 1)
                    dve.wait_ge(wtile_ready, i + (u * NT + 1))
                    for e in range(E):
                        dve.wait_ge(sil_ready, s0 + (e + 1))
                        dve.wait_ge(up_ready, s0 + (e + 1))
                        if e >= 2:
                            dve.wait_ge(h_turned, s0 + (e - 1))
                        v.scalar_tensor_tensor(hh[:, e % 2, :], sil[:, e % 2, :], wtile[:, e:e + 1],
                                               bank(2 + e % 2), ALU.mult, ALU.mult).then_inc(h_ready, 1)
                    dve.wait_ge(down_done, s0 + E)
                    xi = x[:, bass.ds(i, 1), :].rearrange("p o d -> p (o d)")
                    v.scalar_tensor_tensor(xi, ps[:, 6, 0:D], 0.5, xi, ALU.mult, ALU.add).then_inc(y_used, 1)
                dve.wait_ge(y_used, NT * (u + 1) + 1)

            def fly():
                dve.wait_ge(small_loaded, 16 * 14)
                dve.wait_ge(fly_turned, 1)
                v.tensor_tensor(bup[:, :], ps[:, 7, 0:HC], ubias[:, :], ALU.add).then_inc(ffn_w_ready, 1)
                dve.wait_ge(fly_turned, 2)
                v.tensor_tensor(ffbr[:, 2, :], ffbr[:, 0, :], ffbr[:, 1, :], ALU.add)
                v.tensor_copy(wdn[:, :, :].rearrange("p c d -> p (c d)"), bank(7)).then_inc(ffn_w_ready, 1)

            def scan(n0):
                dve.wait_ge(aexp_ready, 1)
                link(v.tensor_scalar(a_neg[:, :, :], a_neg[:, :, :], -1.0, None, ALU.mult))
                dve.wait_ge(scan_loaded, 16 * 6)
                for k in range(TAPS):
                    for c in range(C2):
                        ins = v.tensor_scalar(wxs[:, k, c, :], wxT[:, c, :], dwc[:, c, k:k + 1], None, ALU.mult)
                ins.then_inc(scan_vec_ready, 1)
                for c in range(C2):
                    v.tensor_scalar(diagD[:, c, :], ident[:, :], dcol[:, c:c + 1], None, ALU.mult)
                    link(v.memset(dA[:, c, :, 0:1], 0.0))
                v.tensor_copy(selb[0:96, :, :], self_[0:96]).then_inc(scan_vec_ready, 1)
                for b in range(NB):
                    norm(n0 + b, b)
                    dve.wait_ge(xd_act, 4 * b + 3)
                    v.tensor_tensor(r1[0:96, :], ps[0:96, 6, :], hib[0:96, :], ALU.subtract).then_inc(xd_vec, 1)
                    dve.wait_ge(xd_vec, 2 * b + 1)
                    dve.wait_ge(xd_act, 4 * b + 4)
                    v.tensor_tensor(r2[0:96, :], r1[0:96, :], mib[0:96, :], ALU.subtract).then_inc(xd_vec, 1)
                    for c in range(C2):
                        dve.wait_ge(sp_ready, 2 * b + c + 1)
                        v.scalar_tensor_tensor(dl[:, c, :], xb, 0.0, lb, ALU.max, ALU.add).then_inc(delta_ready, 1)
                        dve.wait_ge(delta_ready, 2 * b + c + 1)
                        dve.wait_ge(xc_ready, 2 * b + c + 1)
                        link(v.tensor_tensor(uu[:, c, :], dl[:, c, :], xc[:, c, :], ALU.mult))
                    for j in range(NS // 2):
                        js = slice(2 * j, 2 * j + 2)
                        dve.wait_ge(b_psum, 4 * b + j + 1)
                        for c in range(C2):
                            v.tensor_tensor(hs[:, c, js, :], uu[:, c, :].unsqueeze(1).to_broadcast([P, 2, L]),
                                            ps[:, 2:4, :], ALU.mult).then_inc(b_used, 1)
                        for c in range(C2):
                            dve.wait_ge(b_used, 8 * b + 2 * j + c + 1)
                            dve.wait_ge(dA_ready, 8 * b + 2 * j + c + 1)
                            h_ = hs[:, c, js, :].rearrange("p n l -> p (n l)")
                            link(v.tensor_tensor_scan(h_, dA[:, c, js, :].rearrange("p n l -> p (n l)"), h_, 0.0,
                                                      ALU.mult, ALU.add))
                        dve.wait_ge(c_psum, 4 * b + j + 1)
                        for c in range(C2):
                            v.tensor_tensor(hs[:, c, js, :], hs[:, c, js, :], ps[:, 4:6, :],
                                            ALU.mult).then_inc(hc_ready, 1)
                    dve.wait_ge(ysum_ready, b + 1)
                    dve.wait_ge(sz_ready, 2 * b + 2)
                    for c in range(C2):
                        v.tensor_tensor(yz[:, c, :], sz[:, c, :], bank(c), ALU.mult).then_inc(yz_ready, 1)
                    dve.wait_ge(o_psum, b + 1)
                    xg = x[:, TPB * b:TPB * (b + 1), :].rearrange("p k d -> p (k d)")
                    v.tensor_tensor(xg, xg, bank(6), ALU.add).then_inc(scan_used, 1)
                    dve.wait_ge(scan_used, b + 1)

            def ffn(u, n0):
                for g in range(NB):
                    norm(n0 + g, g)
                for b in range(NB):
                    n = u * NB + b
                    dve.wait_ge(ff_o_psum, n + 1)
                    xg = x[:, TPB * b:TPB * (b + 1), :].rearrange("p k d -> p (k d)")
                    v.scalar_tensor_tensor(xg, bank(2 + b % 2), 0.5, xg, ALU.mult, ALU.add).then_inc(ff_o_used, 1)
                dve.wait_ge(ff_o_used, NB * (u + 1))

            def attend(n0):
                dve.wait_ge(att_loaded, 16 * 5)
                v.tensor_copy(maskb[:, :, :], maskf).then_inc(att_const, 1)
                for b in range(NB):
                    norm(n0 + b, b)
                    for w in range(2):
                        dve.wait_ge(qkv_psum, 5 * b + 2 * w + 2)
                        v.scalar_tensor_tensor(t1, bank(2 * w), bqk[:, 2 * w:2 * w + 1], cs[:, 0, :],
                                               ALU.add, ALU.mult)
                        link(v.scalar_tensor_tensor(t2, bank(2 * w + 1), bqk[:, 2 * w + 1:2 * w + 2], cs[:, 1, :],
                                                    ALU.add, ALU.mult))
                        if w == 0:
                            if b >= 1:
                                dve.wait_ge(parts_stored, 16 * b)
                            link(v.tensor_tensor(qk[:, 0, :], t1, t2, ALU.add))
                        else:
                            v.tensor_tensor(qk[:, 1, :], t1, t2, ALU.add).then_inc(rope_ready, 1)
                    dve.wait_ge(part_act, 2 * b + 1)
                    v.tensor_tensor(q1, qk, spl[:, 0, :, :], ALU.subtract).then_inc(part_vec, 1)
                    dve.wait_ge(part_act, 2 * b + 2)
                    v.tensor_tensor(spl[:, 2, :, :], q1, spl[:, 1, :, :], ALU.subtract).then_inc(part_vec, 1)
                    dve.wait_ge(qkv_psum, 5 * b + 5)
                    if b == 0:
                        dve.wait_ge(att_const, 2)
                    v.tensor_copy(va[:, :, :, 0:HD],
                                  bank(4).rearrange("p (k h e) -> p k h e", k=TPB, h=NH)).then_inc(v_ready, 1)
                    for j, (qt, h0, nh, pb) in enumerate(MAXSTEPS):
                        dve.wait_ge(max_psum, b * NMS + j + 1)
                        w_ = P * (qt + 1)
                        k_ = 2 * (j % 3)
                        if pb == 1:
                            src = ps[:, k_:k_ + 2, 0:w_]
                        else:
                            src = ps[:, k_:k_ + 2, :].rearrange("p k (h f) -> p (k h) f", f=w_)
                        v.tensor_reduce(nm[:, qt, h0:h0 + nh], src, AX.X, ALU.max, negate=True).then_inc(max_used, 1)
                    for g in range(NG):
                        n = b * NG + g
                        dve.wait_ge(o_turned, n + 1)
                        o4 = bank(7).rearrange("p (k j e) -> p k j e", k=TPB, j=GH)
                        link(v.reciprocal(rden, o4[:, :, :, HD]))
                        for k in range(TPB):
                            ins = v.tensor_tensor(
                                on[:, k, 32 * g:32 * g + 32].rearrange("p (j e) -> p j e", j=GH), o4[:, k, :, 0:HD],
                                rden[:, k, :].unsqueeze(2).to_broadcast([P, GH, HD]), ALU.mult)
                        ins.then_inc(on_ready, 1)
                    dve.wait_ge(ao_psum, b + 1)
                    xg = x[:, TPB * b:TPB * (b + 1), :].rearrange("p k d -> p (k d)")
                    v.tensor_tensor(xg, xg, bank(0), ALU.add).then_inc(ao_used, 1)
                    dve.wait_ge(ao_used, b + 1)

            dve.wait_ge(const_loaded, 48)
            dve.wait_ge(x_loaded, 16)
            v.tensor_copy(ident_b[:, :], ident[:, :]).then_inc(y_used, 1)
            moe(0, 0)
            fly()
            if STAGES > 1:
                scan(NB)
            if STAGES > 2:
                moe(1, 2 * NB)
            if STAGES > 3:
                ffn(0, 3 * NB)
            if STAGES > 4:
                attend(4 * NB)
            if STAGES > 5:
                ffn(1, 5 * NB)
            for b in range(NB):
                v.memset(ve2[:, b:b + 1], 0.0).then_inc(x_done, 1)


def kernel(**inputs):
    import numpy as np
    import concourse.bacc as bacc
    from concourse.bass_utils import run_bass_kernel_spmd

    g = {k: np.asarray(v) for k, v in inputs.items()}
    f32 = np.float32

    def cols(v, n):
        return v.reshape(n, 128).T

    L, E, D = 512, 8, 128
    sw = np.arange(D) ^ 1
    half = 4
    inv = (f32(1.0) / np.power(f32(10000.0), np.arange(half, dtype=f32) / f32(half))).astype(f32)
    ang = np.arange(L, dtype=f32)[:, None] * inv[None, :]
    pair = (np.arange(D) % 8) // 2
    cos = np.cos(ang).astype(f32)[:, pair].T
    sin = np.sin(ang).astype(f32)[:, pair].T * np.where(np.arange(D) % 2 == 0, -1.0, 1.0).astype(f32)[:, None]
    i, j = np.arange(128)[:, None], np.arange(128)[None, :]
    big = f32(-1.0e30)
    mask = np.stack([np.where(j > i, big, f32(0)), np.where(i > j, big, f32(0))], 1).astype(f32)
    sel = np.zeros((96, 16, 128), f32)
    for r in range(96):
        if 8 <= r % 32 < 24:
            sel[r, r % 32 - 8, :] = 1.0
    wx = g["L0_attn_W_x"].reshape(2, 128, 24).transpose(1, 0, 2)
    wx3 = np.zeros((128, 2, 96), f32)
    for r in range(3):
        wx3[:, :, 32 * r:32 * r + 24] = wx
    W_in = g["L0_attn_W_in"]
    Wq, Wk = g["L1_attn_Wq"], g["L1_attn_Wk"]
    bq, bk = g["L1_attn_bq"], g["L1_attn_bk"]
    arrays = {
        "x": g["L0_attn_x"].reshape(-1, D),
        "ident": np.eye(128, dtype=f32),
        "rank8": np.broadcast_to(np.arange(E, 0, -1, dtype=f32), (128, E)),
        "w_router": g["L0_ffn_W_router"].T,
        "w_gate": g["L0_ffn_W_gate"].transpose(2, 0, 1),
        "w_up": g["L0_ffn_W_up"].transpose(2, 0, 1),
        "w_down": g["L0_ffn_W_down"].reshape(E, D, 4, 128).transpose(3, 0, 2, 1),
        "up_w": g["L1_ffn_up_weights"].reshape(9, -1),
        "down_w": g["L1_ffn_down_weights"].reshape(9, -1),
        "up_bias": cols(g["L1_ffn_up_bias"], 4),
        "b_con": g["L1_ffn_b_con"][None], "down_bias": g["L1_ffn_down_bias"][None],
        "w_exp": g["L1_ffn_W_exp"], "b_exp": g["L1_ffn_b_exp"][None], "w_conT": g["L1_ffn_W_con"].T,
        "conv_bias": cols(g["L0_attn_conv_bias"], 2), "b_dt": cols(g["L0_attn_b_dt"], 2),
        "dskip": cols(g["L0_attn_D"], 2),
        "dw": g["L0_attn_dw_kernel"].T.reshape(2, 128, 4).transpose(1, 0, 2),
        "w_dt": g["L0_attn_W_dt"],
        "a_log": g["L0_attn_A_log"].reshape(2, 128, 8).transpose(1, 0, 2),
        "pw": g["L0_attn_pw_kernel"].reshape(2, 128, 256).transpose(1, 0, 2),
        "wxT": W_in[:, :256].T.reshape(2, 128, 128).transpose(1, 0, 2),
        "wz": W_in[:, 256:],
        "w_out": g["L0_attn_W_out"].reshape(2, 128, 128).transpose(1, 0, 2),
        "w_x3": wx3, "sel": sel,
        "wq": np.stack([Wq.T, Wq.T[:, sw], Wk.T, Wk.T[:, sw]], 1),
        "bqk": np.stack([bq, bq[sw], bk, bk[sw]], 1),
        "wv": g["L1_attn_Wv"].T, "wo": g["L1_attn_Wo"].T,
        "bv": g["L1_attn_bv"][None], "bo": g["L1_attn_bo"][None],
        "cossin": np.stack([cos, sin], 1), "mask": mask,
    }
    nc = bacc.Bacc("TRN2", target_bir_lowering=False, num_devices=1)
    maps, aps = {}, {}
    for name, a in arrays.items():
        a = np.ascontiguousarray(a, dtype=f32)
        maps["in_" + name] = a
        aps[name] = nc.dram_tensor("in_" + name, a.shape, F32, kind="ExternalInput").ap()
    import ml_dtypes
    a = np.ones((1, 16, 512), ml_dtypes.bfloat16)
    maps["in_ones_row"] = a
    aps["ones_row"] = nc.dram_tensor("in_ones_row", a.shape, BF16, kind="ExternalInput").ap()
    out = nc.dram_tensor("out_dram", (2048, D), F32, kind="ExternalOutput").ap()
    macaron_kernel(nc, aps, out)
    r = run_bass_kernel_spmd(nc, [maps], core_ids=[0])
    return r.results[0]["out_dram"].reshape(4, 512, 128)
```

```python
from contextlib import ExitStack

import concourse.bass as bass
from concourse import mybir

STAGES = 6

P = 128
ALU = mybir.AluOpType
ACT = mybir.ActivationFunctionType
AX = mybir.AxisListType
F32 = mybir.dt.float32
BF16 = mybir.dt.bfloat16
I32 = mybir.dt.int32


def macaron_kernel(nc, t, out):
    TOK, D = t["x"].shape
    NT = TOK // P
    NB = 4
    TPB = NT // NB
    L = TPB * P
    E = t["w_router"].shape[1]
    F = t["w_gate"].shape[2]
    FC = F // P
    DI = t["pw"].shape[2]
    C2 = DI // P
    NS = t["a_log"].shape[2]
    TAPS = t["dw"].shape[2]
    R = t["w_dt"].shape[0]
    HID = t["w_exp"].shape[1]
    HC = HID // P
    STG = t["up_w"].shape[0]
    NH = 16
    HD = D // NH
    GH = 4
    NG = NH // GH
    SEG = [0, 512, 1024, 896]
    PTW = 1280
    EPS = 1e-5
    CT = NT + 1
    NST = 2 * NT + E - 1
    LD0, LD1 = NST // 2 + 2, NST // 2 + 1
    ST0, ST1 = NST // 2 + 1, NST // 2
    SPARE = E * CT
    KR = 72
    assert D == P and L == 512 and TAPS == 4 and NS == 8 and R == 8

    with ExitStack() as ctx:
        def sb(name, shape, dt=F32):
            return ctx.enter_context(nc.sbuf_tensor(name, shape, dt))

        def sem(name):
            return ctx.enter_context(nc.semaphore(name))

        ps = ctx.enter_context(nc.psum_tensor("ps", [P, 8, 512], F32))

        def bank(k):
            return ps[:, k, :]

        x = sb("x", [P, NT, D])
        xn = sb("xn", [P, NB, TPB, D])
        xnT = sb("xnT", [P, TOK])
        st = sb("st", [P, 2, TPB, 6])
        mv = sb("mv", [P, 2, TPB, 2])
        rs = sb("rs", [P, 2, TPB])
        ve = sb("ve", [P, TPB])
        mhalf = sb("mhalf", [P, TPB])
        ident = sb("ident", [P, P])
        ident_b = sb("ident_b", [P, P], BF16)
        ones = sb("ones", [P, P])
        wr = sb("wr", [P, E])
        wg = sb("wg", [P, E, F])
        wu = sb("wu", [P, E, F])
        wd = sb("wd", [P, E, FC, D])
        r8 = sb("r8", [P, E])
        base8 = sb("base8", [P, E])
        lane = sb("lane", [P, E])
        first4 = sb("first4", [P, E, TPB])
        steps = sb("steps", [P, E, CT - 1])
        tnum = sb("tnum", [1, NST + 3, E])
        before = sb("before", [P, P])
        before_b = sb("before_b", [P, P], BF16)
        ones_b = sb("ones_b", [P, P], BF16)
        lg = sb("lg", [P, TPB, E])
        oh = sb("oh", [P, 2, TPB, E])
        sl = sb("sl", [P, TPB, E])
        ohb = sb("ohb", [P, TPB, E], BF16)
        red = sb("red", [P, 4, TPB])
        cs4 = sb("cs4", [P, E, TPB])
        pre4 = sb("pre4", [P, E, TPB])
        cum = sb("cum", [P, E])
        slots = sb("slots", [P, 2, NT], I32)
        pads = sb("pads", [P, E], I32)
        dm = sb("dm", [P, NT])
        egate = sb("egate", [P, NT])
        gates = sb("gates", [P, 2, NT])
        gsum = sb("gsum", [P, NT])
        cnt = sb("cnt", [P, 4, E])
        cmp = sb("cmp", [P, E, CT - 1])
        shift = sb("shift", [P, E])
        slotf = sb("slotf", [P, 2 * NT])
        rfix = sb("rfix", [P, 2 * NT])
        dense = sb("dense", [P, 2 * NT], I32)
        trow = sb("trow", [1, 3, NST + 3])
        tabs = sb("tabs", [1, 2, NST + 3], I32)
        zrow = sb("zrow", [P, D])
        ve2 = sb("ve2", [P, NB + 1])
        ARENA = 28 * 1024
        ar = sb("ar", [P, ARENA])

        class Arena:
            def __init__(self):
                self.at = 0

            def take(self, count, pattern=None, **k):
                a = ar[:, self.at:self.at + count]
                self.at += count
                assert self.at <= ARENA, self.at
                return a.rearrange(pattern, **k) if pattern else a

        m = Arena()
        sil = m.take(2 * F, "p (b f) -> p b f", b=2)
        hh = m.take(2 * F, "p (b f) -> p b f", b=2)
        hT = m.take(2 * F, "p (b f) -> p b f", b=2)
        xg = m.take(2 * D, "p (b f) -> p b f", b=2)
        xt = m.take(2 * P, "p (b f) -> p b f", b=2)
        yt = m.take(2 * D, "p (b f) -> p b f", b=2)
        rmsk = m.take(2 * NT * E, "p (s e) -> p s e", e=E)
        tmsk = m.take(2 * (NST + 3) * E, "p (m j e) -> p m j e", m=2, e=E)[0:1]
        yg = m.take(2 * 2 * TPB * D, "p (b k i d) -> p b k i d", b=2, k=2, i=TPB)
        bw = m.take(2 * 2 * HID, "p (b f) -> p b f", b=2)
        va_ = m.take(2 * HID, "p (b f) -> p b f", b=2)
        vb_ = m.take(2 * HID, "p (b f) -> p b f", b=2)
        vt_ = m.take(HID)
        wup = sb("wup", [P, HID])
        wdn = sb("wdn", [P, HC, D])
        bup = sb("bup", [P, HC])
        ubias = sb("ubias", [P, HC])
        ffbr = sb("ffbr", [1, 3, D])
        a_neg = sb("a_neg", [P, C2, NS])
        s = Arena()
        pwt = s.take(C2 * DI, "p (c o) -> p c o", c=C2)
        wxT = s.take(C2 * P, "p (c d) -> p c d", c=C2)
        cw = s.take(TAPS * DI, "p (k o) -> p k o", k=TAPS)
        wz = s.take(DI)
        diagD = s.take(C2 * P, "p (c d) -> p c d", c=C2)
        wout = s.take(C2 * D, "p (c d) -> p c d", c=C2)
        wx3 = s.take(C2 * 96, "p (c r) -> p c r", c=C2)
        dA = s.take(C2 * NS * L, "p (c n l) -> p c n l", c=C2, n=NS)
        hs = s.take(C2 * NS * L, "p (c n l) -> p c n l", c=C2, n=NS)
        xc = s.take(C2 * L, "p (c l) -> p c l", c=C2)
        sz = s.take(C2 * L, "p (c l) -> p c l", c=C2)
        xb = s.take(L)
        eb = s.take(L)
        lb = s.take(L)
        dl = s.take(C2 * L, "p (c l) -> p c l", c=C2)
        uu = s.take(C2 * L, "p (c l) -> p c l", c=C2)
        yz = s.take(C2 * L, "p (c l) -> p c l", c=C2)
        xdf = s.take(L)
        r1 = s.take(L)
        r2 = s.take(L)
        hib = s.take(L // 2).bitcast(BF16)
        mib = s.take(L // 2).bitcast(BF16)
        xsb = s.take(L // 2).bitcast(BF16)
        selb = sb("selb", [P, 2 * NS, P], BF16)
        wxs = hs.rearrange("p c n l -> p (c n l)")[:, 4096:4096 + TAPS * C2 * P].rearrange(
            "p (k c d) -> p k c d", k=TAPS, c=C2)
        self_ = hs.rearrange("p c n l -> p (c n l)")[:, 0:2 * NS * P].rearrange("p (j m) -> p j m", j=2 * NS)
        cbias = sb("cbias", [P, C2])
        bdt = sb("bdt", [P, C2])
        dcol = sb("dcol", [P, C2])
        dwc = sb("dwc", [P, C2, TAPS])
        wdt = sb("wdt", [R, DI])
        f = Arena()
        gT = f.take(2 * HC * L, "p (b c l) -> p b c l", b=2, c=HC)
        a = Arena()
        wq = a.take(4 * D, "p (w d) -> p w d", w=4)
        wv = a.take(D)
        wo = a.take(D)
        cs = a.take(2 * L, "p (w l) -> p w l", w=2)
        t1 = a.take(L)
        t2 = a.take(L)
        qk = a.take(2 * L, "p (w l) -> p w l", w=2)
        q1 = a.take(2 * L, "p (w l) -> p w l", w=2)
        spl = a.take(3 * L, "p f -> p f").bitcast(BF16).rearrange("p (j w l) -> p j w l", j=3, w=2)
        qs = a.take(NH * L // 2).bitcast(BF16).rearrange("p (h l) -> p h l", h=NH)
        ks = a.take(NH * L // 2).bitcast(BF16).rearrange("p (h l) -> p h l", h=NH)
        va = a.take(TPB * NH * 32, "p (k h e) -> p k h e", k=TPB, h=NH)
        pt = a.take(GH * PTW, "p (h f) -> p h f", h=GH)
        ob = a.take(L)
        on = a.take(TPB * D, "p (k e) -> p k e", k=TPB)
        onT = a.take(L)
        nm = a.take(TPB * NH // 2).bitcast(BF16).rearrange("p (k h) -> p k h", k=TPB)
        mTs = a.take(L // 2).bitcast(BF16)
        rden = a.take(TPB * GH, "p (k j) -> p k j", k=TPB)
        maskf = a.take(2 * P, "p (w d) -> p w d", w=2)
        maskb = sb("maskb", [P, 2, P], BF16)
        bqk = sb("bqk", [P, 4])
        abr = sb("abr", [1, 2, D])

        qk_dram = nc.dram_tensor("qk_parts", [NB, 3, 2, P, L], BF16, kind="Internal").ap()

        xs_dram = nc.dram_tensor("slot_rows", [(SPARE + 1) * P, D], F32, kind="Internal").ap()
        ys_dram = nc.dram_tensor("slot_results", [NST * P, D], F32, kind="Internal").ap()
        m_dram = nc.dram_tensor("row_maxima", [NB, NH, L], BF16, kind="Internal").ap()

        x_loaded = sem("x_loaded")
        const_loaded = sem("const_loaded")
        moe_loaded = sem("moe_loaded")
        small_loaded = sem("small_loaded")
        pool_chain = sem("pool_chain")
        vec_chain = sem("vec_chain")
        act_chain = sem("act_chain")
        ident_ready = sem("ident_ready")
        ln_stats_ready = sem("ln_stats_ready")
        ln_rstd_ready = sem("ln_rstd_ready")
        xn_ready = sem("xn_ready")
        xn_turned = sem("xn_turned")
        xnT_ready = sem("xnT_ready")
        logits_ready = sem("logits_ready")
        ohb_ready = sem("ohb_ready")
        ranks_psum = sem("ranks_psum")
        slots_ready = sem("slots_ready")
        pads_ready = sem("pads_ready")
        tables_ready = sem("tables_ready")
        egate_ready = sem("egate_ready")
        spare_zeroed = sem("spare_zeroed")
        rows_stored = sem("rows_stored")
        xg_loaded = [sem("xg_loaded_even"), sem("xg_loaded_odd")]
        xg_turned = sem("xg_turned")
        xt_ready = sem("xt_ready")
        y_ready = sem("y_ready")
        y_stored = [sem("y_stored_even"), sem("y_stored_odd")]
        yg_loaded = [sem("yg_loaded_even"), sem("yg_loaded_odd")]
        combined = sem("combined")
        gate_ready = sem("gate_ready")
        up_ready = sem("up_ready")
        sil_ready = sem("sil_ready")
        h_ready = sem("h_ready")
        h_turned = sem("h_turned")
        hT_ready = sem("hT_ready")
        down_done = sem("down_done")
        bw_loaded = [sem("bw_loaded_even"), sem("bw_loaded_odd")]
        wcon_loaded = sem("wcon_loaded")
        fly_ready = sem("fly_ready")
        fly_turned = sem("fly_turned")
        ffn_w_ready = sem("ffn_w_ready")
        scan_loaded = sem("scan_loaded")
        scan_vec_ready = sem("scan_vec_ready")
        cw_psum = sem("cw_psum")
        cw_ready = sem("cw_ready")
        aexp_ready = sem("aexp_ready")
        xc_psum = sem("xc_psum")
        z_psum = sem("z_psum")
        xc_ready = sem("xc_ready")
        sz_ready = sem("sz_ready")
        xd_psum = sem("xd_psum")
        xd_act = sem("xd_act")
        xd_vec = sem("xd_vec")
        xs_ready = sem("xs_ready")
        dt_psum = sem("dt_psum")
        sp_ready = sem("sp_ready")
        delta_ready = sem("delta_ready")
        u_ready = sem("u_ready")
        dA_ready = sem("dA_ready")
        b_psum = sem("b_psum")
        b_used = sem("b_used")
        c_psum = sem("c_psum")
        hc_ready = sem("hc_ready")
        ysum_ready = sem("ysum_ready")
        yz_ready = sem("yz_ready")
        o_psum = sem("o_psum")
        scan_used = sem("scan_used")
        ff_h_psum = sem("ff_h_psum")
        ff_g_ready = sem("ff_g_ready")
        ff_o_psum = sem("ff_o_psum")
        ff_o_used = sem("ff_o_used")
        att_loaded = sem("att_loaded")
        att_const = sem("att_const")
        qkv_psum = sem("qkv_psum")
        rope_ready = sem("rope_ready")
        part_act = sem("part_act")
        part_vec = sem("part_vec")
        parts_stored = sem("parts_stored")
        qk_loaded = sem("qk_loaded")
        v_ready = sem("v_ready")
        max_psum = sem("max_psum")
        max_used = sem("max_used")
        m_turned = sem("m_turned")
        m_copied = sem("m_copied")
        m_stored = sem("m_stored")
        m_loaded = sem("m_loaded")
        s_psum = sem("s_psum")
        p_ready = sem("p_ready")
        pv_psum = sem("pv_psum")
        o_copied = sem("o_copied")
        o_turned = sem("o_turned")
        on_ready = sem("on_ready")
        on_turned = sem("on_turned")
        onT_ready = sem("onT_ready")
        ao_psum = sem("ao_psum")
        ao_used = sem("ao_used")
        x_done = sem("x_done")
        out_stored = sem("out_stored")

        x_tiles = t["x"].rearrange("(i p) d -> p i d", p=P)
        out_tiles = out.rearrange("(i p) d -> p i d", p=P)
        NMAX = [(3, 2, 1), (2, 2, 1), (1, 4, 2), (0, 8, 4)]
        MAXSTEPS = [(qt, h0, nh, pb) for qt, nh, pb in NMAX for h0 in range(0, NH, nh)]
        NMS = len(MAXSTEPS)

        block = ctx.enter_context(nc.Block())

        @block.sync
        def _(sp):
            sp.dma_start(x[:, :, :], x_tiles).then_inc(x_loaded, 16)
            for dst, src in ((ident[:, :], t["ident"]), (wr[:, :], t["w_router"]), (r8[:, :], t["rank8"]),
                             (base8[:, :], t["base8"]), (lane[:, :], t["lane"]), (first4[:, :, :], t["first4"]),
                             (steps[:, :, :], t["steps"]), (tnum[:, :, :], t["tnum"]), (before[:, :], t["before"])):
                sp.dma_start(dst, src).then_inc(const_loaded, 16)
            sp.dma_start(wg[:, :, :], t["w_gate"]).then_inc(moe_loaded, 16)
            sp.dma_start(wu[:, :, :], t["w_up"]).then_inc(moe_loaded, 16)
            sp.dma_start(wd[:, :, :, :], t["w_down"]).then_inc(moe_loaded, 16)
            small = [(ubias[:, :], t["up_bias"]), (ffbr[:, 0, :], t["b_con"]), (ffbr[:, 1, :], t["down_bias"]),
                     (cbias[:, :], t["conv_bias"]), (bdt[:, :], t["b_dt"]), (dcol[:, :], t["dskip"]),
                     (dwc[:, :, :], t["dw"]), (wdt[:, :], t["w_dt"]), (a_neg[:, :, :], t["a_log"]),
                     (bqk[:, :], t["bqk"]), (abr[:, 0, :], t["bv"]), (abr[:, 1, :], t["bo"]),
                     (va_[:, 0, :], t["w_exp"]), (va_[0:1, 1, :], t["b_exp"])]

            for dst, src in small:
                sp.dma_start(dst, src).then_inc(small_loaded, 16)
            def moe(u):
                def load(j, q):
                    r = sp.value_load(tabs[0:1, 1, bass.ds(j, 1)], min_val=0, max_val=SPARE)
                    sp.dma_start(xg[:, q, :], xs_dram[bass.ds(r * P, P), :]).then_inc(xg_loaded[q], 16)

                def store(j, q):
                    sp.dma_start(ys_dram[bass.ds(j * P, P), :], yt[:, q, :]).then_inc(y_stored[q], 16)

                t0, n0 = u * (NST + 1), u * NST
                sp.wait_ge(tables_ready, u + 1)
                sp.wait_ge(rows_stored, 16 * (2 * NT + E) * (u + 1))
                sp.wait_ge(spare_zeroed, 16)
                load(0, 0)
                load(1, 1)
                sp.wait_ge(xg_turned, t0 + 1)
                load(2, 0)
                with sp.Fori(1, NST, 2) as i:
                    for j, q in ((i, 1), (i + 1, 0)):
                        sp.wait_ge(xg_turned, j + (t0 + 1))
                        load(j + 2, q)
                        sp.wait_ge(y_ready, j + (n0 + 1))
                        store(j - 1, 1 - q)
                sp.wait_ge(y_ready, n0 + NST + 1)
                store(NST - 1, 0)
                sp.wait_ge(xg_loaded[0], 16 * LD0 * (u + 1))

            sp.sem_inc(y_stored[0], 16)
            sp.sem_inc(y_stored[1], 16)
            moe(0)
            if STAGES > 1:
                sp.wait_ge(combined, NB)
                sp.wait_ge(fly_turned, 1)
                for dst, src in ((pwt, t["pw"]), (wxT, t["wxT"]), (wz, t["wz"]), (wout, t["w_out"]),
                                 (wx3, t["w_x3"]), (self_[0:96], t["sel"])):
                    sp.dma_start(dst, src).then_inc(scan_loaded, 16)
            if STAGES > 2:
                moe(1)
            if STAGES > 4:
                sp.wait_ge(ff_o_used, NB)
                for dst, src in ((wq, t["wq"]), (wv, t["wv"]), (wo, t["wo"]), (cs, t["cossin"]),
                                 (maskf, t["mask"])):
                    sp.dma_start(dst, src).then_inc(att_loaded, 16)
                sp.wait_ge(att_const, 2)
                sp.dma_start(ks[48:49, :, :], t["ones_row"]).then_inc(att_loaded, 16)
                for b in range(NB):
                    sp.wait_ge(part_vec, 2 * b + 2)
                    sp.wait_ge(part_act, 2 * b + 2)
                    sp.dma_start(qk_dram[b].rearrange("j w p l -> p j w l"), spl).then_inc(parts_stored, 16)
                    sp.wait_ge(parts_stored, 16 * (b + 1))
                    if b >= 1:
                        sp.wait_ge(pv_psum, NG * b)
                    for r, (i, j) in enumerate(((0, 0), (0, 1), (1, 0), (1, 1), (0, 2), (2, 0))):
                        sp.dma_start(qs[8 * r:8 * r + 8, :, :],
                                     qk_dram[b, i, 0].rearrange("(h d) l -> d h l", d=HD)).then_inc(qk_loaded, 16)
                        sp.dma_start(ks[8 * r:8 * r + 8, :, :],
                                     qk_dram[b, j, 1].rearrange("(h d) l -> d h l", d=HD)).then_inc(qk_loaded, 16)
                    sp.wait_ge(m_copied, b + 1)
                    sp.dma_start(m_dram[b], mTs[0:NH, :]).then_inc(m_stored, 16)
                    sp.wait_ge(m_stored, 16 * (b + 1))
                    sp.dma_start(qs[48:49, :, :], m_dram[b].unsqueeze(0)).then_inc(m_loaded, 16)
            for b in range(NB):
                sp.wait_ge(x_done, b + 1)
                sp.dma_start(out_tiles[:, TPB * b:TPB * (b + 1), :],
                             x[:, TPB * b:TPB * (b + 1), :]).then_inc(out_stored, 16)
            sp.wait_ge(out_stored, 16 * NB)

        @block.gpsimd
        def _(pool):
            chain = [0]

            def link(ins):
                chain[0] += 1
                ins.then_inc(pool_chain, 1)
                pool.wait_ge(pool_chain, chain[0])

            def ln_rstd(n):
                pool.wait_ge(ln_stats_ready, n + 1)
                link(nc.gpsimd.tensor_scalar(ve[:, :], mv[:, n % 2, :, 1], EPS, None, ALU.add))
                nc.gpsimd.tensor_tensor(rs[:, n % 2, :], ve[:, :], mhalf[:, :], ALU.pow).then_inc(ln_rstd_ready, 1)

            def scatter(u, g):
                pool.wait_ge(slots_ready, NB * u + g + 1)
                for k in range(2):
                    for i in range(TPB):
                        nc.gpsimd.indirect_dma_start(
                            xs_dram[:, :], bass.IndirectOffsetOnAxis(ap=slots[:, k, TPB * g + i:TPB * g + i + 1], axis=0),
                            xn[:, g, i, :], None).then_inc(rows_stored, 16)

            def pad(u):
                pool.wait_ge(pads_ready, u + 1)
                for e in range(E):
                    nc.gpsimd.indirect_dma_start(
                        xs_dram[:, :], bass.IndirectOffsetOnAxis(ap=pads[:, e:e + 1], axis=0),
                        zrow[:, :], None).then_inc(rows_stored, 16)

            def gather(u):
                pool.wait_ge(y_stored[0], 16 * (ST0 * (u + 1) + 1))
                pool.wait_ge(y_stored[1], 16 * (ST1 * (u + 1) + 1))
                for g in range(NB):
                    if NB * u + g >= 2:
                        pool.wait_ge(combined, NB * u + g - 1)
                    for k in range(2):
                        for i in range(TPB):
                            nc.gpsimd.indirect_dma_start(
                                yg[:, g % 2, k, i, :], None, ys_dram[:, :],
                                bass.IndirectOffsetOnAxis(ap=dense[:, NT * k + TPB * g + i:NT * k + TPB * g + i + 1],
                                                          axis=0),
                            ).then_inc(yg_loaded[g % 2], 16)

            def stage(k, strd, parts, src, dst, up):
                nb = HID // (2 * strd)
                pool.wait_ge(bw_loaded[k % 2], 16 * (k // 2 + 1))
                w = bw[:, k % 2, :].rearrange("p (n s o i) -> p n s o i", n=nb, s=strd, o=2)
                for q in range(parts):
                    np_ = P if q == 0 else 1
                    a_ = src[0:np_, q, :].rearrange("p (n o s) -> p n o s", n=nb, o=2)
                    d_ = dst[0:np_, q, :].rearrange("p (n o s) -> p n o s", n=nb, o=2)
                    t_ = vt_[0:np_, :].rearrange("p (n o s) -> p n o s", n=nb, o=2)
                    for o in range(2):
                        w0 = w[0:np_, :, :, o, 0] if up else w[0:np_, :, :, 0, o]
                        w1 = w[0:np_, :, :, o, 1] if up else w[0:np_, :, :, 1, o]
                        nc.gpsimd.tensor_tensor(d_[:, :, o, :], a_[:, :, 0, :], w0, ALU.mult)
                        link(nc.gpsimd.tensor_tensor(t_[:, :, o, :], a_[:, :, 1, :], w1, ALU.mult))
                        link(nc.gpsimd.tensor_tensor(d_[:, :, o, :], d_[:, :, o, :], t_[:, :, o, :], ALU.add))

            def load_stage(k):
                src = t["up_w"][k] if k < STG else t["down_w"][2 * STG - 1 - k]
                pool.dma_start(bw[:, k % 2, :], src.partition_broadcast(P)).then_inc(bw_loaded[k % 2], 16)

            def fly(k0, parts, up):
                load_stage(k0)
                load_stage(k0 + 1)
                src, dst = va_, vb_
                for k in range(k0, k0 + STG):
                    stage(k, 2 ** k if up else 2 ** (2 * STG - 1 - k), parts, src, dst, up)
                    if k + 2 < k0 + STG:
                        load_stage(k + 2)
                    src, dst = dst, src

            nc.gpsimd.memset(ones[:, :], 1.0)
            nc.gpsimd.memset(vb_[:, :, :], 0.0)
            nc.gpsimd.memset(zrow[:, :], 0.0)
            link(nc.gpsimd.memset(mhalf[:, :], -0.5))
            pool.dma_start(xs_dram[SPARE * P:(SPARE + 1) * P, :], zrow[:, :]).then_inc(spare_zeroed, 16)
            for g in range(NB):
                ln_rstd(g)
                scatter(0, g)
            pad(0)
            pool.wait_ge(small_loaded, 16 * 14)
            fly(0, 2, True)
            nc.gpsimd.tensor_copy(wup[:, :], vb_[:, 0, :]).then_inc(fly_ready, 1)
            gather(0)
            for n in range(NB, NB * min(STAGES, 2)):
                ln_rstd(n)
            if STAGES > 2:
                for g in range(NB):
                    ln_rstd(2 * NB + g)
                    scatter(1, g)
                pad(1)
                pool.dma_start(va_[:, 0, :], t["w_conT"]).then_inc(wcon_loaded, 16)
                pool.wait_ge(wcon_loaded, 16)
                fly(STG, 1, False)
                pool.sem_inc(fly_ready, 1)
                gather(1)
            for n in range(3 * NB, NB * STAGES):
                if n == 4 * NB:
                    pool.wait_ge(ff_o_used, NB)
                    nc.gpsimd.memset(qs[0:KR, :, :], 0.0)
                    nc.gpsimd.memset(va[:, :, :, :], 1.0)
                    nc.gpsimd.memset(ks[0:KR, :, :], 0.0).then_inc(att_const, 1)
                ln_rstd(n)

        @block.tensor
        def _(pe):
            def mm(o, l, r, first=True, last=True):
                return nc.tensor.matmul(o, l, r, start=first, stop=last)

            def turn(n):
                pe.wait_ge(xn_ready, n + 1)
                if n >= 1:
                    pe.wait_ge(xnT_ready, n)
                for k in range(TPB):
                    ins = nc.tensor.transpose(ps[:, 7, k * P:(k + 1) * P], xn[:, n % NB, k, :], ident[:, :])
                ins.then_inc(xn_turned, 1)

            def pre(u, g, n0):
                if NB * u + g >= 1:
                    pe.wait_ge(slots_ready, NB * u + g)
                turn(n0 + g)
                pe.wait_ge(xnT_ready, n0 + g + 1)
                for i in range(TPB):
                    ins = mm(ps[:, 7, E * i:E * i + E], xnT[:, (TPB * g + i) * P:(TPB * g + i + 1) * P], wr[:, :])
                ins.then_inc(logits_ready, 1)
                pe.wait_ge(ohb_ready, NB * u + g + 1)
                o2 = ohb[:, :, :].rearrange("p i e -> p (i e)")
                mm(ps[:, 7, 32:32 + TPB * E], before_b[:, :], o2)
                mm(ps[:, 7, 64:64 + TPB * E], ones_b[:, :], o2).then_inc(ranks_psum, 1)

            def moe(u, n0):
                t0, n1 = u * (NST + 1), u * NST

                def expert(j):
                    return pe.value_load(tabs[0:1, 0, bass.ds(j, 1)], min_val=0, max_val=E - 1)

                def turn_x(q):
                    nc.tensor.transpose(ps[:, 6, 0:P], xg[:, q, :], ident[:, :]).then_inc(xg_turned, 1)

                def gate_up(j, q):
                    pe.wait_ge(xt_ready, j + (t0 + 1))
                    e = expert(j)
                    mm(bank(q), xt[:, q, :], wg[:, bass.ds(e, 1), :].rearrange("p o f -> p (o f)")
                       ).then_inc(gate_ready, 1)
                    mm(bank(2 + q), xt[:, q, :], wu[:, bass.ds(e, 1), :].rearrange("p o f -> p (o f)")
                       ).then_inc(up_ready, 1)

                def turn_h(j, q):
                    pe.wait_ge(h_ready, j + (n1 + 1))
                    for f_ in range(FC):
                        ins = nc.tensor.transpose(ps[:, 4, f_ * P:(f_ + 1) * P],
                                                  hh[:, q, f_ * P:(f_ + 1) * P], ident[:, :])
                    ins.then_inc(h_turned, 1)

                def down(j, q):
                    e = expert(j)
                    pe.wait_ge(hT_ready, j + (n1 + 1))
                    pe.wait_ge(y_ready, j + (n1 + 1))
                    for f_ in range(FC):
                        ins = mm(ps[:, 5, 0:D], hT[:, q, f_ * P:(f_ + 1) * P],
                                 wd[:, bass.ds(e, 1), f_, :].rearrange("p o d -> p (o d)"), f_ == 0, f_ == FC - 1)
                    ins.then_inc(down_done, 1)

                pe.wait_ge(moe_loaded, 48)
                pe.wait_ge(xg_loaded[0], 16 * (LD0 * u + 1))
                turn_x(0)
                gate_up(0, 0)
                pe.wait_ge(xg_loaded[1], 16 * (LD1 * u + 1))
                turn_x(1)
                turn_h(0, 0)
                with pe.Fori(1, NST, 2) as i:
                    for j, q in ((i, 1), (i + 1, 0)):
                        gate_up(j, q)
                        if q == 1:
                            pe.wait_ge(xg_loaded[0], i * 8 + (8 + 16 * (LD0 * u + 1)))
                        else:
                            pe.wait_ge(xg_loaded[1], i * 8 + (8 + 16 * (LD1 * u + 1)))
                        turn_x(1 - q)
                        down(j - 1, 1 - q)
                        turn_h(j, q)
                down(NST - 1, 0)

            def fly_up():
                pe.wait_ge(fly_ready, 1)
                for c in range(HC):
                    ins = mm(ps[:, 7, c:c + 1], vb_[0:1, 1, c * P:(c + 1) * P], ones[0:1, 0:1])
                ins.then_inc(fly_turned, 1)
                pe.wait_ge(ffn_w_ready, 1)

            def fly_down():
                pe.wait_ge(fly_ready, 2)
                for c in range(HC):
                    ins = nc.tensor.transpose(ps[:, 7, c * P:(c + 1) * P], vb_[:, 0, c * P:(c + 1) * P], ident[:, :])
                ins.then_inc(fly_turned, 1)
                pe.wait_ge(ffn_w_ready, 2)

            def scan(n0):
                pe.wait_ge(scan_loaded, 16 * 6)
                pe.wait_ge(scan_vec_ready, 1)
                for k in range(TAPS):
                    for c in range(C2):
                        ins = mm(ps[:, k // 2, (k % 2) * DI:(k % 2 + 1) * DI], wxs[:, k, c, :], pwt[:, c, :],
                                 first=(c == 0), last=(c == C2 - 1))
                ins.then_inc(cw_psum, 1)
                pe.wait_ge(cw_ready, 1)
                pe.wait_ge(scan_vec_ready, 2)
                for b in range(NB):
                    turn(n0 + b)
                    pe.wait_ge(xnT_ready, n0 + b + 1)
                    xb_ = xnT[:, b * L:(b + 1) * L]
                    if b >= 1:
                        pe.wait_ge(scan_used, b)
                    for c in range(C2):
                        for k in (3, 2, 1, 0):
                            d_ = TAPS - 1 - k
                            ins = nc.tensor.matmul(ps[:, c, d_:L], cw[:, k, c * P:(c + 1) * P], xb_[:, 0:L - d_],
                                                   start=(k == 3), stop=(k == 0))
                        ins.then_inc(xc_psum, 1)
                    for c in range(C2):
                        mm(bank(2 + c), wz[:, c * P:(c + 1) * P], xb_).then_inc(z_psum, 1)
                    pe.wait_ge(xc_ready, 2 * b + 2)
                    for c in range(C2):
                        ins = mm(ps[0:96, 6, :], wx3[:, c, :], xc[:, c, :], first=(c == 0), last=(c == 1))
                    ins.then_inc(xd_psum, 1)
                    pe.wait_ge(xd_act, 4 * b + 1)
                    for c in range(C2):
                        mm(bank(c), wdt[:, c * P:(c + 1) * P], xdf[0:R, :]).then_inc(dt_psum, 1)
                    pe.wait_ge(xs_ready, b + 1)
                    pe.wait_ge(sz_ready, 2 * b + 2)
                    pe.wait_ge(sp_ready, 2 * b + 2)

                    def ysum(j):
                        for c in range(C2):
                            pe.wait_ge(hc_ready, 8 * b + 2 * j + c + 1)
                            for q in range(2):
                                ins = mm(bank(c), ident[:, :], hs[:, c, 2 * j + q, :],
                                         first=(j == 0 and q == 0), last=False)
                        return ins

                    for j in range(NS // 2):
                        if j >= 1:
                            pe.wait_ge(b_used, 8 * b + 2 * j)
                        for q in range(2):
                            ins = mm(bank(2 + q), selb[0:96, 2 * j + q, :], xsb[0:96, :])
                        ins.then_inc(b_psum, 1)
                        if j >= 1:
                            pe.wait_ge(hc_ready, 8 * b + 2 * j)
                        for q in range(2):
                            ins = mm(bank(4 + q), selb[0:96, NS + 2 * j + q, :], xsb[0:96, :])
                        ins.then_inc(c_psum, 1)
                        if j >= 1:
                            ysum(j - 1)
                    ysum(NS // 2 - 1)
                    for c in range(C2):
                        ins = mm(bank(c), diagD[:, c, :], xc[:, c, :], first=False, last=True)
                    ins.then_inc(ysum_ready, 1)
                    pe.wait_ge(yz_ready, 2 * b + 2)
                    for k in range(TPB):
                        for c in range(C2):
                            ins = mm(ps[:, 6, k * P:(k + 1) * P], yz[:, c, k * P:(k + 1) * P], wout[:, c, :],
                                     first=(c == 0), last=(c == 1))
                    ins.then_inc(o_psum, 1)

            def ffn(u, n0):
                for g in range(NB):
                    turn(n0 + g)
                for b in range(NB):
                    n = u * NB + b
                    pe.wait_ge(xnT_ready, n0 + b + 1)
                    for c in range(HC):
                        if n * HC + c >= 2:
                            pe.wait_ge(ff_g_ready, n * HC + c - 1)
                        mm(bank(c % 2), wup[:, c * P:(c + 1) * P], xnT[:, b * L:(b + 1) * L]).then_inc(ff_h_psum, 1)
                    if n >= 2:
                        pe.wait_ge(ff_o_used, n - 1)
                    pe.wait_ge(ff_g_ready, n * HC + HC)
                    for k in range(TPB):
                        o_ = ps[:, 2 + b % 2, k * P:(k + 1) * P]
                        mm(o_, ones[0:1, :], ffbr[0:1, 2, :], True, False)
                        for c in range(HC):
                            ins = mm(o_, gT[:, b % 2, c, k * P:(k + 1) * P], wdn[:, c, :], False, c == HC - 1)
                    ins.then_inc(ff_o_psum, 1)

            def attend(n0):
                pe.wait_ge(att_loaded, 16 * 5)
                for b in range(NB):
                    turn(n0 + b)
                    pe.wait_ge(xnT_ready, n0 + b + 1)
                    if b >= 1:
                        pe.wait_ge(ao_used, b)
                    for w in range(4):
                        mm(bank(w), wq[:, w, :], xnT[:, b * L:(b + 1) * L]).then_inc(qkv_psum, 1)
                    for k in range(TPB):
                        o_ = ps[:, 4, k * P:(k + 1) * P]
                        mm(o_, ones[0:1, :], abr[0:1, 0, :], True, False)
                        ins = mm(o_, xnT[:, b * L + k * P:b * L + (k + 1) * P], wv, False, True)
                    ins.then_inc(qkv_psum, 1)
                    pe.wait_ge(v_ready, b + 1)
                    pe.wait_ge(rope_ready, b + 1)
                    pe.wait_ge(qk_loaded, 16 * 12 * (b + 1))
                    pe.wait_ge(att_loaded, 16 * 6)
                    for j, (qt, h0, nh, pb) in enumerate(MAXSTEPS):
                        n = b * NMS + j
                        if n >= 3:
                            pe.wait_ge(max_used, n - 2)
                        w_ = P * (qt + 1)
                        for h in range(h0, h0 + nh):
                            k_ = 2 * (j % 3) + (h - h0) // pb
                            c_ = ((h - h0) % pb) * w_
                            mm(ps[:, k_, c_:c_ + w_], qs[0:48, h, qt * P:(qt + 1) * P], ks[0:48, h, 0:w_],
                               True, False)
                            ins = mm(ps[:, k_, c_ + qt * P:c_ + w_], ident_b[:, :], maskb[:, 0, :], False, True)
                        ins.then_inc(max_psum, 1)
                    pe.wait_ge(max_used, (b + 1) * NMS)
                    mt_ = ps[0:NH, 7, 0:L // 2].bitcast(BF16)
                    for k in range(TPB):
                        ins = nc.tensor.transpose(mt_[:, k * P:(k + 1) * P], nm[:, k, :], ident_b[:, :])
                    ins.then_inc(m_turned, 1)
                    pe.wait_ge(m_loaded, 16 * (b + 1))

                    def scores(h):
                        n = b * NH + h
                        if h >= 2:
                            pe.wait_ge(p_ready, n - 1)
                        s_ = ps[:, 3 * (h % 2):3 * (h % 2) + 3, :].rearrange("p k f -> p (k f)")
                        for kt in range(TPB):
                            w_ = L - kt * P
                            mm(s_[:, SEG[kt]:SEG[kt] + w_], ks[0:KR, h, kt * P:(kt + 1) * P],
                               qs[0:KR, h, kt * P:L], True, False)
                            ins = mm(s_[:, SEG[kt]:SEG[kt] + P], ident_b[:, :], maskb[:, 1, :], False, True)
                        ins.then_inc(s_psum, 1)

                    def values(g):
                        pe.wait_ge(p_ready, b * NH + GH * (g + 1))
                        if b * NG + g >= 1:
                            pe.wait_ge(o_copied, b * NG + g)
                        for kt in range(TPB):
                            w_ = L - kt * P
                            for j in range(GH):
                                ins = nc.tensor.matmul(ps[32 * j:32 * j + 32, 6, kt * P:L], va[:, kt, GH * g + j, :],
                                                       pt[:, j, SEG[kt]:SEG[kt] + w_],
                                                       start=(kt == 0), stop=(kt == TPB - 1))
                        ins.then_inc(pv_psum, 1)

                    def turn_o(g):
                        n = b * NG + g
                        pe.wait_ge(o_copied, n + 1)
                        pe.wait_ge(on_ready, n) if g >= 1 else None
                        for k in range(TPB):
                            ins = nc.tensor.transpose(ps[:, 7, k * P:(k + 1) * P], ob[:, k * P:(k + 1) * P],
                                                      ident[:, :])
                        ins.then_inc(o_turned, 1)

                    for g in range(NG):
                        for h in range(GH * g, GH * g + GH):
                            scores(h)
                        values(g)
                        turn_o(g)
                    pe.wait_ge(on_ready, NG * (b + 1))
                    for k in range(TPB):
                        ins = nc.tensor.transpose(ps[:, 7, k * P:(k + 1) * P], on[:, k, :], ident[:, :])
                    ins.then_inc(on_turned, 1)
                    pe.wait_ge(onT_ready, b + 1)
                    for k in range(TPB):
                        o_ = ps[:, 0, k * P:(k + 1) * P]
                        mm(o_, ones[0:1, :], abr[0:1, 1, :], True, False)
                        ins = mm(o_, onT[:, k * P:(k + 1) * P], wo, False, True)
                    ins.then_inc(ao_psum, 1)

            pe.wait_ge(const_loaded, 16 * 9)
            pe.wait_ge(ident_ready, 1)
            pe.wait_ge(small_loaded, 16 * 14)
            for g in range(NB):
                pre(0, g, 0)
            moe(0, 0)
            fly_up()
            if STAGES > 1:
                scan(NB)
            if STAGES > 2:
                for g in range(NB):
                    pre(1, g, 2 * NB)
                moe(1, 2 * NB)
                fly_down()
            if STAGES > 3:
                ffn(0, 3 * NB)
            if STAGES > 4:
                attend(4 * NB)
            if STAGES > 5:
                ffn(1, 5 * NB)

        @block.scalar
        def _(act):
            chain = [0]

            def link(ins):
                chain[0] += 1
                ins.then_inc(act_chain, 1)
                act.wait_ge(act_chain, chain[0])

            def take_turned(n, g):
                act.wait_ge(xn_turned, n + 1)
                nc.scalar.copy(xnT[:, g * L:(g + 1) * L], bank(7)).then_inc(xnT_ready, 1)

            def moe(u, n0):
                for g in range(NB):
                    take_turned(n0 + g, g)
                act.wait_ge(pads_ready, u + 1)
                nc.scalar.activation(egate[:, :], dm[:, :], ACT.Exp).then_inc(egate_ready, 1)
                nc.scalar.preload_act_table(ACT.Silu)
                t0, n1 = u * (NST + 1), u * NST

                def copy_x(j, q):
                    act.wait_ge(xg_turned, j + (t0 + 1))
                    nc.scalar.copy(xt[:, q, :], ps[:, 6, 0:P]).then_inc(xt_ready, 1)

                def tile(j, q):
                    act.wait_ge(gate_ready, j + (n1 + 1))
                    nc.scalar.activation(sil[:, q, :], bank(q), ACT.Silu).then_inc(sil_ready, 1)
                    copy_x(j + 1, 1 - q)
                    act.wait_ge(h_turned, j + (n1 + 1))
                    nc.scalar.copy(hT[:, q, :], bank(4)).then_inc(hT_ready, 1)

                copy_x(0, 0)
                tile(0, 0)
                with act.Fori(1, NST, 2) as i:
                    tile(i, 1)
                    tile(i + 1, 0)

            def scan(n0):
                act.wait_ge(cw_psum, 1)
                nc.scalar.copy(cw.rearrange("p k o -> p (k o)"),
                               ps[:, 0:2, :].rearrange("p k f -> p (k f)")).then_inc(cw_ready, 1)
                for b in range(NB):
                    take_turned(n0 + b, b)
                    if b >= 1:
                        act.wait_ge(scan_used, b)
                    for c in range(C2):
                        act.wait_ge(xc_psum, 2 * b + c + 1)
                        nc.scalar.activation(xc[:, c, :], bank(c), ACT.Silu,
                                             bias=cbias[:, c:c + 1]).then_inc(xc_ready, 1)
                    for c in range(C2):
                        act.wait_ge(z_psum, 2 * b + c + 1)
                        nc.scalar.activation(sz[:, c, :], bank(2 + c), ACT.Silu).then_inc(sz_ready, 1)
                    act.wait_ge(xd_psum, b + 1)
                    nc.scalar.copy(xdf[0:R, :], ps[0:R, 6, :]).then_inc(xd_act, 1)
                    nc.scalar.copy(hib[0:96, :], ps[0:96, 6, :]).then_inc(xd_act, 1)
                    nc.scalar.copy(xsb[0:32, :], ps[0:32, 6, :]).then_inc(xd_act, 1)
                    act.wait_ge(xd_vec, 2 * b + 1)
                    nc.scalar.copy(mib[0:96, :], r1[0:96, :]).then_inc(xd_act, 1)
                    nc.scalar.copy(xsb[32:64, :], r1[32:64, :])
                    act.wait_ge(xd_vec, 2 * b + 2)
                    nc.scalar.copy(xsb[64:96, :], r2[64:96, :]).then_inc(xs_ready, 1)
                    for c in range(C2):
                        act.wait_ge(dt_psum, 2 * b + c + 1)
                        if c == 1:
                            act.wait_ge(delta_ready, 2 * b + 1)
                        nc.scalar.activation(xb, bank(c), ACT.Identity, bias=bdt[:, c:c + 1])
                        link(nc.scalar.activation(eb, bank(c), ACT.Abs, bias=bdt[:, c:c + 1]))
                        link(nc.scalar.activation(eb, eb, ACT.Exp, scale=-1.0))
                        nc.scalar.activation(lb, eb, ACT.Ln, bias=1.0).then_inc(sp_ready, 1)
                    for j in range(NS // 2):
                        for c in range(C2):
                            act.wait_ge(delta_ready, 2 * b + c + 1)
                            for n in (2 * j, 2 * j + 1):
                                ins = nc.scalar.activation(dA[:, c, n, 1:L], dl[:, c, 1:L], ACT.Exp,
                                                           scale=a_neg[:, c, n:n + 1])
                            ins.then_inc(dA_ready, 1)

            def ffn(u, n0):
                for g in range(NB):
                    take_turned(n0 + g, g)
                for b in range(NB):
                    n = u * NB + b
                    for c in range(HC):
                        act.wait_ge(ff_h_psum, n * HC + c + 1)
                        if n >= 2:
                            act.wait_ge(ff_o_psum, n - 1)
                        nc.scalar.activation(gT[:, b % 2, c, :], bank(c % 2), ACT.Gelu,
                                             bias=bup[:, c:c + 1]).then_inc(ff_g_ready, 1)

            def attend(n0):
                for b in range(NB):
                    take_turned(n0 + b, b)
                    act.wait_ge(rope_ready, b + 1)
                    nc.scalar.copy(spl[:, 0, :, :], qk).then_inc(part_act, 1)
                    act.wait_ge(part_vec, 2 * b + 1)
                    nc.scalar.copy(spl[:, 1, :, :], q1).then_inc(part_act, 1)
                    act.wait_ge(m_turned, b + 1)
                    nc.scalar.copy(mTs[0:NH, :], ps[0:NH, 7, 0:L // 2].bitcast(BF16)).then_inc(m_copied, 1)
                    for g in range(NG):
                        if b * NG + g >= 1:
                            act.wait_ge(pv_psum, b * NG + g)
                        for j in range(GH):
                            h = GH * g + j
                            act.wait_ge(s_psum, b * NH + h + 1)
                            s_ = ps[:, 3 * (h % 2):3 * (h % 2) + 3, :].rearrange("p k f -> p (k f)")
                            nc.scalar.activation(pt[:, j, :], s_[:, 0:PTW], ACT.Exp,
                                                 scale=float(HD) ** -0.5).then_inc(p_ready, 1)
                        act.wait_ge(pv_psum, b * NG + g + 1)
                        if b * NG + g >= 1:
                            act.wait_ge(o_turned, b * NG + g)
                        nc.scalar.copy(ob, bank(6)).then_inc(o_copied, 1)
                    act.wait_ge(on_turned, b + 1)
                    nc.scalar.copy(onT, bank(7)).then_inc(onT_ready, 1)

            moe(0, 0)
            act.wait_ge(small_loaded, 16 * 14)
            nc.scalar.activation(a_neg[:, :, :], a_neg[:, :, :], ACT.Exp).then_inc(aexp_ready, 1)
            if STAGES > 1:
                scan(NB)
            if STAGES > 2:
                moe(1, 2 * NB)
            if STAGES > 3:
                ffn(0, 3 * NB)
            if STAGES > 4:
                attend(4 * NB)
            if STAGES > 5:
                ffn(1, 5 * NB)

        @block.vector
        def _(dve):
            chain = [0]
            v = nc.vector

            def link(ins):
                chain[0] += 1
                ins.then_inc(vec_chain, 1)
                dve.wait_ge(vec_chain, chain[0])

            def norm(n, g):
                q = n % 2
                for k in range(TPB):
                    ins = v.bn_stats(st[:, q, k, :], x[:, TPB * g + k, :])
                link(ins)
                for k in range(TPB):
                    ins = v.bn_aggr(mv[:, q, k, :], st[:, q, k, :])
                ins.then_inc(ln_stats_ready, 1)
                dve.wait_ge(ln_rstd_ready, n + 1)
                if n >= 2:
                    dve.wait_ge(xn_turned, n - 1)
                for k in range(TPB):
                    ins = v.tensor_scalar(xn[:, g, k, :], x[:, TPB * g + k, :], mv[:, q, k, 0:1], rs[:, q, k:k + 1],
                                          ALU.subtract, ALU.mult)
                ins.then_inc(xn_ready, 1)

            def wide(a, n=E):
                return a.unsqueeze(2).to_broadcast([P, TPB, n])

            def pick(k, scores):
                r8w = r8[:, :].unsqueeze(1).to_broadcast([P, TPB, E])
                link(v.tensor_reduce(red[:, k, :], scores, AX.X, ALU.max))
                link(v.tensor_tensor(oh[:, k, :, :], scores, wide(red[:, k, :]), ALU.is_equal))
                link(v.tensor_tensor(oh[:, k, :, :], oh[:, k, :, :], r8w, ALU.mult))
                link(v.tensor_reduce(red[:, 2 + k, :], oh[:, k, :, :], AX.X, ALU.max))
                link(v.tensor_tensor(oh[:, k, :, :], oh[:, k, :, :], wide(red[:, 2 + k, :]), ALU.is_equal))

            def pre(u, g, n0):
                gt = slice(TPB * g, TPB * (g + 1))
                norm(n0 + g, g)
                dve.wait_ge(logits_ready, NB * u + g + 1)
                link(v.tensor_copy(lg[:, :, :], ps[:, 7, 0:TPB * E].rearrange("p (i e) -> p i e", e=E)))
                pick(0, lg[:, :, :])
                link(v.scalar_tensor_tensor(lg[:, :, :], oh[:, 0, :, :], -3.0e38, lg[:, :, :], ALU.mult, ALU.add))
                pick(1, lg[:, :, :])
                v.tensor_tensor(ohb[:, :, :], oh[:, 0, :, :], oh[:, 1, :, :], ALU.add).then_inc(ohb_ready, 1)
                v.tensor_tensor(dm[:, gt], red[:, 1, :], red[:, 0, :], ALU.subtract)
                if g == 0:
                    link(v.tensor_copy(cum[:, :], base8[:, :]))
                link(v.tensor_copy(cs4[:, :, 0], cum[:, :]))
                dve.wait_ge(ranks_psum, NB * u + g + 1)
                tot = ps[:, 7, 64:64 + TPB * E].rearrange("p (i e) -> p e i", e=E)
                link(v.tensor_copy(cs4[:, :, 1:TPB], tot[:, :, 0:TPB - 1]))
                flat = "p e i -> p (e i)"
                link(v.tensor_tensor_scan(pre4[:, :, :].rearrange(flat), first4[:, :, :].rearrange(flat),
                                          cs4[:, :, :].rearrange(flat), 0.0, ALU.mult, ALU.add))
                v.tensor_tensor(cum[:, :], pre4[:, :, TPB - 1], tot[:, :, TPB - 1], ALU.add)
                link(v.tensor_tensor(sl[:, :, :], pre4[:, :, :].rearrange("p e i -> p i e"),
                                     ps[:, 7, 32:32 + TPB * E].rearrange("p (i e) -> p i e", e=E), ALU.add))
                for k in range(2):
                    link(v.tensor_tensor(oh[:, k, :, :], oh[:, k, :, :], sl[:, :, :], ALU.mult))
                with nc.allow_low_precision(reason="slots are whole numbers below 2**24: exact"):
                    v.tensor_reduce(slots[:, 0, gt], oh[:, 0, :, :], AX.X, ALU.add)
                    v.tensor_reduce(slots[:, 1, gt], oh[:, 1, :, :], AX.X, ALU.add).then_inc(slots_ready, 1)

            def tables(u):
                link(v.tensor_tensor(pads[:, :], cum[:, :], lane[:, :], ALU.add))
                c_ = [cnt[:, k, :] for k in range(4)]
                link(v.tensor_copy(slotf[:, :], slots[:, :, :].rearrange("p k i -> p (k i)")))
                link(v.memset(shift[:, :], 0.0))
                link(v.tensor_tensor(c_[0], cum[:, :], base8[:, :], ALU.subtract))
                link(v.tensor_tensor(cmp[:, :, :], c_[0].unsqueeze(2).to_broadcast([P, E, CT - 1]), steps[:, :, :],
                                     ALU.is_gt))
                link(v.tensor_reduce(c_[1], cmp[:, :, :], AX.X, ALU.add))
                link(v.tensor_tensor_scan(c_[2], ones[:, 0:E], c_[1], 0.0, ALU.mult, ALU.add))
                wide_ = [1, NST + 3, E]
                link(v.tensor_tensor(tmsk[:, 0, :, :], tnum[:, :, :], c_[2][0:1, :].unsqueeze(1).to_broadcast(wide_),
                                     ALU.is_ge))
                link(v.tensor_tensor(tmsk[:, 1, :, :], tmsk[:, 0, :, :], c_[1][0:1, :].unsqueeze(1).to_broadcast(wide_),
                                     ALU.mult))
                link(v.tensor_reduce(trow[:, 0, :], tmsk[:, 0, :, :], AX.X, ALU.add))
                link(v.tensor_reduce(trow[:, 1, :], tmsk[:, 1, :, :], AX.X, ALU.add))
                link(v.tensor_scalar(tabs[:, 0, :], trow[:, 0, :], float(E - 1), None, ALU.min))
                link(v.tensor_tensor(trow[:, 1, :], tnum[:, :, 0], trow[:, 1, :], ALU.subtract))
                link(v.scalar_tensor_tensor(trow[:, 2, :], trow[:, 0, :], float(CT), trow[:, 1, :],
                                            ALU.mult, ALU.add))
                v.tensor_scalar(tabs[:, 1, :], trow[:, 2, :], float(SPARE), None, ALU.min).then_inc(tables_ready, 1)
                link(v.tensor_scalar(shift[:, 1:E], c_[1][:, 0:E - 1], float(P), float(-CT * P), ALU.mult, ALU.add))
                wide_ = [P, 2 * NT, E]
                link(v.tensor_tensor(rmsk[:, :, :], slotf[:, :].unsqueeze(2).to_broadcast(wide_),
                                     base8[:, :].unsqueeze(1).to_broadcast(wide_), ALU.is_ge))
                link(v.tensor_tensor(rmsk[:, :, :], rmsk[:, :, :], shift[:, :].unsqueeze(1).to_broadcast(wide_),
                                     ALU.mult))
                link(v.tensor_reduce(rfix[:, :], rmsk[:, :, :], AX.X, ALU.add))
                link(v.tensor_tensor(dense[:, :], slotf[:, :], rfix[:, :], ALU.add))
                v.memset(cs4[:, :, 0], 0.0).then_inc(pads_ready, 1)

            def moe(u, n0):
                t0, n1 = u * (NST + 1), u * NST

                def act_product(j, q):
                    dve.wait_ge(sil_ready, j + (n1 + 1))
                    dve.wait_ge(up_ready, j + (n1 + 1))
                    v.tensor_tensor(hh[:, q, :], sil[:, q, :], bank(2 + q), ALU.mult).then_inc(h_ready, 1)

                def result(j, q, stored):
                    dve.wait_ge(down_done, j + (n1 + 1))
                    dve.wait_ge(y_stored[q], stored)
                    v.tensor_copy(yt[:, q, :], ps[:, 5, 0:D]).then_inc(y_ready, 1)

                act_product(0, 0)
                with dve.Fori(1, NST, 2) as i:
                    act_product(i, 1)
                    result(i - 1, 0, i * 8 + (8 + 16 * ST0 * u))
                    act_product(i + 1, 0)
                    result(i, 1, i * 8 + (8 + 16 * ST1 * u))
                result(NST - 1, 0, 16 * (ST0 * u + NST // 2 + 1))

                dve.wait_ge(egate_ready, u + 1)
                link(v.tensor_scalar(gsum[:, :], egate[:, :], 1.0, None, ALU.add))
                link(v.reciprocal(gsum[:, :], gsum[:, :]))
                link(v.tensor_scalar(gates[:, 0, :], gsum[:, :], 0.5, None, ALU.mult))
                link(v.tensor_tensor(gates[:, 1, :], gates[:, 0, :], egate[:, :], ALU.mult))
                for g in range(NB):
                    dve.wait_ge(yg_loaded[g % 2], 16 * 2 * TPB * (2 * u + g // 2 + 1))
                    for k in range(2):
                        for i in range(TPB):
                            xi = x[:, TPB * g + i, :]
                            ins = v.scalar_tensor_tensor(xi, yg[:, g % 2, k, i, :],
                                                         gates[:, k, TPB * g + i:TPB * g + i + 1], xi,
                                                         ALU.mult, ALU.add)
                        if k == 0:
                            link(ins)
                    ins.then_inc(combined, 1)
                    dve.wait_ge(combined, NB * u + g + 1)

            def fly_up():
                dve.wait_ge(small_loaded, 16 * 14)
                dve.wait_ge(fly_turned, 1)
                v.tensor_tensor(ffbr[:, 2, :], ffbr[:, 0, :], ffbr[:, 1, :], ALU.add)
                v.tensor_tensor(bup[:, :], ps[:, 7, 0:HC], ubias[:, :], ALU.add).then_inc(ffn_w_ready, 1)

            def fly_down():
                dve.wait_ge(fly_turned, 2)
                v.tensor_copy(wdn[:, :, :].rearrange("p c d -> p (c d)"), bank(7)).then_inc(ffn_w_ready, 1)

            def scan(n0):
                dve.wait_ge(aexp_ready, 1)
                link(v.tensor_scalar(a_neg[:, :, :], a_neg[:, :, :], -1.0, None, ALU.mult))
                dve.wait_ge(scan_loaded, 16 * 6)
                for k in range(TAPS):
                    for c in range(C2):
                        ins = v.tensor_scalar(wxs[:, k, c, :], wxT[:, c, :], dwc[:, c, k:k + 1], None, ALU.mult)
                ins.then_inc(scan_vec_ready, 1)
                for c in range(C2):
                    v.tensor_scalar(diagD[:, c, :], ident[:, :], dcol[:, c:c + 1], None, ALU.mult)
                    link(v.memset(dA[:, c, :, 0:1], 0.0))
                v.tensor_copy(selb[0:96, :, :], self_[0:96]).then_inc(scan_vec_ready, 1)
                for b in range(NB):
                    norm(n0 + b, b)
                    dve.wait_ge(xd_act, 4 * b + 3)
                    v.tensor_tensor(r1[0:96, :], ps[0:96, 6, :], hib[0:96, :], ALU.subtract).then_inc(xd_vec, 1)
                    dve.wait_ge(xd_vec, 2 * b + 1)
                    dve.wait_ge(xd_act, 4 * b + 4)
                    v.tensor_tensor(r2[0:96, :], r1[0:96, :], mib[0:96, :], ALU.subtract).then_inc(xd_vec, 1)
                    for c in range(C2):
                        dve.wait_ge(sp_ready, 2 * b + c + 1)
                        v.scalar_tensor_tensor(dl[:, c, :], xb, 0.0, lb, ALU.max, ALU.add).then_inc(delta_ready, 1)
                        dve.wait_ge(delta_ready, 2 * b + c + 1)
                        dve.wait_ge(xc_ready, 2 * b + c + 1)
                        link(v.tensor_tensor(uu[:, c, :], dl[:, c, :], xc[:, c, :], ALU.mult))
                    for j in range(NS // 2):
                        js = slice(2 * j, 2 * j + 2)
                        dve.wait_ge(b_psum, 4 * b + j + 1)
                        for c in range(C2):
                            v.tensor_tensor(hs[:, c, js, :], uu[:, c, :].unsqueeze(1).to_broadcast([P, 2, L]),
                                            ps[:, 2:4, :], ALU.mult).then_inc(b_used, 1)
                        for c in range(C2):
                            dve.wait_ge(b_used, 8 * b + 2 * j + c + 1)
                            dve.wait_ge(dA_ready, 8 * b + 2 * j + c + 1)
                            h_ = hs[:, c, js, :].rearrange("p n l -> p (n l)")
                            link(v.tensor_tensor_scan(h_, dA[:, c, js, :].rearrange("p n l -> p (n l)"), h_, 0.0,
                                                      ALU.mult, ALU.add))
                        dve.wait_ge(c_psum, 4 * b + j + 1)
                        for c in range(C2):
                            v.tensor_tensor(hs[:, c, js, :], hs[:, c, js, :], ps[:, 4:6, :],
                                            ALU.mult).then_inc(hc_ready, 1)
                    dve.wait_ge(ysum_ready, b + 1)
                    dve.wait_ge(sz_ready, 2 * b + 2)
                    for c in range(C2):
                        v.tensor_tensor(yz[:, c, :], sz[:, c, :], bank(c), ALU.mult).then_inc(yz_ready, 1)
                    dve.wait_ge(o_psum, b + 1)
                    xg = x[:, TPB * b:TPB * (b + 1), :].rearrange("p k d -> p (k d)")
                    v.tensor_tensor(xg, xg, bank(6), ALU.add).then_inc(scan_used, 1)
                    dve.wait_ge(scan_used, b + 1)

            def ffn(u, n0):
                for g in range(NB):
                    norm(n0 + g, g)
                for b in range(NB):
                    n = u * NB + b
                    dve.wait_ge(ff_o_psum, n + 1)
                    xg = x[:, TPB * b:TPB * (b + 1), :].rearrange("p k d -> p (k d)")
                    v.scalar_tensor_tensor(xg, bank(2 + b % 2), 0.5, xg, ALU.mult, ALU.add).then_inc(ff_o_used, 1)
                dve.wait_ge(ff_o_used, NB * (u + 1))

            def attend(n0):
                dve.wait_ge(att_loaded, 16 * 5)
                v.tensor_copy(maskb[:, :, :], maskf).then_inc(att_const, 1)
                for b in range(NB):
                    norm(n0 + b, b)
                    for w in range(2):
                        dve.wait_ge(qkv_psum, 5 * b + 2 * w + 2)
                        v.scalar_tensor_tensor(t1, bank(2 * w), bqk[:, 2 * w:2 * w + 1], cs[:, 0, :],
                                               ALU.add, ALU.mult)
                        link(v.scalar_tensor_tensor(t2, bank(2 * w + 1), bqk[:, 2 * w + 1:2 * w + 2], cs[:, 1, :],
                                                    ALU.add, ALU.mult))
                        if w == 0:
                            if b >= 1:
                                dve.wait_ge(parts_stored, 16 * b)
                            link(v.tensor_tensor(qk[:, 0, :], t1, t2, ALU.add))
                        else:
                            v.tensor_tensor(qk[:, 1, :], t1, t2, ALU.add).then_inc(rope_ready, 1)
                    dve.wait_ge(part_act, 2 * b + 1)
                    v.tensor_tensor(q1, qk, spl[:, 0, :, :], ALU.subtract).then_inc(part_vec, 1)
                    dve.wait_ge(part_act, 2 * b + 2)
                    v.tensor_tensor(spl[:, 2, :, :], q1, spl[:, 1, :, :], ALU.subtract).then_inc(part_vec, 1)
                    dve.wait_ge(qkv_psum, 5 * b + 5)
                    if b == 0:
                        dve.wait_ge(att_const, 2)
                    v.tensor_copy(va[:, :, :, 0:HD],
                                  bank(4).rearrange("p (k h e) -> p k h e", k=TPB, h=NH)).then_inc(v_ready, 1)
                    for j, (qt, h0, nh, pb) in enumerate(MAXSTEPS):
                        dve.wait_ge(max_psum, b * NMS + j + 1)
                        w_ = P * (qt + 1)
                        k_ = 2 * (j % 3)
                        if pb == 1:
                            src = ps[:, k_:k_ + 2, 0:w_]
                        else:
                            src = ps[:, k_:k_ + 2, :].rearrange("p k (h f) -> p (k h) f", f=w_)
                        v.tensor_reduce(nm[:, qt, h0:h0 + nh], src, AX.X, ALU.max, negate=True).then_inc(max_used, 1)
                    for g in range(NG):
                        n = b * NG + g
                        dve.wait_ge(o_turned, n + 1)
                        o4 = bank(7).rearrange("p (k j e) -> p k j e", k=TPB, j=GH)
                        link(v.reciprocal(rden, o4[:, :, :, HD]))
                        for k in range(TPB):
                            ins = v.tensor_tensor(
                                on[:, k, 32 * g:32 * g + 32].rearrange("p (j e) -> p j e", j=GH), o4[:, k, :, 0:HD],
                                rden[:, k, :].unsqueeze(2).to_broadcast([P, GH, HD]), ALU.mult)
                        ins.then_inc(on_ready, 1)
                    dve.wait_ge(ao_psum, b + 1)
                    xg = x[:, TPB * b:TPB * (b + 1), :].rearrange("p k d -> p (k d)")
                    v.tensor_tensor(xg, xg, bank(0), ALU.add).then_inc(ao_used, 1)
                    dve.wait_ge(ao_used, b + 1)

            dve.wait_ge(const_loaded, 16 * 9)
            dve.wait_ge(x_loaded, 16)
            v.memset(ones_b[:, :], 1.0)
            v.tensor_copy(before_b[:, :], before[:, :])
            v.tensor_copy(ident_b[:, :], ident[:, :]).then_inc(ident_ready, 1)
            v.memset(ve2[:, NB:NB + 1], 0.0).then_inc(y_ready, 1)
            for g in range(NB):
                pre(0, g, 0)
            tables(0)
            moe(0, 0)
            fly_up()
            if STAGES > 1:
                scan(NB)
            if STAGES > 2:
                for g in range(NB):
                    pre(1, g, 2 * NB)
                tables(1)
                moe(1, 2 * NB)
                fly_down()
            if STAGES > 3:
                ffn(0, 3 * NB)
            if STAGES > 4:
                attend(4 * NB)
            if STAGES > 5:
                ffn(1, 5 * NB)
            for b in range(NB):
                v.memset(ve2[:, b:b + 1], 0.0).then_inc(x_done, 1)


def kernel(**inputs):
    import numpy as np
    import concourse.bacc as bacc
    from concourse.bass_utils import run_bass_kernel_spmd

    g = {k: np.asarray(v) for k, v in inputs.items()}
    f32 = np.float32

    def cols(v, n):
        return v.reshape(n, 128).T

    L, E, D = 512, 8, 128
    sw = np.arange(D) ^ 1
    half = 4
    inv = (f32(1.0) / np.power(f32(10000.0), np.arange(half, dtype=f32) / f32(half))).astype(f32)
    ang = np.arange(L, dtype=f32)[:, None] * inv[None, :]
    pair = (np.arange(D) % 8) // 2
    cos = np.cos(ang).astype(f32)[:, pair].T
    sin = np.sin(ang).astype(f32)[:, pair].T * np.where(np.arange(D) % 2 == 0, -1.0, 1.0).astype(f32)[:, None]
    i, j = np.arange(128)[:, None], np.arange(128)[None, :]
    big = f32(-1.0e30)
    mask = np.stack([np.where(j > i, big, f32(0)), np.where(i > j, big, f32(0))], 1).astype(f32)
    sel = np.zeros((96, 16, 128), f32)
    for r in range(96):
        if 8 <= r % 32 < 24:
            sel[r, r % 32 - 8, :] = 1.0
    wx = g["L0_attn_W_x"].reshape(2, 128, 24).transpose(1, 0, 2)
    wx3 = np.zeros((128, 2, 96), f32)
    for r in range(3):
        wx3[:, :, 32 * r:32 * r + 24] = wx
    W_in = g["L0_attn_W_in"]
    Wq, Wk = g["L1_attn_Wq"], g["L1_attn_Wk"]
    bq, bk = g["L1_attn_bq"], g["L1_attn_bk"]
    arrays = {
        "x": g["L0_attn_x"].reshape(-1, D),
        "ident": np.eye(128, dtype=f32),
        "rank8": np.broadcast_to(np.arange(E, 0, -1, dtype=f32), (128, E)),
        "base8": np.broadcast_to(np.arange(E, dtype=f32) * (17 * 128), (128, E)),
        "lane": np.broadcast_to(np.arange(128, dtype=f32)[:, None], (128, E)),
        "first4": np.broadcast_to(np.arange(4) > 0, (128, E, 4)),
        "steps": np.broadcast_to(np.arange(16, dtype=f32) * 128, (128, E, 16)),
        "tnum": np.broadcast_to(np.arange(42, dtype=f32)[:, None], (1, 42, E)),
        "before": np.triu(np.ones((128, 128), f32), 1),
        "w_router": g["L0_ffn_W_router"].T,
        "w_gate": g["L0_ffn_W_gate"].transpose(2, 0, 1),
        "w_up": g["L0_ffn_W_up"].transpose(2, 0, 1),
        "w_down": g["L0_ffn_W_down"].reshape(E, D, 4, 128).transpose(3, 0, 2, 1),
        "up_w": g["L1_ffn_up_weights"].reshape(9, -1),
        "down_w": g["L1_ffn_down_weights"].reshape(9, -1),
        "up_bias": cols(g["L1_ffn_up_bias"], 4),
        "b_con": g["L1_ffn_b_con"][None], "down_bias": g["L1_ffn_down_bias"][None],
        "w_exp": g["L1_ffn_W_exp"], "b_exp": g["L1_ffn_b_exp"][None], "w_conT": g["L1_ffn_W_con"].T,
        "conv_bias": cols(g["L0_attn_conv_bias"], 2), "b_dt": cols(g["L0_attn_b_dt"], 2),
        "dskip": cols(g["L0_attn_D"], 2),
        "dw": g["L0_attn_dw_kernel"].T.reshape(2, 128, 4).transpose(1, 0, 2),
        "w_dt": g["L0_attn_W_dt"],
        "a_log": g["L0_attn_A_log"].reshape(2, 128, 8).transpose(1, 0, 2),
        "pw": g["L0_attn_pw_kernel"].reshape(2, 128, 256).transpose(1, 0, 2),
        "wxT": W_in[:, :256].T.reshape(2, 128, 128).transpose(1, 0, 2),
        "wz": W_in[:, 256:],
        "w_out": g["L0_attn_W_out"].reshape(2, 128, 128).transpose(1, 0, 2),
        "w_x3": wx3, "sel": sel,
        "wq": np.stack([Wq.T, Wq.T[:, sw], Wk.T, Wk.T[:, sw]], 1),
        "bqk": np.stack([bq, bq[sw], bk, bk[sw]], 1),
        "wv": g["L1_attn_Wv"].T, "wo": g["L1_attn_Wo"].T,
        "bv": g["L1_attn_bv"][None], "bo": g["L1_attn_bo"][None],
        "cossin": np.stack([cos, sin], 1), "mask": mask,
    }
    nc = bacc.Bacc("TRN2", target_bir_lowering=False, num_devices=1)
    maps, aps = {}, {}
    for name, a in arrays.items():
        a = np.ascontiguousarray(a, dtype=f32)
        maps["in_" + name] = a
        aps[name] = nc.dram_tensor("in_" + name, a.shape, F32, kind="ExternalInput").ap()
    import ml_dtypes
    a = np.ones((1, 16, 512), ml_dtypes.bfloat16)
    maps["in_ones_row"] = a
    aps["ones_row"] = nc.dram_tensor("in_ones_row", a.shape, BF16, kind="ExternalInput").ap()
    out = nc.dram_tensor("out_dram", (2048, D), F32, kind="ExternalOutput").ap()
    macaron_kernel(nc, aps, out)
    r = run_bass_kernel_spmd(nc, [maps], core_ids=[0])
    return r.results[0]["out_dram"].reshape(4, 512, 128)
```

```python
from contextlib import ExitStack

import concourse.bass as bass
from concourse import mybir

P = 128
ALU = mybir.AluOpType
ACT = mybir.ActivationFunctionType
AX = mybir.AxisListType
F32 = mybir.dt.float32
BF16 = mybir.dt.bfloat16
I32 = mybir.dt.int32


def macaron_kernel(nc, t, out):
    TOK, D = t["x"].shape
    NT = TOK // P
    NB = 4
    TPB = NT // NB
    L = TPB * P
    E = t["w_router"].shape[1]
    F = t["w_gate"].shape[2]
    FC = F // P
    DI = t["pw"].shape[2]
    C2 = DI // P
    NS = t["a_log"].shape[2]
    TAPS = t["dw"].shape[2]
    R = t["w_dt"].shape[0]
    HID = t["w_exp"].shape[1]
    HC = HID // P
    STG = t["up_w"].shape[0]
    NH = 16
    HD = D // NH
    GH = 4
    NG = NH // GH
    SEG = [0, 512, 1024, 896]
    PTW = 1280
    EPS = 1e-5
    CT = NT + 1
    NST = 2 * NT + E - 1
    LD0, LD1 = NST // 2 + 2, NST // 2 + 1
    ST0, ST1 = NST // 2 + 1, NST // 2
    SPARE = E * CT
    KP = 6 * HD
    KR = KP + 1
    assert D == P and L == 512 and TAPS == 4 and NS == 8 and R == 8

    with ExitStack() as ctx:
        def sb(name, shape, dt=F32):
            return ctx.enter_context(nc.sbuf_tensor(name, shape, dt))

        def sem(name):
            return ctx.enter_context(nc.semaphore(name))

        ps = ctx.enter_context(nc.psum_tensor("ps", [P, 8, 512], F32))

        def bank(k):
            return ps[:, k, :]

        x = sb("x", [P, NT, D])
        xn = sb("xn", [P, NB, TPB, D])
        xnT = sb("xnT", [P, TOK])
        st = sb("st", [P, 2, TPB, 6])
        mv = sb("mv", [P, 2, TPB, 2])
        rs = sb("rs", [P, 2, TPB])
        ve = sb("ve", [P, TPB])
        mhalf = sb("mhalf", [P, TPB])
        ident = sb("ident", [P, P])
        ident_b = sb("ident_b", [P, P], BF16)
        ones = sb("ones", [P, P])
        wr = sb("wr", [P, E])
        wbig = sb("wbig", [P, 3 * E * F])
        wg = wbig[:, 0:E * F].rearrange("p (e f) -> p e f", e=E)
        wu = wbig[:, E * F:2 * E * F].rearrange("p (e f) -> p e f", e=E)
        wd = wbig[:, 2 * E * F:3 * E * F].rearrange("p (e c d) -> p e c d", e=E, c=FC)
        r8 = sb("r8", [P, E])
        base8 = sb("base8", [P, E])
        first4 = sb("first4", [P, E, TPB])
        steps = sb("steps", [P, E, CT - 1])
        tnum = sb("tnum", [1, NST + 3, E])
        before = sb("before", [P, P])
        before_b = sb("before_b", [P, P], BF16)
        ones_b = sb("ones_b", [P, P], BF16)
        lg = sb("lg", [P, TPB, E])
        oh = sb("oh", [P, 2, TPB, E])
        sl = sb("sl", [P, TPB, E])
        ohb = sb("ohb", [P, TPB, E], BF16)
        red = sb("red", [P, 4, TPB])
        cs4 = sb("cs4", [P, E, TPB])
        pre4 = sb("pre4", [P, E, TPB])
        cum = sb("cum", [P, E])
        slots = sb("slots", [P, 2, NT], I32)
        pads = sb("pads", [P, E], I32)
        dm = sb("dm", [P, NT])
        egate = sb("egate", [P, NT])
        gates = sb("gates", [P, 2, NT])
        gsum = sb("gsum", [P, NT])
        cnt = sb("cnt", [P, 4, E])
        cmp = sb("cmp", [P, E, CT - 1])
        shift = sb("shift", [P, E])
        slotf = sb("slotf", [P, 2 * NT])
        rfix = sb("rfix", [P, 2 * NT])
        dense = sb("dense", [P, 2 * NT], I32)
        trow = sb("trow", [1, 3, NST + 3])
        tabs = sb("tabs", [1, 2, NST + 3], I32)
        zrow = sb("zrow", [P, D])
        ve2 = sb("ve2", [P, NB + 1])
        ARENA = 29632
        ar = sb("ar", [P, ARENA])

        class Arena:
            def __init__(self):
                self.at = 0

            def take(self, count, pattern=None, **k):
                a = ar[:, self.at:self.at + count]
                self.at += count
                assert self.at <= ARENA, self.at
                return a.rearrange(pattern, **k) if pattern else a

        m = Arena()
        sil = m.take(2 * F, "p (b f) -> p b f", b=2)
        hh = m.take(2 * F, "p (b f) -> p b f", b=2)
        hT = m.take(2 * F, "p (b f) -> p b f", b=2)
        xg = m.take(2 * D, "p (b f) -> p b f", b=2)
        xt = m.take(2 * P, "p (b f) -> p b f", b=2)
        yt = m.take(2 * D, "p (b f) -> p b f", b=2)
        rmsk = m.take(2 * NT * E, "p (s e) -> p s e", e=E)
        tmsk = m.take(2 * (NST + 3) * E, "p (m j e) -> p m j e", m=2, e=E)[0:1]
        bw = m.take(2 * 2 * HID, "p (b f) -> p b f", b=2)
        va_ = m.take(2 * HID, "p (b f) -> p b f", b=2)
        vb_ = m.take(2 * HID, "p (b f) -> p b f", b=2)
        vt_ = m.take(HID)
        wup = sb("wup", [P, HID])
        wdn = sb("wdn", [P, HC, D])
        bup = sb("bup", [P, HC])
        ubias = sb("ubias", [P, HC])
        ffbr = sb("ffbr", [1, 3, D])
        a_neg = sb("a_neg", [P, C2, NS])
        s = Arena()
        cw = s.take(TAPS * DI, "p (k o) -> p k o", k=TAPS)
        wz = s.take(DI)
        diagD = s.take(C2 * P, "p (c d) -> p c d", c=C2)
        wout = s.take(C2 * D, "p (c d) -> p c d", c=C2)
        wx3 = s.take(C2 * 96, "p (c r) -> p c r", c=C2)
        dA = s.take(C2 * 6 * L, "p (c n l) -> p c n l", c=C2, n=6)
        hs = s.take(C2 * NS * L, "p (c n l) -> p c n l", c=C2, n=NS)
        xc = s.take(2 * C2 * L, "p (b c l) -> p b c l", b=2, c=C2)
        sz = s.take(2 * C2 * L, "p (b c l) -> p b c l", b=2, c=C2)
        xb = s.take(C2 * L, "p (c l) -> p c l", c=C2)
        eb = s.take(C2 * L, "p (c l) -> p c l", c=C2)
        dl = s.take(2 * C2 * L, "p (b c l) -> p b c l", b=2, c=C2)
        uu = s.take(2 * C2 * L, "p (b c l) -> p b c l", b=2, c=C2)
        yz = s.take(C2 * L, "p (c l) -> p c l", c=C2)
        pwt = yz[:, 0, 0:C2 * DI].rearrange("p (c o) -> p c o", c=C2)
        wxT = yz[:, 1, 0:C2 * P].rearrange("p (c d) -> p c d", c=C2)
        xdf = s.take(L)
        r1 = s.take(L)
        hib = s.take(L // 2).bitcast(BF16)
        mib = s.take(L // 2).bitcast(BF16)
        xsb = s.take(L).bitcast(BF16).rearrange("p (b l) -> p b l", b=2)
        selb = sb("selb", [P, 2 * NS, P], BF16)
        wxs = hs.rearrange("p c n l -> p (c n l)")[:, 4096:4096 + TAPS * C2 * P].rearrange(
            "p (k c d) -> p k c d", k=TAPS, c=C2)
        self_ = hs.rearrange("p c n l -> p (c n l)")[:, 0:2 * NS * P].rearrange("p (j m) -> p j m", j=2 * NS)
        yg = hs.rearrange("p c n l -> p (c n l)")[:, 2048:2048 + 4 * TPB * D].rearrange(
            "p (b k i d) -> p b k i d", b=2, k=2, i=TPB)
        cbias = sb("cbias", [P, C2])
        bdt = sb("bdt", [P, C2])
        dcol = sb("dcol", [P, C2])
        dwc = sb("dwc", [P, C2, TAPS])
        wdt = sb("wdt", [R, DI])
        a = Arena()
        wq = a.take(4 * D, "p (w d) -> p w d", w=4)
        wv = a.take(D)
        wo = a.take(D)
        cs = a.take(2 * L, "p (w l) -> p w l", w=2)
        t1 = a.take(L)
        t2 = a.take(L)
        qk = a.take(2 * L, "p (w l) -> p w l", w=2)
        q1 = a.take(2 * L, "p (w l) -> p w l", w=2)
        qs = a.take(NH * L).bitcast(BF16).rearrange("p (b h l) -> p b h l", b=2, h=NH)
        ks = a.take(NH * L).bitcast(BF16).rearrange("p (b h l) -> p b h l", b=2, h=NH)
        va = a.take(2 * TPB * NH * 32, "p (b k h e) -> p b k h e", b=2, k=TPB, h=NH)
        ob = a.take(L)
        on = a.take(TPB * D, "p (k e) -> p k e", k=TPB)
        nm = a.take(TPB * NH // 2).bitcast(BF16).rearrange("p (k h) -> p k h", k=TPB)
        mTs = a.take(L // 2).bitcast(BF16)
        rden = a.take(TPB * GH, "p (k j) -> p k j", k=TPB)
        maskf = a.take(2 * P, "p (w d) -> p w d", w=2)
        pt = wbig[:, 0:2 * GH * PTW].rearrange("p (b h f) -> p b h f", b=2, h=GH)
        rest = 2 * GH * PTW
        spl = wbig[:, rest:rest + 3 * L].bitcast(BF16).rearrange("p (j w l) -> p j w l", j=3, w=2)
        onT = wbig[:, rest + 3 * L:rest + 4 * L]
        gT = wbig[:, 0:2 * HC * L].rearrange("p (b c l) -> p b c l", b=2, c=HC)
        maskb = sb("maskb", [P, 2, P], BF16)
        bqk = sb("bqk", [P, 4])
        abr = a.take(2 * D, "p (w d) -> p w d", w=2)[0:1]

        qk_dram = nc.dram_tensor("qk_parts", [NB, 3, 2, P, L], BF16, kind="Internal").ap()

        xs_dram = nc.dram_tensor("slot_rows", [(SPARE + 1) * P, D], F32, kind="Internal").ap()
        ys_dram = nc.dram_tensor("slot_results", [NST * P, D], F32, kind="Internal").ap()
        m_dram = nc.dram_tensor("row_maxima", [NB, NH, L], BF16, kind="Internal").ap()

        x_loaded = sem("x_loaded")
        x_rest_loaded = sem("x_rest_loaded")
        const_loaded = sem("const_loaded")
        moe_loaded = sem("moe_loaded")
        small_loaded = sem("small_loaded")
        pool_chain = sem("pool_chain")
        vec_chain = sem("vec_chain")
        act_chain = sem("act_chain")
        ident_ready = sem("ident_ready")
        ln_stats_ready = sem("ln_stats_ready")
        ln_rstd_ready = sem("ln_rstd_ready")
        xn_ready = sem("xn_ready")
        xn_turned = sem("xn_turned")
        xnT_ready = sem("xnT_ready")
        logits_ready = sem("logits_ready")
        ohb_ready = sem("ohb_ready")
        ranks_psum = sem("ranks_psum")
        slots_ready = sem("slots_ready")
        pads_ready = sem("pads_ready")
        pads_stored = sem("pads_stored")
        dense_ready = sem("dense_ready")
        tables_ready = sem("tables_ready")
        egate_ready = sem("egate_ready")
        spare_zeroed = sem("spare_zeroed")
        rows_stored = sem("rows_stored")
        xg_loaded = [sem("xg_loaded_even"), sem("xg_loaded_odd")]
        xg_turned = sem("xg_turned")
        xt_ready = sem("xt_ready")
        y_ready = sem("y_ready")
        y_stored = [sem("y_stored_even"), sem("y_stored_odd")]
        yg_loaded = [sem("yg_loaded_even"), sem("yg_loaded_odd")]
        combined = sem("combined")
        gate_ready = sem("gate_ready")
        up_ready = sem("up_ready")
        sil_ready = sem("sil_ready")
        h_ready = sem("h_ready")
        h_turned = sem("h_turned")
        hT_ready = sem("hT_ready")
        down_done = sem("down_done")
        bw_loaded = [sem("bw_loaded_even"), sem("bw_loaded_odd")]
        wcon_loaded = sem("wcon_loaded")
        fly_ready = sem("fly_ready")
        fly_turned = sem("fly_turned")
        ffn_w_ready = sem("ffn_w_ready")
        scan_loaded = sem("scan_loaded")
        scan_vec_ready = sem("scan_vec_ready")
        cw_psum = sem("cw_psum")
        cw_ready = sem("cw_ready")
        aexp_ready = sem("aexp_ready")
        xc_psum = sem("xc_psum")
        z_psum = sem("z_psum")
        xc_ready = sem("xc_ready")
        sz_ready = sem("sz_ready")
        xd_psum = sem("xd_psum")
        xd_act = sem("xd_act")
        xd_vec = sem("xd_vec")
        xs_ready = sem("xs_ready")
        dt_psum = sem("dt_psum")
        dt_taken = sem("dt_taken")
        sp_ready = sem("sp_ready")
        delta_ready = sem("delta_ready")
        dA_ready = sem("dA_ready")
        b_psum = sem("b_psum")
        b_used = sem("b_used")
        c_psum = sem("c_psum")
        hc_ready = sem("hc_ready")
        ysum_ready = sem("ysum_ready")
        yz_ready = sem("yz_ready")
        o_psum = sem("o_psum")
        scan_used = sem("scan_used")
        ff_h_psum = sem("ff_h_psum")
        ff_g_ready = sem("ff_g_ready")
        ff_o_psum = sem("ff_o_psum")
        ff_o_used = sem("ff_o_used")
        att_loaded = sem("att_loaded")
        att_const = sem("att_const")
        ones_loaded = sem("ones_loaded")
        qkv_psum = sem("qkv_psum")
        qkv_used = sem("qkv_used")
        rope_ready = sem("rope_ready")
        part_act = sem("part_act")
        part_vec = sem("part_vec")
        parts_stored = sem("parts_stored")
        qk_loaded = sem("qk_loaded")
        v_ready = sem("v_ready")
        max_psum = sem("max_psum")
        max_used = sem("max_used")
        m_turned = sem("m_turned")
        m_copied = sem("m_copied")
        m_stored = sem("m_stored")
        m_loaded = sem("m_loaded")
        s_psum = sem("s_psum")
        p_ready = sem("p_ready")
        pv_psum = sem("pv_psum")
        o_copied = sem("o_copied")
        o_turned = sem("o_turned")
        on_ready = sem("on_ready")
        on_turned = sem("on_turned")
        onT_ready = sem("onT_ready")
        ao_psum = sem("ao_psum")
        ao_used = sem("ao_used")
        out_stored = sem("out_stored")

        x_tiles = t["x"].rearrange("(i p) d -> p i d", p=P)
        out_tiles = out.rearrange("(i p) d -> p i d", p=P)
        FFN_NORM = [3 * NB, 3 * NB + 1, 3 * NB + 3, 3 * NB + 5]
        FFN_BANK = [2, 3, 4, 2, 5, 6, 2, 5]
        ATT_NORM = [3 * NB + 2, 3 * NB + 4, 3 * NB + 6, 3 * NB + 7]
        MAXSTEPS = [(qt, h0, nh) for qt, nh in ((3, 1), (2, 1), (1, 2), (0, 4)) for h0 in range(0, NH, nh)]
        NMS = len(MAXSTEPS)
        products = [(kt, j) for kt in range(TPB) for j in range(GH)]
        VALUE_STEPS = [products[0:3], products[3:6], products[6:10], products[10:16]]
        PLACES = 8
        PER = -(-NMS // PLACES)

        def max_steps(g, k):
            place = GH * g + k - 6
            return range(PER * place, min(PER * (place + 1), NMS)) if 0 <= place < PLACES else range(0)

        ROUTE_BANK = (5, 7)

        block = ctx.enter_context(nc.Block())

        @block.sync
        def _(sp):
            sp.dma_start(x[:, 0:TPB, :], x_tiles[:, 0:TPB, :]).then_inc(x_loaded, 16)
            for dst, src in ((ident[:, :], t["ident"]), (wr[:, :], t["w_router"]), (r8[:, :], t["rank8"]),
                             (base8[:, :], t["base8"]), (first4[:, :, :], t["first4"]),
                             (steps[:, :, :], t["steps"]), (tnum[:, :, :], t["tnum"]), (before[:, :], t["before"])):
                sp.dma_start(dst, src).then_inc(const_loaded, 16)
            sp.dma_start(x[:, TPB:NT, :], x_tiles[:, TPB:NT, :]).then_inc(x_rest_loaded, 16)
            sp.dma_start(wg, t["w_gate"]).then_inc(moe_loaded, 16)
            sp.dma_start(wu, t["w_up"]).then_inc(moe_loaded, 16)
            sp.dma_start(wd, t["w_down"]).then_inc(moe_loaded, 16)
            small = [(ubias[:, :], t["up_bias"]), (ffbr[:, 0, :], t["b_con"]), (ffbr[:, 1, :], t["down_bias"]),
                     (cbias[:, :], t["conv_bias"]), (bdt[:, :], t["b_dt"]), (dcol[:, :], t["dskip"]),
                     (dwc[:, :, :], t["dw"]), (wdt[:, :], t["w_dt"]), (a_neg[:, :, :], t["a_log"]),
                     (bqk[:, :], t["bqk"]),
                     (va_[:, 0, :], t["w_exp"]), (va_[0:1, 1, :], t["b_exp"])]

            for dst, src in small:
                sp.dma_start(dst, src).then_inc(small_loaded, 16)
            def moe(u):
                def load(j, q):
                    r = sp.value_load(tabs[0:1, 1, bass.ds(j, 1)], min_val=0, max_val=SPARE)
                    sp.dma_start(xg[:, q, :], xs_dram[bass.ds(r * P, P), :]).then_inc(xg_loaded[q], 16)

                def store(j, q):
                    sp.dma_start(ys_dram[bass.ds(j * P, P), :], yt[:, q, :]).then_inc(y_stored[q], 16)

                t0, n0 = u * (NST + 1), u * NST
                sp.wait_ge(spare_zeroed, 16)
                sp.wait_ge(pads_ready, u + 1)
                for e in range(E):
                    r = sp.value_load(pads[0:1, e:e + 1], min_val=0, max_val=SPARE * P - P)
                    sp.dma_start(xs_dram[bass.ds(r, P), :], zrow[:, :]).then_inc(pads_stored, 16)
                sp.wait_ge(tables_ready, u + 1)
                sp.wait_ge(rows_stored, 16 * 2 * NT * (u + 1))
                sp.wait_ge(pads_stored, 16 * E * (u + 1))
                load(0, 0)
                load(1, 1)
                sp.wait_ge(xg_turned, t0 + 1)
                load(2, 0)
                with sp.Fori(1, NST, 2) as i:
                    for j, q in ((i, 1), (i + 1, 0)):
                        sp.wait_ge(xg_turned, j + (t0 + 1))
                        load(j + 2, q)
                        sp.wait_ge(y_ready, j + (n0 + 1))
                        store(j - 1, 1 - q)
                sp.wait_ge(y_ready, n0 + NST + 1)
                store(NST - 1, 0)
                sp.wait_ge(xg_loaded[0], 16 * LD0 * (u + 1))

            sp.sem_inc(y_stored[0], 16)
            sp.sem_inc(y_stored[1], 16)
            moe(0)
            sp.wait_ge(fly_turned, 1)
            for dst, src in ((pwt, t["pw"]), (wxT, t["wxT"]), (wz, t["wz"]), (wout, t["w_out"]),
                             (wx3, t["w_x3"]), (self_[0:96], t["sel"])):
                sp.dma_start(dst, src).then_inc(scan_loaded, 16)
            moe(1)
            sp.wait_ge(fly_turned, 2)
            for dst, src in ((wq, t["wq"]), (wv, t["wv"]), (wo, t["wo"]), (cs, t["cossin"]),
                             (maskf, t["mask"]), (abr[:, 0, :], t["bv"]), (abr[:, 1, :], t["bo"])):
                sp.dma_start(dst, src).then_inc(att_loaded, 16)
            for w in range(2):
                sp.dma_start(ks[KP:KR, w, :, :], t["ones_row"]).then_inc(ones_loaded, 16)
            for b in range(NB):
                q = b % 2
                sp.wait_ge(part_vec, 2 * b + 2)
                sp.wait_ge(part_act, 2 * b + 2)
                sp.dma_start(qk_dram[b].rearrange("j w p l -> p j w l"), spl).then_inc(parts_stored, 16)
                sp.wait_ge(parts_stored, 16 * (b + 1))
                if b >= 2:
                    sp.wait_ge(s_psum, 2 * NH * (b - 1))
                for r, (i, j) in enumerate(((0, 0), (0, 1), (1, 0), (1, 1), (0, 2), (2, 0))):
                    sp.dma_start(qs[HD * r:HD * (r + 1), q, :, :],
                                 qk_dram[b, i, 0].rearrange("(h d) l -> d h l", d=HD)).then_inc(qk_loaded, 16)
                    sp.dma_start(ks[HD * r:HD * (r + 1), q, :, :],
                                 qk_dram[b, j, 1].rearrange("(h d) l -> d h l", d=HD)).then_inc(qk_loaded, 16)
                sp.wait_ge(m_copied, b + 1)
                sp.dma_start(m_dram[b], mTs[0:NH, :]).then_inc(m_stored, 16)
                sp.wait_ge(m_stored, 16 * (b + 1))
                sp.dma_start(qs[KP:KR, q, :, :], m_dram[b].unsqueeze(0)).then_inc(m_loaded, 16)
            for b in range(NB):
                sp.wait_ge(ff_o_used, NB + b + 1)
                sp.dma_start(out_tiles[:, TPB * b:TPB * (b + 1), :],
                             x[:, TPB * b:TPB * (b + 1), :]).then_inc(out_stored, 16)
            sp.wait_ge(out_stored, 16 * NB)

        @block.gpsimd
        def _(pool):
            chain = [0]

            def link(ins):
                chain[0] += 1
                ins.then_inc(pool_chain, 1)
                pool.wait_ge(pool_chain, chain[0])

            def ln_rstd(n):
                pool.wait_ge(ln_stats_ready, n + 1)
                link(nc.gpsimd.tensor_scalar(ve[:, :], mv[:, n % 2, :, 1], EPS, None, ALU.add))
                nc.gpsimd.tensor_tensor(rs[:, n % 2, :], ve[:, :], mhalf[:, :], ALU.pow).then_inc(ln_rstd_ready, 1)

            def scatter(u, g):
                pool.wait_ge(slots_ready, NB * u + g + 1)
                for k in range(2):
                    for i in range(TPB):
                        nc.gpsimd.indirect_dma_start(
                            xs_dram[:, :], bass.IndirectOffsetOnAxis(ap=slots[:, k, TPB * g + i:TPB * g + i + 1], axis=0),
                            xn[:, g, i, :], None).then_inc(rows_stored, 16)

            def gather(u):
                pool.wait_ge(dense_ready, u + 1)
                pool.wait_ge(y_stored[0], 16 * (ST0 * (u + 1) + 1))
                pool.wait_ge(y_stored[1], 16 * (ST1 * (u + 1) + 1))
                for g in range(NB):
                    if NB * u + g >= 2:
                        pool.wait_ge(combined, NB * u + g - 1)
                    for k in range(2):
                        for i in range(TPB):
                            nc.gpsimd.indirect_dma_start(
                                yg[:, g % 2, k, i, :], None, ys_dram[:, :],
                                bass.IndirectOffsetOnAxis(ap=dense[:, NT * k + TPB * g + i:NT * k + TPB * g + i + 1],
                                                          axis=0),
                            ).then_inc(yg_loaded[g % 2], 16)
                        if k == 0 and g >= 1:
                            ln_rstd(NB + g - 1 if u == 0 else (FFN_NORM[0], FFN_NORM[1], FFN_NORM[2])[g - 1])
                    if u == 1 and g == 2:
                        ln_rstd(ATT_NORM[0])
                if u == 0:
                    ln_rstd(2 * NB - 1)

            def stage(k, strd, parts, src, dst, up):
                nb = HID // (2 * strd)
                pool.wait_ge(bw_loaded[k % 2], 16 * (k // 2 + 1))
                w = bw[:, k % 2, :].rearrange("p (n s o i) -> p n s o i", n=nb, s=strd, o=2)
                for q in range(parts):
                    np_ = P if q == 0 else 1
                    a_ = src[0:np_, q, :].rearrange("p (n o s) -> p n o s", n=nb, o=2)
                    d_ = dst[0:np_, q, :].rearrange("p (n o s) -> p n o s", n=nb, o=2)
                    t_ = vt_[0:np_, :].rearrange("p (n o s) -> p n o s", n=nb, o=2)
                    for o in range(2):
                        w0 = w[0:np_, :, :, o, 0] if up else w[0:np_, :, :, 0, o]
                        w1 = w[0:np_, :, :, o, 1] if up else w[0:np_, :, :, 1, o]
                        nc.gpsimd.tensor_tensor(d_[:, :, o, :], a_[:, :, 0, :], w0, ALU.mult)
                        link(nc.gpsimd.tensor_tensor(t_[:, :, o, :], a_[:, :, 1, :], w1, ALU.mult))
                        link(nc.gpsimd.tensor_tensor(d_[:, :, o, :], d_[:, :, o, :], t_[:, :, o, :], ALU.add))

            def load_stage(k):
                src = t["up_w"][k] if k < STG else t["down_w"][2 * STG - 1 - k]
                pool.dma_start(bw[:, k % 2, :], src.partition_broadcast(P)).then_inc(bw_loaded[k % 2], 16)

            def fly(k0, parts, up):
                load_stage(k0)
                load_stage(k0 + 1)
                src, dst = va_, vb_
                for k in range(k0, k0 + STG):
                    stage(k, 2 ** k if up else 2 ** (2 * STG - 1 - k), parts, src, dst, up)
                    if k + 2 < k0 + STG:
                        load_stage(k + 2)
                    src, dst = dst, src

            nc.gpsimd.memset(ones[:, :], 1.0)
            nc.gpsimd.memset(vb_[:, :, :], 0.0)
            nc.gpsimd.memset(zrow[:, :], 0.0)
            link(nc.gpsimd.memset(mhalf[:, :], -0.5))
            pool.dma_start(xs_dram[SPARE * P:(SPARE + 1) * P, :], zrow[:, :]).then_inc(spare_zeroed, 16)
            ln_rstd(0)
            ln_rstd(1)
            for g in range(NB):
                scatter(0, g)
                if g + 2 < NB:
                    ln_rstd(g + 2)
            pool.wait_ge(small_loaded, 16 * 12)
            fly(0, 2, True)
            nc.gpsimd.tensor_copy(wup[:, :], vb_[:, 0, :]).then_inc(fly_ready, 1)
            gather(0)
            ln_rstd(2 * NB)
            for g in range(NB):
                if g + 1 < NB:
                    ln_rstd(2 * NB + g + 1)
                scatter(1, g)
            pool.dma_start(va_[:, 0, :], t["w_conT"]).then_inc(wcon_loaded, 16)
            pool.wait_ge(wcon_loaded, 16)
            fly(STG, 1, False)
            pool.sem_inc(fly_ready, 1)
            nc.gpsimd.memset(va, 1.0).then_inc(att_const, 1)
            gather(1)
            for n in range(ATT_NORM[1], 6 * NB):
                ln_rstd(n)

        @block.tensor
        def _(pe):
            def mm(o, l, r, first=True, last=True):
                return nc.tensor.matmul(o, l, r, start=first, stop=last)

            def turn(n):
                pe.wait_ge(xn_ready, n + 1)
                if n >= 1:
                    pe.wait_ge(xnT_ready, n)
                for k in range(TPB):
                    ins = nc.tensor.transpose(ps[:, 7, k * P:(k + 1) * P], xn[:, n % NB, k, :], ident[:, :])
                ins.then_inc(xn_turned, 1)

            def logits(u, g, n0):
                rb = ROUTE_BANK[u]
                pe.wait_ge(xnT_ready, n0 + g + 1)
                if g >= 1:
                    pe.wait_ge(slots_ready, NB * u + g)
                for i in range(TPB):
                    ins = mm(ps[:, rb, E * i:E * i + E], xnT[:, (TPB * g + i) * P:(TPB * g + i + 1) * P], wr[:, :])
                ins.then_inc(logits_ready, 1)

            def ranks(u, g):
                rb = ROUTE_BANK[u]
                pe.wait_ge(ohb_ready, NB * u + g + 1)
                o2 = ohb[:, :, :].rearrange("p i e -> p (i e)")
                mm(ps[:, rb, 32:32 + TPB * E], before_b[:, :], o2)
                mm(ps[:, rb, 64:64 + TPB * E], ones_b[:, :], o2).then_inc(ranks_psum, 1)

            def moe(u, n0):
                t0, n1 = u * (NST + 1), u * NST

                def expert(j):
                    return pe.value_load(tabs[0:1, 0, bass.ds(j, 1)], min_val=0, max_val=E - 1)

                def turn_x(q):
                    nc.tensor.transpose(ps[:, 6, 0:P], xg[:, q, :], ident[:, :]).then_inc(xg_turned, 1)

                def gate_up(j, q, e):
                    pe.wait_ge(xt_ready, j + (t0 + 1))
                    mm(bank(q), xt[:, q, :], wg[:, bass.ds(e, 1), :].rearrange("p o f -> p (o f)")
                       ).then_inc(gate_ready, 1)
                    mm(bank(2 + q), xt[:, q, :], wu[:, bass.ds(e, 1), :].rearrange("p o f -> p (o f)")
                       ).then_inc(up_ready, 1)

                def turn_h(j, q):
                    pe.wait_ge(h_ready, j + (n1 + 1))
                    for f_ in range(FC):
                        ins = nc.tensor.transpose(ps[:, 4, f_ * P:(f_ + 1) * P],
                                                  hh[:, q, f_ * P:(f_ + 1) * P], ident[:, :])
                    ins.then_inc(h_turned, 1)

                def down(j, q, e):
                    pe.wait_ge(hT_ready, j + (n1 + 1))
                    pe.wait_ge(y_ready, j + (n1 + 1))
                    for f_ in range(FC):
                        ins = mm(ps[:, 5, 0:D], hT[:, q, f_ * P:(f_ + 1) * P],
                                 wd[:, bass.ds(e, 1), f_, :].rearrange("p o d -> p (o d)"), f_ == 0, f_ == FC - 1)
                    ins.then_inc(down_done, 1)

                def tile(j, q, last=False):
                    e_down = expert(j - 1)
                    if not last:
                        e_next = expert(j + 1)
                    if q == 1:
                        pe.wait_ge(xg_loaded[0], j * 8 + (8 + 16 * (LD0 * u + 1)))
                    else:
                        pe.wait_ge(xg_loaded[1], j * 8 + (8 + 16 * (LD1 * u + 1) - 8))
                    turn_x(1 - q)
                    down(j - 1, 1 - q, e_down)
                    turn_h(j, q)
                    if not last:
                        gate_up(j + 1, 1 - q, e_next)

                pe.wait_ge(moe_loaded, 48)
                pe.wait_ge(xg_loaded[0], 16 * (LD0 * u + 1))
                turn_x(0)
                gate_up(0, 0, expert(0))
                pe.wait_ge(xg_loaded[1], 16 * (LD1 * u + 1))
                turn_x(1)
                turn_h(0, 0)
                gate_up(1, 1, expert(1))
                with pe.Fori(1, NST - 2, 2) as i:
                    tile(i, 1)
                    tile(i + 1, 0)
                tile(NST - 2, 1)
                tile(NST - 1, 0, last=True)
                down(NST - 1, 0, expert(NST - 1))

            def fly_up():
                pe.wait_ge(fly_ready, 1)
                for c in range(HC):
                    ins = mm(ps[:, 7, c:c + 1], vb_[0:1, 1, c * P:(c + 1) * P], ones[0:1, 0:1])
                ins.then_inc(fly_turned, 1)
                pe.wait_ge(ffn_w_ready, 1)

            def fly_down():
                pe.wait_ge(fly_ready, 2)
                for c in range(HC):
                    ins = nc.tensor.transpose(ps[:, 7, c * P:(c + 1) * P], vb_[:, 0, c * P:(c + 1) * P], ident[:, :])
                ins.then_inc(fly_turned, 1)
                pe.wait_ge(ffn_w_ready, 2)

            def scan(n0):
                pe.wait_ge(scan_loaded, 16 * 6)
                pe.wait_ge(scan_vec_ready, 1)
                for k in range(TAPS):
                    for c in range(C2):
                        ins = mm(ps[:, k // 2, (k % 2) * DI:(k % 2 + 1) * DI], wxs[:, k, c, :], pwt[:, c, :],
                                 first=(c == 0), last=(c == C2 - 1))
                ins.then_inc(cw_psum, 1)
                pe.wait_ge(cw_ready, 1)
                pe.wait_ge(scan_vec_ready, 2)

                def convolved(b, c):
                    if c == 0:
                        pe.wait_ge(xnT_ready, n0 + b + 1)
                        if b >= 2:
                            pe.wait_ge(scan_used, b - 1)
                    elif b == 2:
                        pe.wait_ge(xnT_ready, n0 + NB)
                    elif b > 2:
                        pe.wait_ge(slots_ready, NB + b - 2)
                    for k in (3, 2, 1, 0):
                        d_ = TAPS - 1 - k
                        ins = nc.tensor.matmul(ps[:, 6 + c, d_:L], cw[:, k, c * P:(c + 1) * P],
                                               xnT[:, b * L:(b + 1) * L - d_], start=(k == 3), stop=(k == 0))
                    ins.then_inc(xc_psum, 1)

                def gate(b, c):
                    if c == 0:
                        pe.wait_ge(xc_ready, 2 * b + 1)
                    else:
                        pe.wait_ge(sz_ready, 2 * b + 1)
                    mm(bank(6), wz[:, c * P:(c + 1) * P], xnT[:, b * L:(b + 1) * L]).then_inc(z_psum, 1)

                def projected(b):
                    pe.wait_ge(xc_ready, 2 * b + 2)
                    pe.wait_ge(sz_ready, 2 * b + 2)
                    for c in range(C2):
                        ins = mm(ps[0:96, 6, :], wx3[:, c, :], xc[:, b % 2, c, :], first=(c == 0), last=(c == 1))
                    ins.then_inc(xd_psum, 1)

                def delta(b, c):
                    if c == 0:
                        pe.wait_ge(xd_act, 4 * b + 3)
                        pe.wait_ge(xd_vec, 2 * b + 1)
                    else:
                        pe.wait_ge(dt_taken, 2 * b + 1)
                    mm(bank(6), wdt[:, c * P:(c + 1) * P], xdf[0:R, :]).then_inc(dt_psum, 1)

                def b_rows(t_):
                    b, j = divmod(t_, NS // 2)
                    if j == 0:
                        pe.wait_ge(xs_ready, b + 1)
                    if t_:
                        pe.wait_ge(b_used, 2 * t_)
                    for q in range(2):
                        ins = mm(bank(2 + q), selb[0:96, 2 * j + q, :], xsb[0:96, b % 2, :])
                    ins.then_inc(b_psum, 1)

                def c_rows(t_):
                    b, j = divmod(t_, NS // 2)
                    if t_:
                        pe.wait_ge(hc_ready, 2 * t_)
                    for q in range(2):
                        ins = mm(bank(4 + q), selb[0:96, NS + 2 * j + q, :], xsb[0:96, b % 2, :])
                    ins.then_inc(c_psum, 1)

                def ysum(b, j):
                    for c in range(C2):
                        pe.wait_ge(hc_ready, 8 * b + 2 * j + c + 1)
                        for q in range(2):
                            ins = mm(bank(c), ident[:, :], hs[:, c, 2 * j + q, :], first=False,
                                     last=(j == NS // 2 - 1 and q == 1))
                        if j == NS // 2 - 1:
                            ins.then_inc(ysum_ready, 1)

                turn(n0)
                for c in range(C2):
                    convolved(0, c)
                gate(0, 0)
                gate(0, 1)
                projected(0)
                delta(0, 0)
                delta(0, 1)
                turn(n0 + 1)
                b_rows(0)
                c_rows(0)
                for b in range(NB):
                    f_ = b + 1
                    if b >= 1:
                        pe.wait_ge(yz_ready, 2 * b)
                    for c in range(C2):
                        mm(bank(c), diagD[:, c, :], xc[:, b % 2, c, :], first=True, last=False)
                    for j in range(NS // 2):
                        t_ = b * (NS // 2) + j
                        if f_ < NB:
                            if j == 0:
                                convolved(f_, 0)
                            if j == 1:
                                gate(f_, 0)
                            if j == 2:
                                delta(f_, 0)
                        if j == 3 and b == 0:
                            turn(n0 + 3)
                        if j == 3 and b >= 1:
                            ranks(1, b - 1)
                        if t_ + 1 < NB * (NS // 2):
                            b_rows(t_ + 1)
                        if j == 0 and f_ < NB:
                            convolved(f_, 1)
                        if j == 1:
                            if f_ < NB:
                                gate(f_, 1)
                                pe.wait_ge(xc_ready, 2 * f_ + 2)
                            else:
                                pe.wait_ge(slots_ready, NB + b - 1)
                            turn(n0 + 2 if b == 0 else n0 + NB + b - 1)
                            if f_ < NB:
                                projected(f_)
                        if j == 2:
                            if f_ < NB:
                                delta(f_, 1)
                            if b >= 1:
                                logits(1, b - 1, n0 + NB)
                        ysum(b, j)
                        if t_ + 1 < NB * (NS // 2):
                            c_rows(t_ + 1)
                    pe.wait_ge(yz_ready, 2 * b + 2)
                    if f_ < NB:
                        pe.wait_ge(dt_taken, 2 * f_ + 2)
                    else:
                        pe.wait_ge(scan_used, NB - 1)
                    for k in range(TPB):
                        for c in range(C2):
                            ins = mm(ps[:, 6, k * P:(k + 1) * P], yz[:, c, k * P:(k + 1) * P], wout[:, c, :],
                                     first=(c == 0), last=(c == 1))
                    ins.then_inc(o_psum, 1)
                pe.wait_ge(slots_ready, 2 * NB - 1)
                turn(n0 + 2 * NB - 1)
                logits(1, NB - 1, n0 + NB)
                ranks(1, NB - 1)

            def ffn(u, b, norm_, pieces=range(2 * TPB)):
                n = u * NB + b
                for c in pieces:
                    if c == 0:
                        pe.wait_ge(xnT_ready, norm_ + 1)
                    if c < HC:
                        if n * HC + c >= 2:
                            pe.wait_ge(ff_g_ready, n * HC + c - 1)
                        mm(bank(c % 2), wup[:, c * P:(c + 1) * P], xnT[:, b * L:(b + 1) * L]).then_inc(ff_h_psum, 1)
                        continue
                    if c == HC:
                        pe.wait_ge(ff_g_ready, n * HC + HC)
                        if b == 3:
                            pe.wait_ge(ff_o_used, n - 2)
                    k = c - HC
                    o_ = ps[:, FFN_BANK[n], k * P:(k + 1) * P]
                    mm(o_, ones[0:1, :], ffbr[0:1, 2, :], True, False)
                    for h in range(HC):
                        ins = mm(o_, gT[:, b % 2, h, k * P:(k + 1) * P], wdn[:, h, :], False, h == HC - 1)
                    if k == TPB - 1:
                        ins.then_inc(ff_o_psum, 1)

            def attend(n0):

                def project(b, piece):
                    xb_ = xnT[:, b * L:(b + 1) * L]
                    if piece == 0:
                        pe.wait_ge(xnT_ready, ATT_NORM[b] + 1)
                        if b >= 1:
                            pe.wait_ge(max_used, NMS * b)
                        mm(bank(5), wq[:, 0, :], xb_).then_inc(qkv_psum, 1)
                        mm(bank(6), wq[:, 1, :], xb_).then_inc(qkv_psum, 1)
                    if piece == 1:
                        if b >= 1:
                            pe.wait_ge(m_copied, b)
                        mm(bank(7), wq[:, 2, :], xb_).then_inc(qkv_psum, 1)
                        pe.wait_ge(qkv_used, 5 * b + 1)
                        mm(bank(5), wq[:, 3, :], xb_).then_inc(qkv_psum, 1)
                    if piece == 2:
                        pe.wait_ge(qkv_used, 5 * b + 2)
                        for k in range(TPB):
                            o_ = ps[:, 6, k * P:(k + 1) * P]
                            mm(o_, ones[0:1, :], abr[0:1, 0, :], True, False)
                            ins = mm(o_, xb_[:, k * P:(k + 1) * P], wv, False, True)
                        ins.then_inc(qkv_psum, 1)

                def maxima(b, steps_):
                    q = b % 2
                    for j in steps_:
                        qt, h0, nh = MAXSTEPS[j]
                        n = b * NMS + j
                        if j == 0:
                            pe.wait_ge(qk_loaded, 16 * 12 * (b + 1))
                            pe.wait_ge(qkv_used, 5 * b + 5)
                        if n >= 2:
                            pe.wait_ge(max_used, n - 1)
                        w_ = P * (qt + 1)
                        for h in range(h0, h0 + nh):
                            c_ = (h - h0) * w_
                            mm(ps[:, 5 + j % 2, c_:c_ + w_], qs[0:KP, q, h, qt * P:(qt + 1) * P],
                               ks[0:KP, q, h, 0:w_], True, False)
                            ins = mm(ps[:, 5 + j % 2, c_ + qt * P:c_ + w_], ident_b[:, :], maskb[:, 0, :],
                                     False, True)
                        ins.then_inc(max_psum, 1)

                def turn_max(b):
                    pe.wait_ge(max_used, NMS * (b + 1))
                    if b == 0:
                        pe.wait_ge(xnT_ready, n0 + NB)
                    if b >= 2:
                        pe.wait_ge(xnT_ready, n0 + NB + b - 1)
                    mt_ = ps[0:NH, 7, 0:L // 2].bitcast(BF16)
                    for k in range(TPB):
                        ins = nc.tensor.transpose(mt_[:, k * P:(k + 1) * P], nm[:, k, :], ident_b[:, :])
                    ins.then_inc(m_turned, 1)

                def scores(n, k):
                    b, q, h = n // NG, n // NG % 2, GH * (n % NG) + k
                    if n % NG == 0 and k == 0:
                        pe.wait_ge(m_loaded, 16 * (b + 1))
                    i = GH * n + k
                    if i:
                        pe.wait_ge(p_ready, 2 * i - 1)
                    s_ = ps[:, 0:3, :].rearrange("p k f -> p (k f)")
                    for kt in range(TPB):
                        if kt == 1 and i:
                            pe.wait_ge(p_ready, 2 * i)
                        w_ = L - kt * P
                        mm(s_[:, SEG[kt]:SEG[kt] + w_], ks[0:KR, q, h, kt * P:(kt + 1) * P],
                           qs[0:KR, q, h, kt * P:L], True, False)
                        ins = mm(s_[:, SEG[kt]:SEG[kt] + P], ident_b[:, :], maskb[:, 1, :], False, True)
                        if kt in (0, TPB - 1):
                            ins.then_inc(s_psum, 1)

                def values(n, k, part):
                    b, q, g = n // NG, n // NG % 2, n % NG
                    if k == 0 and part == 0:
                        pe.wait_ge(p_ready, 2 * GH * (n + 1))
                        pe.wait_ge(v_ready, b + 1)
                        if n >= 1:
                            pe.wait_ge(o_copied, n)
                    steps_ = VALUE_STEPS[k]
                    half = (len(steps_) + 1) // 2
                    for kt, j in (steps_[half:] if part else steps_[:half]):
                        w_ = L - kt * P
                        ins = nc.tensor.matmul(ps[32 * j:32 * j + 32, 3, kt * P:L], va[:, q, kt, GH * g + j, :],
                                               pt[:, n % 2, j, SEG[kt]:SEG[kt] + w_],
                                               start=(kt == 0), stop=(kt == TPB - 1))
                    if k == GH - 1 and part == 1:
                        ins.then_inc(pv_psum, 1)

                def turn_o(n):
                    pe.wait_ge(o_copied, n + 1)
                    if n >= 1:
                        pe.wait_ge(on_ready, n)
                    if n >= NG:
                        pe.wait_ge(ao_used, n // NG)
                    for k in range(TPB):
                        ins = nc.tensor.transpose(ps[:, 4, k * P:(k + 1) * P], ob[:, k * P:(k + 1) * P], ident[:, :])
                    ins.then_inc(o_turned, 1)

                def turn_on(b):
                    pe.wait_ge(on_ready, NG * (b + 1))
                    for k in range(TPB):
                        ins = nc.tensor.transpose(ps[:, 4, k * P:(k + 1) * P], on[:, k, :], ident[:, :])
                    ins.then_inc(on_turned, 1)

                def output(b):
                    pe.wait_ge(onT_ready, b + 1)
                    for k in range(TPB):
                        o_ = ps[:, 4, k * P:(k + 1) * P]
                        mm(o_, ones[0:1, :], abr[0:1, 1, :], True, False)
                        ins = mm(o_, onT[:, k * P:(k + 1) * P], wo, False, True)
                    ins.then_inc(ao_psum, 1)

                for b in range(2):
                    turn(FFN_NORM[b])
                    ffn(0, b, FFN_NORM[b])
                turn(ATT_NORM[0])
                pe.wait_ge(att_loaded, 16 * 7)
                pe.wait_ge(att_const, 2)
                for piece in range(3):
                    project(0, piece)
                pe.wait_ge(qkv_used, 3)
                turn(FFN_NORM[2])
                ffn(0, 2, FFN_NORM[2])
                turn(ATT_NORM[1])
                turn(FFN_NORM[3])
                for c in range(HC + TPB):
                    ffn(0, 3, FFN_NORM[3], range(c, c + 1))
                    if c == 1:
                        turn(ATT_NORM[2])
                    if c >= 1:
                        maxima(0, range(2 * c - 2, 2 * c))
                maxima(0, range(2 * (HC + TPB - 1), NMS // 2))
                turn(ATT_NORM[3])
                maxima(0, range(NMS // 2, NMS))
                turn_max(0)
                project(1, 0)
                project(1, 1)
                pe.wait_ge(ones_loaded, 16 * 2)
                for n in range(NB * NG + 1):
                    b, g = divmod(n, NG)
                    for k in range(GH):
                        if n < NB * NG:
                            scores(n, k)
                        if k == 0 and n >= 2:
                            turn_o(n - 2)
                        ms = max_steps(g, k) if b + 1 < NB else range(0)
                        for part in range(2):
                            maxima(b + 1, ms[2 * part:2 * part + 2])
                            if n >= 1:
                                values(n - 1, k, part)
                        maxima(b + 1, ms[4:])
                        if g == 3 and b + 1 < NB and k == 2:
                            turn_max(b + 1)
                        if g == 3 and b + 2 < NB and k >= 2:
                            project(b + 2, k - 2)
                        if g == 1 and b + 1 < NB and k == 0:
                            project(b + 1, 2)
                        if g == 1 and b >= 1:
                            if k == 1:
                                turn_on(b - 1)
                            if k == 3:
                                output(b - 1)
                        if g == 2 and b >= 1 and k == 1:
                            pe.wait_ge(m_copied, min(b + 1, NB))
                            if b + 1 < NB:
                                pe.wait_ge(qkv_used, 5 * b + 8)
                            turn(n0 + NB + b - 1)
                ffn(1, 0, 5 * NB, range(1))
                turn_o(NB * NG - 1)
                ffn(1, 0, 5 * NB, range(1, HC + TPB))
                turn_on(NB - 1)
                ffn(1, 1, 5 * NB + 1, range(2))
                output(NB - 1)
                ffn(1, 1, 5 * NB + 1, range(2, HC + TPB))
                turn(6 * NB - 1)
                ffn(1, 2, 5 * NB + 2)
                ffn(1, 3, 5 * NB + 3)

            pe.wait_ge(const_loaded, 16 * 8)
            pe.wait_ge(ident_ready, 1)
            for g in range(NB):
                turn(g)
                logits(0, g, 0)
                ranks(0, g)
            moe(0, 0)
            fly_up()
            scan(NB)
            moe(1, 2 * NB)
            fly_down()
            attend(4 * NB)

        @block.scalar
        def _(act):
            chain = [0]

            def link(ins):
                chain[0] += 1
                ins.then_inc(act_chain, 1)
                act.wait_ge(act_chain, chain[0])

            def take_turned(n, g):
                act.wait_ge(xn_turned, n + 1)
                nc.scalar.copy(xnT[:, g * L:(g + 1) * L], bank(7)).then_inc(xnT_ready, 1)

            def moe(u, n0):
                if u == 0:
                    for g in range(NB):
                        take_turned(n0 + g, g)
                act.wait_ge(pads_ready, u + 1)
                nc.scalar.activation(egate[:, :], dm[:, :], ACT.Exp).then_inc(egate_ready, 1)
                nc.scalar.preload_act_table(ACT.Silu)
                t0, n1 = u * (NST + 1), u * NST

                def copy_x(j, q):
                    act.wait_ge(xg_turned, j + (t0 + 1))
                    nc.scalar.copy(xt[:, q, :], ps[:, 6, 0:P]).then_inc(xt_ready, 1)

                def tile(j, q):
                    act.wait_ge(gate_ready, j + (n1 + 1))
                    nc.scalar.activation(sil[:, q, :], bank(q), ACT.Silu).then_inc(sil_ready, 1)
                    copy_x(j + 1, 1 - q)
                    act.wait_ge(h_turned, j + (n1 + 1))
                    nc.scalar.copy(hT[:, q, :], bank(4)).then_inc(hT_ready, 1)

                copy_x(0, 0)
                tile(0, 0)
                with act.Fori(1, NST, 2) as i:
                    tile(i, 1)
                    tile(i + 1, 0)

            def scan(n0):
                act.wait_ge(cw_psum, 1)
                nc.scalar.copy(cw.rearrange("p k o -> p (k o)"),
                               ps[:, 0:2, :].rearrange("p k f -> p (k f)")).then_inc(cw_ready, 1)

                def silus(b):
                    for c in range(C2):
                        act.wait_ge(xc_psum, 2 * b + c + 1)
                        nc.scalar.activation(xc[:, b % 2, c, :], bank(6 + c), ACT.Silu,
                                             bias=cbias[:, c:c + 1]).then_inc(xc_ready, 1)
                    for c in range(C2):
                        act.wait_ge(z_psum, 2 * b + c + 1)
                        nc.scalar.activation(sz[:, b % 2, c, :], bank(6), ACT.Silu).then_inc(sz_ready, 1)

                def high_middle(b):
                    act.wait_ge(xd_psum, b + 1)
                    nc.scalar.copy(xdf[0:R, :], ps[0:R, 6, :]).then_inc(xd_act, 1)
                    nc.scalar.copy(hib[0:96, :], ps[0:96, 6, :]).then_inc(xd_act, 1)
                    nc.scalar.copy(xsb[0:32, b % 2, :], ps[0:32, 6, :]).then_inc(xd_act, 1)
                    act.wait_ge(xd_vec, 2 * b + 1)
                    nc.scalar.copy(mib[0:96, :], r1[0:96, :])
                    nc.scalar.copy(xsb[32:64, b % 2, :], r1[32:64, :]).then_inc(xd_act, 1)

                def low(b):
                    act.wait_ge(xd_vec, 2 * b + 2)
                    nc.scalar.copy(xsb[64:96, b % 2, :], r1[64:96, :]).then_inc(xs_ready, 1)

                def softplus(b):
                    for c in range(C2):
                        act.wait_ge(dt_psum, 2 * b + c + 1)
                        if b >= 1:
                            act.wait_ge(delta_ready, 2 * b)
                        nc.scalar.activation(xb[:, c, :], bank(6), ACT.Identity, bias=bdt[:, c:c + 1])
                        nc.scalar.activation(eb[:, c, :], bank(6), ACT.Abs, bias=bdt[:, c:c + 1]).then_inc(dt_taken, 1)

                def softplus_log(b):
                    act.wait_ge(dt_taken, 2 * b + 2)
                    link(nc.scalar.activation(eb, eb, ACT.Exp, scale=-1.0))
                    nc.scalar.activation(eb, eb, ACT.Ln, bias=1.0).then_inc(sp_ready, 1)

                def decay(b, j):
                    t_ = b * (NS // 2) + j
                    if t_ >= 3:
                        act.wait_ge(hc_ready, 2 * (t_ - 2))
                    for c in range(C2):
                        act.wait_ge(delta_ready, 2 * b + c + 1)
                        for q in range(2):
                            n = 2 * j + q
                            ins = nc.scalar.activation(dA[:, c, 2 * (t_ % 3) + q, 1:L], dl[:, b % 2, c, 1:L], ACT.Exp,
                                                       scale=a_neg[:, c, n:n + 1])
                        ins.then_inc(dA_ready, 1)

                take_turned(n0, 0)
                silus(0)
                high_middle(0)
                softplus(0)
                low(0)
                softplus_log(0)
                take_turned(n0 + 1, 1)
                for b in range(NB):
                    decay(b, 0)
                    decay(b, 1)
                    decay(b, 2)
                    if b + 1 < NB:
                        silus(b + 1)
                    if b == 0:
                        take_turned(n0 + 2, 2)
                    else:
                        take_turned(n0 + NB + b - 1, b - 1)
                    if b + 1 < NB:
                        high_middle(b + 1)
                    decay(b, 3)
                    if b + 1 < NB:
                        softplus(b + 1)
                        low(b + 1)
                        softplus_log(b + 1)
                    if b == 0:
                        take_turned(n0 + 3, 3)
                take_turned(n0 + 2 * NB - 1, NB - 1)

            def ffn(u, b):
                n = u * NB + b
                for c in range(HC):
                    act.wait_ge(ff_h_psum, n * HC + c + 1)
                    if n >= 2:
                        act.wait_ge(ff_o_psum, n - 1)
                    nc.scalar.activation(gT[:, b % 2, c, :], bank(c % 2), ACT.Gelu,
                                         bias=bup[:, c:c + 1]).then_inc(ff_g_ready, 1)

            def attend(n0):
                def high(b):
                    act.wait_ge(rope_ready, 2 * b + 2)
                    if b >= 1:
                        act.wait_ge(parts_stored, 16 * b)
                    nc.scalar.copy(spl[:, 0, :, :], qk).then_inc(part_act, 1)

                def middle(b):
                    act.wait_ge(part_vec, 2 * b + 1)
                    nc.scalar.copy(spl[:, 1, :, :], q1).then_inc(part_act, 1)

                def copy_max(b):
                    act.wait_ge(m_turned, b + 1)
                    if b >= 1:
                        act.wait_ge(m_stored, 16 * b)
                    nc.scalar.copy(mTs[0:NH, :], ps[0:NH, 7, 0:L // 2].bitcast(BF16)).then_inc(m_copied, 1)

                for b in range(2):
                    take_turned(FFN_NORM[b], b)
                    ffn(0, b)
                take_turned(ATT_NORM[0], 0)
                high(0)
                middle(0)
                take_turned(FFN_NORM[2], 2)
                ffn(0, 2)
                take_turned(ATT_NORM[1], 1)
                take_turned(FFN_NORM[3], 3)
                ffn(0, 3)
                nc.scalar.preload_act_table(ACT.Exp)
                take_turned(ATT_NORM[2], 2)
                take_turned(ATT_NORM[3], 3)
                copy_max(0)
                s_ = ps[:, 0:3, :].rearrange("p k f -> p (k f)")
                for n in range(NB * NG + 1):
                    b, g = divmod(n, NG)
                    for k in range(GH):
                        if n < NB * NG:
                            if n >= 2:
                                act.wait_ge(pv_psum, n - 1)
                            for h_, (c0, c1) in enumerate(((0, L), (L, PTW))):
                                act.wait_ge(s_psum, 2 * (GH * n + k) + h_ + 1)
                                nc.scalar.activation(pt[:, n % 2, k, c0:c1], s_[:, c0:c1], ACT.Exp,
                                                     scale=float(HD) ** -0.5).then_inc(p_ready, 1)
                        if g == 0 and b + 1 < NB and k == 0:
                            high(b + 1)
                        if g == 0 and b + 1 < NB and k == 1:
                            middle(b + 1)
                        if g == 1 and b >= 1 and k == 1:
                            act.wait_ge(on_turned, b)
                            nc.scalar.copy(onT, bank(4)).then_inc(onT_ready, 1)
                        if g == 2 and b >= 1 and k == 1:
                            take_turned(n0 + NB + b - 1, b - 1)
                        if g == 3 and b + 1 < NB and k == 2:
                            copy_max(b + 1)
                    if n >= 1:
                        act.wait_ge(pv_psum, n)
                        if n >= 2:
                            act.wait_ge(o_turned, n - 1)
                        nc.scalar.copy(ob, bank(3)).then_inc(o_copied, 1)
                ffn(1, 0)
                act.wait_ge(on_turned, NB)
                nc.scalar.copy(onT, bank(4)).then_inc(onT_ready, 1)
                ffn(1, 1)
                take_turned(6 * NB - 1, NB - 1)
                ffn(1, 2)
                ffn(1, 3)

            moe(0, 0)
            act.wait_ge(small_loaded, 16 * 12)
            nc.scalar.activation(a_neg[:, :, :], a_neg[:, :, :], ACT.Exp).then_inc(aexp_ready, 1)
            scan(NB)
            moe(1, 2 * NB)
            attend(4 * NB)

        @block.vector
        def _(dve):
            chain = [0]
            v = nc.vector

            def link(ins):
                chain[0] += 1
                ins.then_inc(vec_chain, 1)
                dve.wait_ge(vec_chain, chain[0])

            def stats(n, g):
                q = n % 2
                for k in range(TPB):
                    ins = v.bn_stats(st[:, q, k, :], x[:, TPB * g + k, :])
                link(ins)
                for k in range(TPB):
                    ins = v.bn_aggr(mv[:, q, k, :], st[:, q, k, :])
                ins.then_inc(ln_stats_ready, 1)

            def normalise(n, g):
                q = n % 2
                dve.wait_ge(ln_rstd_ready, n + 1)
                if n >= NB:
                    dve.wait_ge(xn_turned, n - NB + 1)
                for k in range(TPB):
                    ins = v.tensor_scalar(xn[:, n % NB, k, :], x[:, TPB * g + k, :], mv[:, q, k, 0:1], rs[:, q, k:k + 1],
                                          ALU.subtract, ALU.mult)
                ins.then_inc(xn_ready, 1)

            def norm(n, g):
                stats(n, g)
                normalise(n, g)

            def wide(a, n=E):
                return a.unsqueeze(2).to_broadcast([P, TPB, n])

            def pick(k, scores):
                r8w = r8[:, :].unsqueeze(1).to_broadcast([P, TPB, E])
                link(v.tensor_reduce(red[:, k, :], scores, AX.X, ALU.max))
                link(v.tensor_tensor(oh[:, k, :, :], scores, wide(red[:, k, :]), ALU.is_equal))
                link(v.tensor_tensor(oh[:, k, :, :], oh[:, k, :, :], r8w, ALU.mult))
                link(v.tensor_reduce(red[:, 2 + k, :], oh[:, k, :, :], AX.X, ALU.max))
                link(v.tensor_tensor(oh[:, k, :, :], oh[:, k, :, :], wide(red[:, 2 + k, :]), ALU.is_equal))

            def choose(u, g):
                gt = slice(TPB * g, TPB * (g + 1))
                rb = ROUTE_BANK[u]
                dve.wait_ge(logits_ready, NB * u + g + 1)
                link(v.tensor_copy(lg[:, :, :], ps[:, rb, 0:TPB * E].rearrange("p (i e) -> p i e", e=E)))
                pick(0, lg[:, :, :])
                link(v.scalar_tensor_tensor(lg[:, :, :], oh[:, 0, :, :], -3.0e38, lg[:, :, :], ALU.mult, ALU.add))
                pick(1, lg[:, :, :])
                v.tensor_tensor(ohb[:, :, :], oh[:, 0, :, :], oh[:, 1, :, :], ALU.add).then_inc(ohb_ready, 1)
                v.tensor_tensor(dm[:, gt], red[:, 1, :], red[:, 0, :], ALU.subtract)

            def place(u, g):
                gt = slice(TPB * g, TPB * (g + 1))
                rb = ROUTE_BANK[u]
                if g == 0:
                    link(v.tensor_copy(cum[:, :], base8[:, :]))
                link(v.tensor_copy(cs4[:, :, 0], cum[:, :]))
                dve.wait_ge(ranks_psum, NB * u + g + 1)
                tot = ps[:, rb, 64:64 + TPB * E].rearrange("p (i e) -> p e i", e=E)
                link(v.tensor_copy(cs4[:, :, 1:TPB], tot[:, :, 0:TPB - 1]))
                flat = "p e i -> p (e i)"
                link(v.tensor_tensor_scan(pre4[:, :, :].rearrange(flat), first4[:, :, :].rearrange(flat),
                                          cs4[:, :, :].rearrange(flat), 0.0, ALU.mult, ALU.add))
                v.tensor_tensor(cum[:, :], pre4[:, :, TPB - 1], tot[:, :, TPB - 1], ALU.add)
                link(v.tensor_tensor(sl[:, :, :], pre4[:, :, :].rearrange("p e i -> p i e"),
                                     ps[:, rb, 32:32 + TPB * E].rearrange("p (i e) -> p i e", e=E), ALU.add))
                for k in range(2):
                    link(v.tensor_tensor(oh[:, k, :, :], oh[:, k, :, :], sl[:, :, :], ALU.mult))
                with nc.allow_low_precision(reason="slots are whole numbers below 2**24: exact"):
                    v.tensor_reduce(slots[:, 0, gt], oh[:, 0, :, :], AX.X, ALU.add)
                    v.tensor_reduce(slots[:, 1, gt], oh[:, 1, :, :], AX.X, ALU.add).then_inc(slots_ready, 1)

            def tables(u):
                v.tensor_copy(pads[:, :], cum[:, :]).then_inc(pads_ready, 1)
                dve.wait_ge(pads_ready, u + 1)
                c_ = [cnt[:, k, :] for k in range(4)]
                link(v.tensor_copy(slotf[:, :], slots[:, :, :].rearrange("p k i -> p (k i)")))
                link(v.memset(shift[:, :], 0.0))
                link(v.tensor_tensor(c_[0], cum[:, :], base8[:, :], ALU.subtract))
                link(v.tensor_tensor(cmp[:, :, :], c_[0].unsqueeze(2).to_broadcast([P, E, CT - 1]), steps[:, :, :],
                                     ALU.is_gt))
                link(v.tensor_reduce(c_[1], cmp[:, :, :], AX.X, ALU.add))
                link(v.tensor_tensor_scan(c_[2], ones[:, 0:E], c_[1], 0.0, ALU.mult, ALU.add))
                wide_ = [1, NST + 3, E]
                link(v.tensor_tensor(tmsk[:, 0, :, :], tnum[:, :, :], c_[2][0:1, :].unsqueeze(1).to_broadcast(wide_),
                                     ALU.is_ge))
                link(v.tensor_tensor(tmsk[:, 1, :, :], tmsk[:, 0, :, :], c_[1][0:1, :].unsqueeze(1).to_broadcast(wide_),
                                     ALU.mult))
                link(v.tensor_reduce(trow[:, 0, :], tmsk[:, 0, :, :], AX.X, ALU.add))
                link(v.tensor_reduce(trow[:, 1, :], tmsk[:, 1, :, :], AX.X, ALU.add))
                link(v.tensor_scalar(tabs[:, 0, :], trow[:, 0, :], float(E - 1), None, ALU.min))
                link(v.tensor_tensor(trow[:, 1, :], tnum[:, :, 0], trow[:, 1, :], ALU.subtract))
                link(v.scalar_tensor_tensor(trow[:, 2, :], trow[:, 0, :], float(CT), trow[:, 1, :],
                                            ALU.mult, ALU.add))
                v.tensor_scalar(tabs[:, 1, :], trow[:, 2, :], float(SPARE), None, ALU.min).then_inc(tables_ready, 1)
                link(v.tensor_scalar(shift[:, 1:E], c_[1][:, 0:E - 1], float(P), float(-CT * P), ALU.mult, ALU.add))
                wide_ = [P, 2 * NT, E]
                link(v.tensor_tensor(rmsk[:, :, :], slotf[:, :].unsqueeze(2).to_broadcast(wide_),
                                     base8[:, :].unsqueeze(1).to_broadcast(wide_), ALU.is_ge))
                link(v.tensor_tensor(rmsk[:, :, :], rmsk[:, :, :], shift[:, :].unsqueeze(1).to_broadcast(wide_),
                                     ALU.mult))
                link(v.tensor_reduce(rfix[:, :], rmsk[:, :, :], AX.X, ALU.add))
                v.tensor_tensor(dense[:, :], slotf[:, :], rfix[:, :], ALU.add).then_inc(dense_ready, 1)

            def moe(u, n0):
                t0, n1 = u * (NST + 1), u * NST

                def act_product(j, q):
                    dve.wait_ge(sil_ready, j + (n1 + 1))
                    dve.wait_ge(up_ready, j + (n1 + 1))
                    v.tensor_tensor(hh[:, q, :], sil[:, q, :], bank(2 + q), ALU.mult).then_inc(h_ready, 1)

                def result(j, q, stored):
                    dve.wait_ge(down_done, j + (n1 + 1))
                    dve.wait_ge(y_stored[q], stored)
                    v.tensor_copy(yt[:, q, :], ps[:, 5, 0:D]).then_inc(y_ready, 1)

                act_product(0, 0)
                with dve.Fori(1, NST, 2) as i:
                    act_product(i, 1)
                    result(i - 1, 0, i * 8 + (8 + 16 * ST0 * u))
                    act_product(i + 1, 0)
                    result(i, 1, i * 8 + (8 + 16 * ST1 * u))
                result(NST - 1, 0, 16 * (ST0 * u + NST // 2 + 1))

                dve.wait_ge(egate_ready, u + 1)
                link(v.tensor_scalar(gsum[:, :], egate[:, :], 1.0, None, ALU.add))
                link(v.reciprocal(gsum[:, :], gsum[:, :]))
                link(v.tensor_scalar(gates[:, 0, :], gsum[:, :], 0.5, None, ALU.mult))
                link(v.tensor_tensor(gates[:, 1, :], gates[:, 0, :], egate[:, :], ALU.mult))

            def combine(u, g):
                dve.wait_ge(yg_loaded[g % 2], 16 * 2 * TPB * (2 * u + g // 2 + 1))
                for k in range(2):
                    for i in range(TPB):
                        xi = x[:, TPB * g + i, :]
                        ins = v.scalar_tensor_tensor(xi, yg[:, g % 2, k, i, :],
                                                     gates[:, k, TPB * g + i:TPB * g + i + 1], xi,
                                                     ALU.mult, ALU.add)
                    if k == 0:
                        link(ins)
                ins.then_inc(combined, 1)
                dve.wait_ge(combined, NB * u + g + 1)

            def fly_up():
                dve.wait_ge(small_loaded, 16 * 12)
                dve.wait_ge(fly_turned, 1)
                v.tensor_tensor(ffbr[:, 2, :], ffbr[:, 0, :], ffbr[:, 1, :], ALU.add)
                v.tensor_tensor(bup[:, :], ps[:, 7, 0:HC], ubias[:, :], ALU.add).then_inc(ffn_w_ready, 1)

            def fly_down():
                dve.wait_ge(fly_turned, 2)
                v.tensor_copy(wdn[:, :, :].rearrange("p c d -> p (c d)"), bank(7)).then_inc(ffn_w_ready, 1)

            def scan(n0):
                dve.wait_ge(aexp_ready, 1)
                link(v.tensor_scalar(a_neg[:, :, :], a_neg[:, :, :], -1.0, None, ALU.mult))
                dve.wait_ge(scan_loaded, 16 * 6)
                for k in range(TAPS):
                    for c in range(C2):
                        ins = v.tensor_scalar(wxs[:, k, c, :], wxT[:, c, :], dwc[:, c, k:k + 1], None, ALU.mult)
                ins.then_inc(scan_vec_ready, 1)
                for c in range(C2):
                    v.tensor_scalar(diagD[:, c, :], ident[:, :], dcol[:, c:c + 1], None, ALU.mult)
                    link(v.memset(dA[:, c, :, 0:1], 0.0))
                v.tensor_copy(selb[0:96, :, :], self_[0:96]).then_inc(scan_vec_ready, 1)

                def rest(b):
                    dve.wait_ge(xd_act, 4 * b + 3)
                    v.tensor_tensor(r1[0:96, :], ps[0:96, 6, :], hib[0:96, :], ALU.subtract).then_inc(xd_vec, 1)

                def rest2(b):
                    dve.wait_ge(xd_vec, 2 * b + 1)
                    dve.wait_ge(xd_act, 4 * b + 4)
                    v.tensor_tensor(r1[0:96, :], r1[0:96, :], mib[0:96, :], ALU.subtract).then_inc(xd_vec, 1)

                def delta_u(b, c):
                    dve.wait_ge(sp_ready, b + 1)
                    v.scalar_tensor_tensor(dl[:, b % 2, c, :], xb[:, c, :], 0.0, eb[:, c, :], ALU.max, ALU.add).then_inc(delta_ready, 1)
                    dve.wait_ge(delta_ready, 2 * b + c + 1)
                    dve.wait_ge(xc_ready, 2 * b + c + 1)
                    link(v.tensor_tensor(uu[:, b % 2, c, :], dl[:, b % 2, c, :], xc[:, b % 2, c, :], ALU.mult))

                def inputs(b, j):
                    dve.wait_ge(b_psum, 4 * b + j + 1)
                    for c in range(C2):
                        v.tensor_tensor(hs[:, c, 2 * j:2 * j + 2, :],
                                        uu[:, b % 2, c, :].unsqueeze(1).to_broadcast([P, 2, L]),
                                        ps[:, 2:4, :], ALU.mult).then_inc(b_used, 1)

                def states(b, j):
                    for c in range(C2):
                        dve.wait_ge(b_used, 8 * b + 2 * j + c + 1)
                        dve.wait_ge(dA_ready, 8 * b + 2 * j + c + 1)
                        h_ = hs[:, c, 2 * j:2 * j + 2, :].rearrange("p n l -> p (n l)")
                        t_ = 4 * b + j
                        a_ = dA[:, c, 2 * (t_ % 3):2 * (t_ % 3) + 2, :].rearrange("p n l -> p (n l)")
                        link(v.tensor_tensor_scan(h_, a_, h_, 0.0, ALU.mult, ALU.add))
                    dve.wait_ge(c_psum, 4 * b + j + 1)
                    for c in range(C2):
                        v.tensor_tensor(hs[:, c, 2 * j:2 * j + 2, :], hs[:, c, 2 * j:2 * j + 2, :], ps[:, 4:6, :],
                                        ALU.mult).then_inc(hc_ready, 1)

                for g in range(2):
                    combine(0, g)
                    norm(n0 + g, g)
                rest(0)
                rest2(0)
                delta_u(0, 0)
                delta_u(0, 1)
                for b in range(NB):
                    inputs(b, 0)
                    if b == 0:
                        combine(0, 2)
                        norm(n0 + 2, 2)
                    else:
                        normalise(n0 + NB + b - 1, b - 1)
                    states(b, 0)
                    if b == 0:
                        combine(0, 3)
                        norm(n0 + 3, 3)
                    inputs(b, 1)
                    states(b, 1)
                    inputs(b, 2)
                    if b + 1 < NB:
                        rest(b + 1)
                    states(b, 2)
                    if b + 1 < NB:
                        rest2(b + 1)
                    if b >= 1:
                        choose(1, b - 1)
                    inputs(b, 3)
                    states(b, 3)
                    if b + 1 < NB:
                        delta_u(b + 1, 0)
                        delta_u(b + 1, 1)
                    dve.wait_ge(sz_ready, 2 * b + 2)
                    for c in range(C2):
                        dve.wait_ge(ysum_ready, 2 * b + c + 1)
                        v.tensor_tensor(yz[:, c, :], sz[:, b % 2, c, :], bank(c), ALU.mult).then_inc(yz_ready, 1)
                    if b >= 1:
                        place(1, b - 1)
                    dve.wait_ge(o_psum, b + 1)
                    xr = x[:, TPB * b:TPB * (b + 1), :].rearrange("p k d -> p (k d)")
                    v.tensor_tensor(xr, xr, bank(6), ALU.add).then_inc(scan_used, 1)
                    dve.wait_ge(scan_used, b + 1)
                    stats(n0 + NB + b, b)
                normalise(n0 + 2 * NB - 1, NB - 1)
                choose(1, NB - 1)
                place(1, NB - 1)

            def ffn(u, b):
                n = u * NB + b
                dve.wait_ge(ff_o_psum, n + 1)
                xr = x[:, TPB * b:TPB * (b + 1), :].rearrange("p k d -> p (k d)")
                v.scalar_tensor_tensor(xr, bank(FFN_BANK[n]), 0.5, xr, ALU.mult, ALU.add).then_inc(ff_o_used, 1)

            def attend(n0):
                def rope(b, w):
                    if b >= 1 and w == 0:
                        dve.wait_ge(part_act, 2 * b)
                    dve.wait_ge(qkv_psum, 5 * b + 2 * w + 1)
                    v.scalar_tensor_tensor(t1, bank(5 + 2 * w), bqk[:, 2 * w:2 * w + 1], cs[:, 0, :],
                                           ALU.add, ALU.mult).then_inc(qkv_used, 1)
                    dve.wait_ge(qkv_psum, 5 * b + 2 * w + 2)
                    v.scalar_tensor_tensor(t2, bank(6 - w), bqk[:, 2 * w + 1:2 * w + 2], cs[:, 1, :],
                                           ALU.add, ALU.mult).then_inc(qkv_used, 1)
                    dve.wait_ge(qkv_used, 5 * b + 2 * w + 2)
                    v.tensor_tensor(qk[:, w, :], t1, t2, ALU.add).then_inc(rope_ready, 1)
                    dve.wait_ge(rope_ready, 2 * b + w + 1)

                def take_values(b):
                    dve.wait_ge(qkv_psum, 5 * b + 5)
                    if b >= 2:
                        dve.wait_ge(pv_psum, NG * (b - 1))
                    if b == 0:
                        dve.wait_ge(att_const, 2)
                    v.tensor_copy(va[:, b % 2, :, :, 0:HD],
                                  bank(6).rearrange("p (k h e) -> p k h e", k=TPB, h=NH)).then_inc(v_ready, 1)
                    dve.wait_ge(v_ready, b + 1)
                    v.memset(ve2[:, 0:1], 0.0).then_inc(qkv_used, 1)

                def middle(b):
                    dve.wait_ge(part_act, 2 * b + 1)
                    v.tensor_tensor(q1, qk, spl[:, 0, :, :], ALU.subtract).then_inc(part_vec, 1)

                def low(b):
                    dve.wait_ge(part_act, 2 * b + 2)
                    v.tensor_tensor(spl[:, 2, :, :], q1, spl[:, 1, :, :], ALU.subtract).then_inc(part_vec, 1)

                def maxima(b, steps_):
                    for j in steps_:
                        qt, h0, nh = MAXSTEPS[j]
                        if j == 0 and b >= 1:
                            dve.wait_ge(m_turned, b)
                        dve.wait_ge(max_psum, b * NMS + j + 1)
                        src = ps[:, 5 + j % 2, 0:nh * P * (qt + 1)].rearrange("p (h f) -> p h f", h=nh)
                        v.tensor_reduce(nm[:, qt, h0:h0 + nh], src, AX.X, ALU.max, negate=True).then_inc(max_used, 1)

                def divide(n):
                    g = n % NG
                    if g == 0 and n:
                        dve.wait_ge(on_turned, n // NG)
                    dve.wait_ge(o_turned, n + 1)
                    o4 = bank(4).rearrange("p (k j e) -> p k j e", k=TPB, j=GH)
                    link(v.reciprocal(rden, o4[:, :, :, HD]))
                    for k in range(TPB):
                        ins = v.tensor_tensor(
                            on[:, k, 32 * g:32 * g + 32].rearrange("p (j e) -> p j e", j=GH), o4[:, k, :, 0:HD],
                            rden[:, k, :].unsqueeze(2).to_broadcast([P, GH, HD]), ALU.mult)
                    ins.then_inc(on_ready, 1)

                def add_output(b):
                    dve.wait_ge(ao_psum, b + 1)
                    xr = x[:, TPB * b:TPB * (b + 1), :].rearrange("p k d -> p (k d)")
                    v.tensor_tensor(xr, xr, bank(4), ALU.add).then_inc(ao_used, 1)
                    dve.wait_ge(ao_used, b + 1)
                    norm(n0 + NB + b, b)

                def ffn_norm(b):
                    ffn(0, b)
                    dve.wait_ge(ff_o_used, b + 1)
                    norm(ATT_NORM[b], b)

                for b in range(2):
                    combine(1, b)
                    norm(FFN_NORM[b], b)
                ffn_norm(0)
                combine(1, 2)
                norm(FFN_NORM[2], 2)
                dve.wait_ge(att_loaded, 16 * 7)
                v.tensor_copy(maskb[:, :, :], maskf).then_inc(att_const, 1)
                rope(0, 0)
                rope(0, 1)
                take_values(0)
                middle(0)
                low(0)
                ffn_norm(1)
                combine(1, 3)
                norm(FFN_NORM[3], 3)
                ffn_norm(2)
                maxima(0, range(NMS // 2))
                ffn_norm(3)
                maxima(0, range(NMS // 2, NMS))
                rope(1, 0)
                rope(1, 1)
                for n in range(NB * NG + 1):
                    b, g = divmod(n, NG)
                    for k in range(GH):
                        if k == 0 and n >= 2:
                            divide(n - 2)
                        if g == 0 and b + 1 < NB and k == 0:
                            middle(b + 1)
                        if g == 0 and b + 1 < NB and k == 1:
                            low(b + 1)
                        if g == 1 and b + 1 < NB and k == 0:
                            take_values(b + 1)
                        if g == 3 and b + 2 < NB and k >= 2:
                            rope(b + 2, k - 2)
                        if b + 1 < NB:
                            maxima(b + 1, max_steps(g, k))
                        if g == 1 and b >= 1 and k == 3:
                            add_output(b - 1)
                divide(NB * NG - 1)
                ffn(1, 0)
                add_output(NB - 1)
                for b in range(1, NB):
                    ffn(1, b)

            dve.wait_ge(x_loaded, 16)
            stats(0, 0)
            normalise(0, 0)
            dve.wait_ge(const_loaded, 16 * 8)
            v.memset(ones_b[:, :], 1.0)
            v.tensor_copy(before_b[:, :], before[:, :])
            v.tensor_copy(ident_b[:, :], ident[:, :]).then_inc(ident_ready, 1)
            v.memset(ve2[:, NB:NB + 1], 0.0).then_inc(y_ready, 1)
            dve.wait_ge(x_rest_loaded, 16)
            for g in range(NB):
                if g:
                    normalise(g, g)
                if g + 1 < NB:
                    stats(g + 1, g + 1)
                choose(0, g)
                place(0, g)
            tables(0)
            moe(0, 0)
            fly_up()
            scan(NB)
            tables(1)
            moe(1, 2 * NB)
            fly_down()
            attend(4 * NB)


def kernel(**inputs):
    import numpy as np
    import concourse.bacc as bacc
    from concourse.bass_utils import run_bass_kernel_spmd

    g = {k: np.asarray(v) for k, v in inputs.items()}
    f32 = np.float32

    def cols(v, n):
        return v.reshape(n, 128).T

    L, E, D = 512, 8, 128
    sw = np.arange(D) ^ 1
    half = 4
    inv = (f32(1.0) / np.power(f32(10000.0), np.arange(half, dtype=f32) / f32(half))).astype(f32)
    ang = np.arange(L, dtype=f32)[:, None] * inv[None, :]
    pair = (np.arange(D) % 8) // 2
    cos = np.cos(ang).astype(f32)[:, pair].T
    sin = np.sin(ang).astype(f32)[:, pair].T * np.where(np.arange(D) % 2 == 0, -1.0, 1.0).astype(f32)[:, None]
    i, j = np.arange(128)[:, None], np.arange(128)[None, :]
    big = f32(-1.0e30)
    mask = np.stack([np.where(j > i, big, f32(0)), np.where(i > j, big, f32(0))], 1).astype(f32)
    sel = np.zeros((96, 16, 128), f32)
    for r in range(96):
        if 8 <= r % 32 < 24:
            sel[r, r % 32 - 8, :] = 1.0
    wx = g["L0_attn_W_x"].reshape(2, 128, 24).transpose(1, 0, 2)
    wx3 = np.zeros((128, 2, 96), f32)
    for r in range(3):
        wx3[:, :, 32 * r:32 * r + 24] = wx
    W_in = g["L0_attn_W_in"]
    Wq, Wk = g["L1_attn_Wq"], g["L1_attn_Wk"]
    bq, bk = g["L1_attn_bq"], g["L1_attn_bk"]
    arrays = {
        "x": g["L0_attn_x"].reshape(-1, D),
        "ident": np.eye(128, dtype=f32),
        "rank8": np.broadcast_to(np.arange(E, 0, -1, dtype=f32), (128, E)),
        "base8": np.broadcast_to(np.arange(E, dtype=f32) * (17 * 128), (128, E)),
        "first4": np.broadcast_to(np.arange(4) > 0, (128, E, 4)),
        "steps": np.broadcast_to(np.arange(16, dtype=f32) * 128, (128, E, 16)),
        "tnum": np.broadcast_to(np.arange(42, dtype=f32)[:, None], (1, 42, E)),
        "before": np.triu(np.ones((128, 128), f32), 1),
        "w_router": g["L0_ffn_W_router"].T,
        "w_gate": g["L0_ffn_W_gate"].transpose(2, 0, 1),
        "w_up": g["L0_ffn_W_up"].transpose(2, 0, 1),
        "w_down": g["L0_ffn_W_down"].reshape(E, D, 4, 128).transpose(3, 0, 2, 1),
        "up_w": g["L1_ffn_up_weights"].reshape(9, -1),
        "down_w": g["L1_ffn_down_weights"].reshape(9, -1),
        "up_bias": cols(g["L1_ffn_up_bias"], 4),
        "b_con": g["L1_ffn_b_con"][None], "down_bias": g["L1_ffn_down_bias"][None],
        "w_exp": g["L1_ffn_W_exp"], "b_exp": g["L1_ffn_b_exp"][None], "w_conT": g["L1_ffn_W_con"].T,
        "conv_bias": cols(g["L0_attn_conv_bias"], 2), "b_dt": cols(g["L0_attn_b_dt"], 2),
        "dskip": cols(g["L0_attn_D"], 2),
        "dw": g["L0_attn_dw_kernel"].T.reshape(2, 128, 4).transpose(1, 0, 2),
        "w_dt": g["L0_attn_W_dt"],
        "a_log": g["L0_attn_A_log"].reshape(2, 128, 8).transpose(1, 0, 2),
        "pw": g["L0_attn_pw_kernel"].reshape(2, 128, 256).transpose(1, 0, 2),
        "wxT": W_in[:, :256].T.reshape(2, 128, 128).transpose(1, 0, 2),
        "wz": W_in[:, 256:],
        "w_out": g["L0_attn_W_out"].reshape(2, 128, 128).transpose(1, 0, 2),
        "w_x3": wx3, "sel": sel,
        "wq": np.stack([Wq.T, Wq.T[:, sw], Wk.T, Wk.T[:, sw]], 1),
        "bqk": np.stack([bq, bq[sw], bk, bk[sw]], 1),
        "wv": g["L1_attn_Wv"].T, "wo": g["L1_attn_Wo"].T,
        "bv": g["L1_attn_bv"][None], "bo": g["L1_attn_bo"][None],
        "cossin": np.stack([cos, sin], 1), "mask": mask,
    }
    nc = bacc.Bacc("TRN2", target_bir_lowering=False, num_devices=1)
    maps, aps = {}, {}
    for name, a in arrays.items():
        a = np.ascontiguousarray(a, dtype=f32)
        maps["in_" + name] = a
        aps[name] = nc.dram_tensor("in_" + name, a.shape, F32, kind="ExternalInput").ap()
    import ml_dtypes
    a = np.ones((1, 16, 512), ml_dtypes.bfloat16)
    maps["in_ones_row"] = a
    aps["ones_row"] = nc.dram_tensor("in_ones_row", a.shape, BF16, kind="ExternalInput").ap()
    out = nc.dram_tensor("out_dram", (2048, D), F32, kind="ExternalOutput").ap()
    macaron_kernel(nc, aps, out)
    r = run_bass_kernel_spmd(nc, [maps], core_ids=[0])
    return r.results[0]["out_dram"].reshape(4, 512, 128)
```
